# Optimizing a Trainium2 kernel written in Bass

```python
import numpy as np
import jax
import jax.numpy as jnp

def _softmax(x, axis=-1):
    return jax.nn.softmax(x, axis=axis)

def _gelu(x):
    return jax.nn.gelu(x, approximate=True)

def _silu(x):
    return jax.nn.silu(x)

def _sigmoid(x):
    return jax.nn.sigmoid(x)

def _layernorm(x, axis=-1, eps=1e-05):
    m = jnp.mean(x, axis=axis, keepdims=True)
    v = jnp.var(x, axis=axis, keepdims=True)
    return (x - m) / jnp.sqrt(v + eps)

def _scatter_add(tgt, idx, src, axis=0):
    return tgt.at[idx].add(src)

def _segment_sum(src, seg, n):
    return jax.ops.segment_sum(src, seg, n)
kernel_name = 'mk_gnn_resnorm_d2_gnn_r8_f874ca'

def setup_inputs(seed: int=0):
    np.random.seed(seed)
    _w = jnp.asarray

    def _rec_inputs():
        import jax
        import jax.numpy as jnp
        _gk = jax.random.key(seed)
        x = -0.000202 + 1 * jax.random.normal(jax.random.fold_in(_gk, 1), (12500, 128), jnp.float32)
        src = jax.random.randint(jax.random.fold_in(_gk, 2), (200000,), 0, 12500, jnp.int32)
        dst = jax.random.randint(jax.random.fold_in(_gk, 3), (200000,), 0, 12500, jnp.int32)
        _o = jnp.argsort(dst, stable=True)
        src = src[_o]
        dst = dst[_o]
        edge_attr_64 = 0.000167468 + 1.0002 * jax.random.normal(jax.random.fold_in(_gk, 11), (200000, 64), jnp.float32)
        return (x, src, dst, edge_attr_64)
    x, src, dst, edge_attr_64 = _rec_inputs()

    def _L0_gnn_setup():
        import jax, jax.numpy as jnp
        import numpy as np
        N_NODES = 6250
        N_EDGES = 100000
        D_IN = 128
        D_OUT = 128
        key = jax.random.key(seed)
        ks = jax.random.split(key, 6)
        x = jax.random.normal(ks[0], (N_NODES, D_IN), dtype=jnp.float32)
        edge_index = jax.random.randint(ks[1], (2, N_EDGES), 0, N_NODES, dtype=jnp.int32)
        s1 = 1.0 / np.sqrt(2 * D_IN)
        s2 = 1.0 / np.sqrt(D_IN)
        W1 = jax.random.normal(ks[2], (2 * D_IN, D_IN), dtype=jnp.float32) * s1
        b1 = jnp.zeros((D_IN,), dtype=jnp.float32)
        W2 = jax.random.normal(ks[3], (D_IN, 1), dtype=jnp.float32) * s2
        b2 = jnp.zeros((1,), dtype=jnp.float32)
        Wl = jax.random.normal(ks[4], (D_IN, D_OUT), dtype=jnp.float32) * s2
        bl = jnp.zeros((D_OUT,), dtype=jnp.float32)
        return {'x': x, 'edge_index': edge_index, 'W1': W1, 'b1': b1, 'W2': W2, 'b2': b2, 'Wl': Wl, 'bl': bl}
    _L0_gnn_all = _L0_gnn_setup()
    _L0_gnn_in = {k: v for k, v in _L0_gnn_all.items() if k in ('W1', 'b1', 'W2', 'b2', 'Wl', 'bl')}
    del _L0_gnn_all

    def _L1_gnn_setup():
        import jax, jax.numpy as jnp
        import numpy as np
        N = 5000
        E = 80000
        ND = 128
        ED = 64
        LN_EPS = 1e-05
        key = jax.random.key(seed)
        ks = jax.random.split(key, 16)
        s = lambda k, shape, fan_in: jax.random.normal(k, shape, dtype=jnp.float32) * (1.0 / np.sqrt(fan_in))
        return {'node_features': jax.random.normal(ks[0], (N, ND), dtype=jnp.float32), 'edge_indices': jax.random.randint(ks[1], (2, E), 0, N, dtype=jnp.int32), 'edge_features': jax.random.normal(ks[2], (E, ED), dtype=jnp.float32), 'W1': s(ks[3], (2 * ND + ED, ND), 2 * ND + ED), 'b1': jnp.zeros((ND,), jnp.float32), 'ln_g': jnp.ones((ND,), jnp.float32), 'ln_b': jnp.zeros((ND,), jnp.float32), 'W2': s(ks[4], (ND, ND), ND), 'b2': jnp.zeros((ND,), jnp.float32), 'gate_w': s(ks[5], (ED, 1), ED), 'gate_b': jnp.zeros((1,), jnp.float32), 'W_ih': s(ks[6], (3 * ND, ND), ND), 'b_ih': jnp.zeros((3 * ND,), jnp.float32), 'W_hh': s(ks[7], (3 * ND, ND), ND), 'b_hh': jnp.zeros((3 * ND,), jnp.float32)}
    _L1_gnn_all = _L1_gnn_setup()
    _L1_gnn_in = {k: v for k, v in _L1_gnn_all.items() if k in ('W1', 'b1', 'ln_g', 'ln_b', 'W2', 'b2', 'gate_w', 'gate_b', 'W_ih', 'b_ih', 'W_hh', 'b_hh')}
    del _L1_gnn_all
    return {'x': x, 'src': src, 'dst': dst, 'edge_attr_64': edge_attr_64, 'L0_gnn_W1': _L0_gnn_in['W1'], 'L0_gnn_b1': _L0_gnn_in['b1'], 'L0_gnn_W2': _L0_gnn_in['W2'], 'L0_gnn_b2': _L0_gnn_in['b2'], 'L0_gnn_Wl': _L0_gnn_in['Wl'], 'L0_gnn_bl': _L0_gnn_in['bl'], 'L1_gnn_W1': _L1_gnn_in['W1'], 'L1_gnn_b1': _L1_gnn_in['b1'], 'L1_gnn_ln_g': _L1_gnn_in['ln_g'], 'L1_gnn_ln_b': _L1_gnn_in['ln_b'], 'L1_gnn_W2': _L1_gnn_in['W2'], 'L1_gnn_b2': _L1_gnn_in['b2'], 'L1_gnn_gate_w': _L1_gnn_in['gate_w'], 'L1_gnn_gate_b': _L1_gnn_in['gate_b'], 'L1_gnn_W_ih': _L1_gnn_in['W_ih'], 'L1_gnn_b_ih': _L1_gnn_in['b_ih'], 'L1_gnn_W_hh': _L1_gnn_in['W_hh'], 'L1_gnn_b_hh': _L1_gnn_in['b_hh']}

def reference(x, src, dst, edge_attr_64, L0_gnn_W1, L0_gnn_b1, L0_gnn_W2, L0_gnn_b2, L0_gnn_Wl, L0_gnn_bl, L1_gnn_W1, L1_gnn_b1, L1_gnn_ln_g, L1_gnn_ln_b, L1_gnn_W2, L1_gnn_b2, L1_gnn_gate_w, L1_gnn_gate_b, L1_gnn_W_ih, L1_gnn_b_ih, L1_gnn_W_hh, L1_gnn_b_hh):
    import jax
    import jax.numpy as jnp

    def _L0_gnn_ref(x, edge_index, W1, b1, W2, b2, Wl, bl):
        import jax, jax.numpy as jnp
        import numpy as np
        N_NODES = 6250
        N_EDGES = 100000
        D_IN = 128
        D_OUT = 128
        row, col = (edge_index[0], edge_index[1])
        n, d = x.shape
        xc = x[row]
        xn = x[col]
        h = jax.nn.relu(xc @ W1[:d] + xn @ W1[d:] + b1)
        mask = jax.nn.sigmoid(h @ W2 + b2)[:, 0]
        seg_sum = jax.ops.segment_sum(mask, row, num_segments=n)
        w = mask / (seg_sum[row] + 1e-09)
        agg = jax.ops.segment_sum(w[:, None] * xn, row, num_segments=n)
        deg = jax.ops.segment_sum(jnp.ones_like(mask), row, num_segments=n)
        out_emb = jnp.where((deg > 0)[:, None], 0.5 * x + 0.5 * agg, x)
        return jax.nn.relu(out_emb @ Wl + bl)

    def _L1_gnn_ref(node_features, edge_indices, edge_features, W1, b1, ln_g, ln_b, W2, b2, gate_w, gate_b, W_ih, b_ih, W_hh, b_hh):
        import jax, jax.numpy as jnp
        import numpy as np
        N = 5000
        E = 80000
        ND = 128
        ED = 64
        LN_EPS = 1e-05
        src, dst = (edge_indices[0], edge_indices[1])
        edge_inputs = jnp.concatenate([node_features[src], node_features[dst], edge_features], axis=1)
        h = edge_inputs @ W1 + b1
        mu = jnp.mean(h, axis=-1, keepdims=True)
        var = jnp.var(h, axis=-1, keepdims=True)
        h = (h - mu) * jax.lax.rsqrt(var + LN_EPS) * ln_g + ln_b
        h = jax.nn.relu(h)
        messages = h @ W2 + b2
        gate = jax.nn.sigmoid(edge_features @ gate_w + gate_b)
        messages = messages * gate
        agg = jax.ops.segment_sum(messages, dst, num_segments=node_features.shape[0])
        gi = agg @ W_ih.T + b_ih
        gh = node_features @ W_hh.T + b_hh
        i_r, i_z, i_n = jnp.split(gi, 3, axis=1)
        h_r, h_z, h_n = jnp.split(gh, 3, axis=1)
        r = jax.nn.sigmoid(i_r + h_r)
        z = jax.nn.sigmoid(i_z + h_z)
        n = jnp.tanh(i_n + r * h_n)
        return (1.0 - z) * n + z * node_features
    edge_index = jnp.stack([src, dst])
    x = _layernorm(x + _L0_gnn_ref(x, edge_index, L0_gnn_W1, L0_gnn_b1, L0_gnn_W2, L0_gnn_b2, L0_gnn_Wl, L0_gnn_bl), axis=-1)
    x = _layernorm(x + _L1_gnn_ref(x, edge_index, edge_attr_64, L1_gnn_W1, L1_gnn_b1, L1_gnn_ln_g, L1_gnn_ln_b, L1_gnn_W2, L1_gnn_b2, L1_gnn_gate_w, L1_gnn_gate_b, L1_gnn_W_ih, L1_gnn_b_ih, L1_gnn_W_hh, L1_gnn_b_hh), axis=-1)
    return x

_drawn_inputs = setup_inputs


def setup_inputs(seed=0):
    import zlib

    import numpy as np

    out = dict(_drawn_inputs(seed))
    spreads = {'L0_gnn_b1': (0.0, 0.8),
     'L0_gnn_bl': (0.0, 0.1),
     'L1_gnn_b1': (0.0, 0.1),
     'L1_gnn_ln_g': (1.0, 0.2),
     'L1_gnn_ln_b': (0.0, 0.1),
     'L1_gnn_b2': (0.0, 0.1),
     'L1_gnn_b_ih': (0.0, 0.521),
     'L1_gnn_b_hh': (0.0, 0.641)}
    factors = {}
    for name, (base, spread) in spreads.items():
        noise = np.random.default_rng([zlib.crc32(name.encode()), seed]).standard_normal(out[name].shape)
        drawn = base * np.exp(spread * noise) if base else spread * noise
        out[name] = jnp.asarray(drawn.astype(out[name].dtype))
    for name, factor in factors.items():
        out[name] = (out[name] * factor).astype(out[name].dtype)
    return out
```

```python
from contextlib import ExitStack, contextmanager

import concourse.bass as bass
from concourse import mybir
from concourse.alu_op_type import AluOpType as ALU

ACT = mybir.ActivationFunctionType
F32 = mybir.dt.float32
BF16 = mybir.dt.bfloat16
I32 = mybir.dt.int32
I16 = mybir.dt.int16

P = 128
N = 12500
E = 200000
D = 128
DE = 64
TILES = -(-N // P)
LASTROWS = N - (TILES - 1) * P
CHUNKS = -(-E // P)
BLOCKS = -(-(CHUNKS + TILES - 1) // P)
STEPS = BLOCKS * P
G = 8
R = 4
GROUPS = STEPS // G
BODIES = GROUPS // R
KEYROWS = 2048
ROW = KEYROWS * P // P
EP = 125
EC = E // EP
BASE = 1 << 28
LOW = (1 << 14) - 1
PAD = BASE | (LOW << 14)
assert N <= LOW and EP * EC == E and BODIES * R * G == STEPS and E % P == 64


def load_values(nc, engine, ap, most):
    _, values = nc.values_load_multi_w_load_instructions(
        ap, engines=(engine,), min_val=0, max_val=most,
        skip_runtime_bounds_check_because="the schedule bounds them")
    return values


@contextmanager
def stage_semaphores(nc):
    held = []

    def sem(name):
        held.append(nc.alloc_semaphore(name))
        return held[-1]
    yield sem
    nc.all_engine_barrier()
    nc.clear_and_free_semaphores(held)
    nc.all_engine_barrier()


class Shared:
    pass


def constants_stage(nc, s, ins):
    with nc.Block() as block:
        @block.gpsimd
        def _(pool):
            nc.gpsimd.iota(s.lane_i[:, :], [[1, P]], base=0, channel_multiplier=0).then_inc(s.const_i, 1)
            nc.gpsimd.iota(s.part_i[:, :], [[0, P]], base=0, channel_multiplier=1).then_inc(s.const_i, 1)
            nc.gpsimd.iota(s.step_i[:, :], [[1, STEPS]], base=0, channel_multiplier=0).then_inc(s.const_i, 1)
            nc.gpsimd.iota(s.chunk_i[:, :], [[1, BLOCKS]], base=0,
                           channel_multiplier=BLOCKS).then_inc(s.const_i, 1)

        @block.vector
        def _(dve):
            dve.memset(s.ones_b[:, :], 1.0)
            dve.memset(s.ones_f[:, :], 1.0)
            dve.wait_ge(s.const_i, 4)
            dve.tensor_copy(s.lane_b[:, :], s.lane_i[:, :])
            dve.tensor_copy(s.step_f[:, :], s.step_i[:, :])
            dve.tensor_copy(s.chunk_f[:, :], s.chunk_i[:, :])
            dve.tensor_copy(s.part_f[:, :], s.part_i[:, :])
            dve.tensor_copy(s.lane_f[:, :], s.lane_i[:, :]).then_inc(s.const_f, 1)
            dve.wait_ge(s.const_f, 1)
            dve.tensor_tensor(s.ident_b[:, :], s.lane_f[:, :], s.part_f[:, :], ALU.is_equal)
            dve.tensor_tensor(s.ident_f[:, :], s.lane_f[:, :], s.part_f[:, :], ALU.is_equal)
            for j in range(7):
                dve.tensor_scalar(s.bit[:, j:j + 1], s.part_i[:, 0:1], j, 1,
                                  ALU.logical_shift_right, ALU.bitwise_and).then_inc(s.const_f, 1)
            dve.wait_ge(s.const_f, 8)
            dve.tensor_scalar(s.sign[:, 1:8], s.bit[:, 0:7], -2.0, 1.0, ALU.mult, ALU.add)
            dve.memset(s.sign[:, 0:1], 1.0)
            dve.memset(s.sign[:, 8:9], 1.0).then_inc(s.const_f, 1)
            dve.wait_ge(s.const_f, 9)
            dve.tensor_tensor(s.flip[:, 0:8], s.sign[:, 0:8], s.sign[:, 1:9], ALU.mult)


def prepare_stage(nc, s, ins):
    with ExitStack() as ctx:
        sb = lambda name, shape, dt: ctx.enter_context(nc.sbuf_tensor(name, shape, dt))
        sem = ctx.enter_context(stage_semaphores(nc))
        keys = [sb("keys_even", [P, ROW], F32), sb("keys_odd", [P, ROW], F32)]
        src_i = sb("src_i", [P, EC], I32)
        dst_i = sb("dst_i", [P, EC], I32)
        dkey = sb("dkey", [P, EC], I32)
        padkey = sb("padkey", [P, P], I32)
        xs = sb("xs", [P, 4, 2, D], F32)
        w0 = sb("w0", [P, 2 * D], F32)
        b0 = sb("b0", [1, 2 * D], F32)
        xT = sb("xT", [P, 2, 2 * P], F32)
        ab = sb("ab", [P, 4, 2, 2 * D], F32)
        rest = sb("rest", [P, 2, 2, D], F32)
        turn = ctx.enter_context(nc.psum_tensor("turn", [P, 16, P], F32))
        xtp = ctx.enter_context(nc.psum_tensor("xtp", [P, 2, 4, P], F32))
        abp = ctx.enter_context(nc.psum_tensor("abp", [P, 2, 2, 2 * D], F32))
        edges_in, w_in, x_pad = sem("edges_in"), sem("w_in"), sem("x_pad")
        x_in = [sem(f"x_in{i}") for i in range(4)]
        sort_dve, sort_turn, sort_evac = sem("sort_dve"), sem("sort_turn"), sem("sort_evac")
        dkey_made, keys_out = sem("dkey_made"), sem("keys_out")
        xT_made, xT_evac, ab_made, ab_evac = sem("xT_made"), sem("xT_evac"), sem("ab_made"), sem("ab_evac")
        split_done = sem("split_done")
        b_out = [sem(f"b_out{i}") for i in range(4)]
        x_copied = sem("x_copied")
        NG = TILES // 2

        plan = []
        k = 2
        while k <= ROW * P:
            if k >= ROW:
                plan.append(("flip", (k // ROW).bit_length() - 1))
            if k > ROW:
                plan.append(("turn",))
                d = k // 2
                while d >= ROW:
                    plan.append(("cross", d // ROW))
                    d //= 2
                plan.append(("turn",))
            d = min(k // 2, ROW // 2)
            while d >= 1:
                plan.append(("row", k, d))
                d //= 2
            k *= 2
        counts = []
        total = 2
        for e in plan:
            total += {"flip": 1, "turn": 0, "cross": 2, "row": 2 if e[0] != "row" or e[1] >= ROW else 4}[e[0]]
            counts.append(total)
        sorted_in = []
        at = 0
        for e in plan:
            if e[0] != "turn":
                at = 1 - at
            else:
                at = 1 - at
            sorted_in.append(at)

        with nc.Block() as block:
            @block.sync
            def _(sp):
                sp.dma_start(src_i[0:EP, :], ins["src"].rearrange("(p c) -> p c", c=EC)).then_inc(edges_in, 16)
                sp.dma_start(dst_i[0:EP, :], ins["dst"].rearrange("(p c) -> p c", c=EC)).then_inc(edges_in, 16)
                sp.dma_start(w0[:, 0:D], ins["L0_gnn_W1"][0:D, :]).then_inc(w_in, 16)
                sp.dma_start(w0[:, D:2 * D], ins["L0_gnn_W1"][D:2 * D, :]).then_inc(w_in, 16)
                sp.dma_start(b0[:, 0:D], ins["L0_gnn_b1"].rearrange("(a d) -> a d", a=1)).then_inc(w_in, 16)
                def load_x(i):
                    if i >= 4:
                        sp.wait_ge(xT_made, i - 3)
                    full = 2 if i < NG - 1 else 1
                    xt = ins["x"][2 * i * P:(2 * i + full) * P, :].rearrange("(t p) d -> p t d", p=P)
                    sp.dma_start(xs[:, i % 4, 0:full, :], xt).then_inc(x_in[i % 4], 16)
                    if full == 1:
                        sp.wait_ge(x_pad, 2)
                        sp.dma_start(xs[0:LASTROWS, i % 4, 1, :],
                                     ins["x"][(TILES - 1) * P:N, :]).then_inc(x_in[i % 4], 16)
                for i in range(4):
                    load_x(i)
                sp.dma_start(s.bx[0:N, D:2 * D], ins["x"][:, :]).then_inc(x_copied, 16)
                sp.wait_ge(dkey_made, 2)
                flat = s.keys1.rearrange("r e -> (r e)")
                whole = (E // P) * P
                cut = whole - (EP - 1) * EC
                sp.dma_start(flat[0:(EP - 1) * EC].rearrange("(p c) -> p c", c=EC),
                             dkey[0:EP - 1, :]).then_inc(keys_out, 16)
                sp.dma_start(flat[(EP - 1) * EC:whole].rearrange("(a c) -> a c", a=1),
                             dkey[EP - 1:EP, 0:cut]).then_inc(keys_out, 16)
                sp.dma_start(flat[whole:whole + 64].rearrange("(a c) -> a c", a=1),
                             padkey[0:1, 0:64]).then_inc(keys_out, 16)
                sp.dma_start(flat[whole + 64:whole + P].rearrange("(a c) -> a c", a=1),
                             dkey[EP - 1:EP, cut:EC]).then_inc(keys_out, 16)
                sp.dma_start(s.keys1[CHUNKS:STEPS, :], padkey[0:STEPS - CHUNKS, :]).then_inc(keys_out, 16)
                for i in range(NG):
                    if i + 4 < NG:
                        load_x(i + 4)
                    sp.wait_ge(ab_evac, i + 1)
                    full = 2 if i < NG - 1 else 1
                    out = s.bx[2 * i * P:(2 * i + full) * P, 0:D].rearrange("(t p) d -> p t d", p=P)
                    sp.dma_start(out, ab[:, i % 4, 0:full, D:2 * D]).then_inc(b_out[i % 4], 16)
                    if full == 1:
                        sp.dma_start(s.bx[(TILES - 1) * P:N, 0:D],
                                     ab[0:LASTROWS, i % 4, 1, D:2 * D]).then_inc(b_out[i % 4], 16)
                for i in range(4):
                    sp.wait_ge(b_out[i], 16 * (len(range(i, NG, 4)) + (i == (NG - 1) % 4)))
                sp.wait_ge(sort_dve, counts[-1])
                sp.dma_start(s.keys0.rearrange("(p c) e -> p (c e)", p=P),
                             keys[sorted_in[-1]].bitcast(I32)[:, :]).then_inc(keys_out, 16)
                sp.wait_ge(x_copied, 16)
                sp.wait_ge(keys_out, 16 * 6)

            @block.gpsimd
            def _(pool):
                nc.gpsimd.memset(b0[:, D:2 * D], 0.0).then_inc(x_pad, 1)
                for i in range(NG):
                    tab = s.split[:, 2 * i:2 * i + 2, :, :]
                    if i == NG - 4:
                        pool.wait_ge(xT_made, NG - 4)
                        nc.gpsimd.memset(xs[:, (NG - 1) % 4, 1, :], 0.0).then_inc(x_pad, 1)
                    pool.wait_ge(ab_evac, i + 1)
                    if i >= 2:
                        pool.wait_ge(split_done, 3 * (i - 1))
                    nc.gpsimd.tensor_tensor(rest[:, i % 2], ab[:, i % 4, :, 0:D], tab[:, :, 0, :],
                                            ALU.subtract).then_inc(split_done, 1)
                    pool.wait_ge(split_done, 3 * i + 1)
                    nc.gpsimd.tensor_copy(tab[:, :, 1, :], rest[:, i % 2]).then_inc(split_done, 1)
                    pool.wait_ge(split_done, 3 * i + 2)
                    nc.gpsimd.tensor_tensor(tab[:, :, 2, :], rest[:, i % 2], tab[:, :, 1, :],
                                            ALU.subtract).then_inc(split_done, 1)

            @block.scalar
            def _(act):
                for i in range(NG + 1):
                    if i < NG:
                        act.wait_ge(xT_made, i + 1)
                        if i >= 2:
                            act.wait_ge(ab_made, i - 1)
                        nc.scalar.copy(xT[:, i % 2, :], xtp[:, i % 2, 0:2]).then_inc(xT_evac, 1)
                    if i >= 1:
                        j = i - 1
                        act.wait_ge(ab_made, j + 1)
                        if j >= 4:
                            act.wait_ge(b_out[j % 4], 16 * (j // 4))
                            act.wait_ge(split_done, 3 * (j - 3))
                        nc.scalar.copy(s.split[:, 2 * j:2 * j + 2, 0, :], abp[:, j % 2, :, 0:D])
                        nc.scalar.copy(ab[:, j % 4], abp[:, j % 2]).then_inc(ab_evac, 1)
                turns = 0
                for i, e in enumerate(plan):
                    if e[0] == "turn":
                        turns += 1
                        for q in range(4):
                            act.wait_ge(sort_turn, 4 * (turns - 1) + q + 1)
                            nc.scalar.copy(keys[sorted_in[i]][:, q * 512:(q + 1) * 512],
                                           turn[:, 4 * q:4 * q + 4, :]).then_inc(sort_evac, 1)

            @block.tensor
            def _(pe):
                pe.wait_ge(x_pad, 1)
                pe.wait_ge(w_in, 48)
                for i in range(NG + 1):
                    if i < NG:
                        if i >= 2:
                            pe.wait_ge(xT_evac, i - 1)
                        pe.wait_ge(x_in[i % 4], 16 * (i // 4 + 1 + (i == NG - 1)))
                        for t in range(2):
                            last = nc.tensor.transpose(xtp[:, i % 2, t, :], xs[:, i % 4, t, :], s.ident_f[:, :])
                        last.then_inc(xT_made, 1)
                    if i >= 1:
                        j = i - 1
                        pe.wait_ge(xT_evac, j + 1)
                        if j >= 2:
                            pe.wait_ge(ab_evac, j - 1)
                        for t in range(2):
                            nc.tensor.matmul(abp[:, j % 2, t, :], xT[:, j % 2, t * P:(t + 1) * P], w0[:, :],
                                             start=True, stop=False)
                            last = nc.tensor.matmul(abp[:, j % 2, t, :], s.ones_f[0:1, :], b0[:, :],
                                                    start=False, stop=True)
                        last.then_inc(ab_made, 1)
                turns = 0
                for i, e in enumerate(plan):
                    if e[0] == "turn":
                        pe.wait_ge(sort_dve, counts[i])
                        source = keys[1 - sorted_in[i]]
                        for q in range(4):
                            if turns >= 1:
                                pe.wait_ge(sort_evac, 4 * (turns - 1) + q + 1)
                            for b in range(4 * q, 4 * q + 4):
                                last = nc.tensor.transpose(turn[:, b, :], source[:, b * P:(b + 1) * P],
                                                           s.ident_f[:, :])
                            last.then_inc(sort_turn, 1)
                        turns += 1

            @block.vector
            def _(dve):
                dve.memset(padkey[:, :], PAD)
                dve.memset(keys[0].bitcast(I32)[:, :], PAD).then_inc(sort_dve, 1)
                dve.wait_ge(edges_in, 32)
                dve.tensor_scalar(src_i[0:EP, :], src_i[0:EP, :], 0, None, ALU.bitwise_or)
                dve.tensor_scalar(dkey[0:EP, :], dst_i[0:EP, :], 14, BASE, ALU.logical_shift_left,
                                  ALU.bitwise_or).then_inc(dkey_made, 1)
                dve.wait_ge(dkey_made, 1)
                dve.tensor_tensor(dkey[0:EP, :], dkey[0:EP, :], src_i[0:EP, :],
                                  ALU.bitwise_or).then_inc(dkey_made, 1)
                dve.wait_ge(dkey_made, 2)
                dve.tensor_scalar(src_i[0:EP, :], src_i[0:EP, :], 14, BASE, ALU.logical_shift_left,
                                  ALU.bitwise_or).then_inc(dkey_made, 1)
                dve.wait_ge(dkey_made, 3)
                dve.wait_ge(sort_dve, 1)
                dve.tensor_tensor(keys[0].bitcast(I32)[0:EP, 0:EC], src_i[0:EP, :], dst_i[0:EP, :],
                                  ALU.bitwise_or).then_inc(sort_dve, 1)
                at, done, turns = 0, 2, 0

                def exchange(lo, hi, a, b):
                    dve.tensor_tensor(lo, a, b, ALU.min).then_inc(sort_dve, 1)
                    dve.tensor_tensor(hi, a, b, ALU.max).then_inc(sort_dve, 1)

                for i, e in enumerate(plan):
                    a, b = keys[at], keys[1 - at]
                    at = 1 - at
                    if e[0] == "turn":
                        turns += 1
                        continue
                    dve.wait_ge(sort_dve, done)
                    if turns:
                        dve.wait_ge(sort_evac, 4 * turns)
                    if e[0] == "flip":
                        dve.tensor_scalar(b[:, :], a[:, :], s.flip[:, e[1]:e[1] + 1], None,
                                          ALU.mult).then_inc(sort_dve, 1)
                    elif e[0] == "cross":
                        x, y = (v[:, :].rearrange("c (b r two d) -> c b r two d", two=2, d=e[1], b=16)
                                for v in (a, b))
                        exchange(y[:, :, :, 0, :], y[:, :, :, 1, :], x[:, :, :, 0, :], x[:, :, :, 1, :])
                    elif e[1] >= ROW:
                        x, y = (v[:, :].rearrange("p (r two d) -> p r two d", two=2, d=e[2]) for v in (a, b))
                        exchange(y[:, :, 0, :], y[:, :, 1, :], x[:, :, 0, :], x[:, :, 1, :])
                    else:
                        x, y = (v[:, :].rearrange("p (m s r two d) -> p m s r two d", s=2, two=2, d=e[2],
                                                  r=e[1] // (2 * e[2])) for v in (a, b))
                        exchange(y[:, :, 0, :, 0, :], y[:, :, 0, :, 1, :], x[:, :, 0, :, 0, :], x[:, :, 0, :, 1, :])
                        exchange(y[:, :, 1, :, 1, :], y[:, :, 1, :, 0, :], x[:, :, 1, :, 0, :], x[:, :, 1, :, 1, :])
                    done = counts[i]


def schedule_stage(nc, s, l):
    keys = (s.keys0, s.keys1)[l]
    with ExitStack() as ctx:
        sb = lambda name, shape, dt: ctx.enter_context(nc.sbuf_tensor(f"{name}_{l}", shape, dt))
        sems = ctx.enter_context(stage_semaphores(nc))
        sem = lambda name: sems(f"{name}_{l}")
        lastkey = sb("lastkey", [P, BLOCKS], I32)
        ends_i = sb("ends_i", [P, BLOCKS], I32)
        ends = sb("ends", [P, BLOCKS], F32)
        past = sb("past", [P, BLOCKS, STEPS], BF16)
        chunk_of = sb("chunk_of", [P, BLOCKS], I32)
        rows = sb("rows", [P, BLOCKS, P], I32)
        stepkey = sb("stepkey", [P, STEPS], F32)
        side = sb("side", [P, STEPS], I32)
        trow = sb("trow", [P, STEPS], F32)
        crow = sb("crow", [1, STEPS], F32)
        tile_i, edge_i = sb("tile_i", [1, STEPS], I16), sb("edge_i", [1, STEPS], I16)
        gather_i = sb("gather_i", [P, STEPS], I32)
        place = sb("place", [P, STEPS], BF16)
        counted = ctx.enter_context(nc.psum_tensor(f"counted_{l}", [P, 4, 512], F32))
        listed = ctx.enter_context(nc.psum_tensor(f"listed_{l}", [P, 512], F32))
        turned = ctx.enter_context(nc.psum_tensor(f"keys_turned_{l}", [P, 2, 4, P], F32))
        last_in, chain, counted_up, past_made = sem("last_in"), sem("chain"), sem("counted_up"), sem("past_made")
        rows_in, turned_up, evac, chunk_made = sem("rows_in"), sem("turned_up"), sem("evac"), sem("chunk_made")
        tiles_made, made, stored = sem("tiles_made"), sem("made"), sem("stored")
        widths = [min(512, STEPS - 512 * b) for b in range(-(-STEPS // 512))]
        quads = [(b, min(b + 4, BLOCKS)) for b in range(0, BLOCKS, 4)]
        with nc.Block() as block:
            @block.sync
            def _(sp):
                view = keys[0:STEPS, :].rearrange("(p j) e -> p j e", j=BLOCKS)[:, :, P - 1:P]
                with nc.allow_non_contiguous_dma(reason="one key of each chunk"):
                    sp.dma_start(lastkey[:, :].rearrange("p (j a) -> p j a", a=1), view).then_inc(last_in, 16)
                sp.wait_ge(tiles_made, 1 + l)
                sp.dma_start(s.tile_of[l][:, :], tile_i[:, :]).then_inc(stored, 16)
                if l == 1:
                    sp.dma_start(s.edge_of[:, :], edge_i[:, :]).then_inc(stored, 16)
                sp.wait_ge(made, 2)
                sp.dma_start(s.gather_of[l][:, :], gather_i[:, :]).then_inc(stored, 16)
                sp.dma_start(s.place_of[l][:, :], place[:, :]).then_inc(stored, 16)
                sp.wait_ge(stored, 16 * (3 + l))

            @block.gpsimd
            def _(pool):
                pool.wait_ge(chunk_made, 1)
                for b in range(BLOCKS):
                    pool.indirect_dma_start(
                        out=rows[:, b, :], out_offset=None, in_=keys[:, :],
                        in_offset=bass.IndirectOffsetOnAxis(ap=chunk_of[:, b:b + 1], axis=0),
                    ).then_inc(rows_in, 16)

            @block.tensor
            def _(pe):
                pe.wait_ge(past_made, 1)
                for b in range(BLOCKS):
                    for j in range(BLOCKS):
                        last = nc.tensor.matmul(listed[:, b:b + 1], past[:, j, b * P:(b + 1) * P],
                                                s.ones_b[:, 0:1], start=(j == 0), stop=(j == BLOCKS - 1))
                last.then_inc(counted_up, 1)
                for b, w in enumerate(widths):
                    for j in range(BLOCKS):
                        last = nc.tensor.matmul(counted[:, b, 0:w], s.ones_b[:, :], past[:, j, b * 512:b * 512 + w],
                                                start=(j == 0), stop=(j == BLOCKS - 1))
                last.then_inc(counted_up, 1)
                pe.wait_ge(rows_in, 16 * BLOCKS)
                for n, (b, e) in enumerate(quads):
                    if n >= 2:
                        pe.wait_ge(evac, n - 1)
                    for k in range(b, e):
                        last = nc.tensor.transpose(turned[:, n % 2, k - b, :], rows.bitcast(F32)[:, k, :],
                                                   s.ident_f[:, :])
                    last.then_inc(turned_up, 1)

            @block.vector
            def _(dve):
                dve.wait_ge(last_in, 16)
                dve.tensor_scalar(ends_i[:, :], lastkey[:, :], 21, 127,
                                  ALU.logical_shift_right, ALU.bitwise_and).then_inc(chain, 1)
                dve.wait_ge(chain, 1)
                dve.tensor_scalar(ends[:, :], ends_i[:, :], float(TILES - 1), None, ALU.min).then_inc(chain, 1)
                dve.wait_ge(chain, 2)
                dve.tensor_tensor(ends[:, :], ends[:, :], s.chunk_f[:, :], ALU.add).then_inc(chain, 1)
                dve.wait_ge(chain, 3)
                for j in range(BLOCKS):
                    last = dve.tensor_scalar(past[:, j, :], s.step_f[:, :], ends[:, j:j + 1], None, ALU.is_gt)
                last.then_inc(past_made, 1)
                dve.wait_ge(counted_up, 1)
                dve.tensor_copy(chunk_of[:, :], listed[:, 0:BLOCKS]).then_inc(chunk_made, 1)
                dve.wait_ge(counted_up, 2)
                for b, w in enumerate(widths):
                    cut = slice(b * 512, b * 512 + w)
                    last = dve.tensor_tensor(trow[:, cut], s.step_f[:, cut], counted[:, b, 0:w], ALU.subtract)
                    if l == 1:
                        last = dve.tensor_scalar(crow[:, cut], counted[0:1, b, 0:w], 2.0, float((E - P) // 64),
                                                 ALU.mult, ALU.min)
                last.then_inc(chain, 1)
                dve.wait_ge(chain, 4)
                dve.tensor_copy(tile_i[:, :], trow[0:1, :]).then_inc(tiles_made, 1)
                if l == 1:
                    dve.tensor_copy(edge_i[:, :], crow[:, :]).then_inc(tiles_made, 1)
                for n, (b, e) in enumerate(quads):
                    dve.wait_ge(turned_up, n + 1)
                    dve.tensor_copy(stepkey[:, b * P:e * P],
                                    turned[:, n % 2].rearrange("p k e -> p (k e)")[:, 0:(e - b) * P]).then_inc(evac, 1)
                dve.wait_ge(evac, len(quads))
                dve.tensor_scalar(gather_i[:, :], stepkey.bitcast(I32)[:, :], LOW, None,
                                  ALU.bitwise_and).then_inc(made, 1)
                dve.tensor_scalar(side[:, :], stepkey.bitcast(I32)[:, :], 14, LOW,
                                  ALU.logical_shift_right, ALU.bitwise_and).then_inc(chain, 1)
                dve.wait_ge(chain, 5)
                dve.scalar_tensor_tensor(place[:, :], trow[:, :], -float(P), side[:, :],
                                         ALU.mult, ALU.add).then_inc(made, 1)


def edge_stage0(nc, s, ins):
    W = D + 1
    with ExitStack() as ctx:
        sb = lambda name, shape, dt: ctx.enter_context(nc.sbuf_tensor(name, shape, dt))
        ps = lambda name, shape, dt: ctx.enter_context(nc.psum_tensor(name, shape, dt))
        sem = ctx.enter_context(stage_semaphores(nc))
        idx = [sb(f"idx{q}", [P, G], I32) for q in range(R)]
        bx = [sb(f"bxrows{q}", [P, G, 2 * D + 1], F32) for q in range(R)]
        hot = [sb(f"hot{q}", [P, G, P], BF16) for q in range(R)]
        hotT = [sb(f"hotT{i}", [P, G, P], BF16) for i in range(2)]
        hotw = [sb(f"hotw{i}", [P, G, P], F32) for i in range(2)]
        h = sb("h", [P, 2, 4, D], F32)
        logit = sb("logit", [P, 2, G], F32)
        sig = sb("sig", [P, 2, G], F32)
        mask = sb("mask", [P, 2, G], F32)
        w2 = sb("w2", [P, D], F32)
        b2 = sb("b2", [P, 1], F32)
        tiny = sb("tiny", [P, 1], F32)
        hotT_ps = ps("hotT_ps", [P, G, P], BF16)
        pre = ps("pre", [P, 2, 4, D], F32)
        out = ps("scattered", [P, 2, 4, 256], F32)
        w_in, zeroed = sem("w2_in"), sem("zeroed")
        idx_in = [sem(f"idx_in{q}") for q in range(R)]
        rows_in = [sem(f"bx_in{q}") for q in range(R)]
        hot_made, hot_turned, hotT_made = sem("hot_made"), sem("hot_turned"), sem("hotT_made")
        pre_made, pre_used, dotted = sem("pre_made"), sem("pre_used"), sem("dotted")
        sig_made, mask_made, hotw_made = sem("sig_made"), sem("mask_made"), sem("hotw_made")
        scattered, added = sem("scattered_up"), sem("added")
        issue, act_go = sem("issue"), sem("act_go")
        tile_of, place_of = sb("tile_row", [1, STEPS], I16), sb("places", [P, STEPS], BF16)
        gather_of, acc = s.gather_of[0], s.acc
        steps_in = sem("steps_in")

        with nc.Block() as block:
            @block.sync
            def _(sp):
                sp.dma_start(tile_of[:, :], s.tile_of[0][:, :]).then_inc(steps_in, 16)
                sp.dma_start(place_of[:, :], s.place_of[0][:, :]).then_inc(steps_in, 16)
                with nc.allow_non_contiguous_dma(reason="a row for every partition"):
                    sp.dma_start(w2[:, :], ins["L0_gnn_W2"].rearrange("d a -> a d").to_broadcast([P, D])
                                 ).then_inc(w_in, 16)
                    sp.dma_start(b2[:, :], ins["L0_gnn_b2"].rearrange("(a d) -> a d", a=1).to_broadcast([P, 1])
                                 ).then_inc(w_in, 16)

                def load_idx(g, q, round_):
                    sp.dma_start(idx[q][:, :], gather_of[:, bass.ds(g * G, G)]).then_inc(idx_in[q], 16)
                for q in range(R):
                    load_idx(q, q, 0)
                with sp.Fori(1, BODIES) as o:
                    for q in range(R):
                        sp.wait_ge(rows_in[q], o * (16 * G))
                        load_idx(o * R + q, q, o)

            @block.gpsimd
            def _(pool):
                for q in range(R):
                    nc.gpsimd.memset(bx[q][:, :, 2 * D:2 * D + 1], 1.0).then_inc(zeroed, 1)

                def gather(q):
                    for k in range(G):
                        pool.indirect_dma_start(
                            out=bx[q][:, k, 0:2 * D], out_offset=None, in_=s.bx[:, :],
                            in_offset=bass.IndirectOffsetOnAxis(ap=idx[q][:, k:k + 1], axis=0),
                        ).then_inc(rows_in[q], 16)
                for q in range(R):
                    pool.wait_ge(idx_in[q], 16)
                    gather(q)
                with pool.Fori(1, BODIES) as o:
                    for q in range(R):
                        pool.wait_ge(idx_in[q], o * 16 + 16)
                        pool.wait_ge(scattered, (o - 1) * (2 * R) + 2 * q + 2)
                        pool.sem_inc(issue, 1)
                        gather(q)

            @block.tensor
            def _(pe):
                def turn(g, q, first):
                    pe.wait_ge(hot_made, g + 1)
                    if not first:
                        pe.wait_ge(hotT_made, g)
                    for k in range(G):
                        last = nc.tensor.transpose(hotT_ps[:, k, :], hot[q][:, k, :], s.ident_b[:, :])
                    last.then_inc(hot_turned, 1)

                def products(g, q, first):
                    tiles = load_values(nc, mybir.EngineType.PE, tile_of[0:1, bass.ds(g * G, G)], TILES - 1)
                    pe.wait_ge(hotT_made, g + 1)
                    for half in range(2):
                        if not first:
                            pe.wait_ge(pre_used, g * 2 + half - 1)
                        for k in range(4):
                            for part in range(3):
                                last = nc.tensor.matmul(pre[:, half, k, :], hotT[q % 2][:, 4 * half + k, :],
                                                        s.split[:, bass.ds(tiles[4 * half + k], 1), part, :],
                                                        start=(part == 0), stop=(part == 2))
                        last.then_inc(pre_made, 1)

                def scatter(g, q, first):
                    pe.wait_ge(hotw_made, g + 1)
                    for half in range(2):
                        if not first:
                            pe.wait_ge(added, g * 8 + 4 * half - 4)
                        for k in range(4):
                            last = nc.tensor.matmul(out[:, half, k, 0:W], hotw[q % 2][:, 4 * half + k, :],
                                                    bx[q][:, 4 * half + k, D:D + W], start=True, stop=True)
                        last.then_inc(scattered, 1)

                pe.wait_ge(zeroed, R)
                pe.wait_ge(steps_in, 32)
                for q in range(R):
                    if q >= 1:
                        products(q - 1, q - 1, q == 1)
                    turn(q, q, q == 0)
                    if q >= 2:
                        scatter(q - 2, q - 2, q == 2)
                with pe.Fori(1, BODIES) as o:
                    for q in range(R):
                        products(o * R + (q - 1), (q - 1) % R, False)
                        turn(o * R + q, q, False)
                        scatter(o * R + (q - 2), (q - 2) % R, False)
                products(GROUPS - 1, R - 1, False)
                scatter(GROUPS - 2, R - 2, False)
                scatter(GROUPS - 1, R - 1, False)

            @block.scalar
            def _(act):
                act.wait_ge(w_in, 32)
                act.wait_ge(zeroed, R + 1)

                def turn_evac(g, q, first):
                    act.wait_ge(hot_turned, g + 1)
                    if not first:
                        act.wait_ge(pre_made, g * 2 - 2)
                    act.sem_inc(act_go, 1)
                    nc.scalar.copy(hotT[q % 2][:, :, :], hotT_ps[:, :, :]).then_inc(hotT_made, 1)

                def weigh(g, q, first):
                    act.wait_ge(dotted, g + 1)
                    act.sem_inc(act_go, 1)
                    nc.scalar.activation(sig[:, q % 2, :], logit[:, q % 2, :], ACT.Sigmoid,
                                         bias=b2[:, 0:1]).then_inc(sig_made, 1)
                    act.wait_ge(sig_made, g + 1)
                    act.sem_inc(act_go, 1)
                    nc.scalar.activation(mask[:, q % 2, :], sig[:, q % 2, :], ACT.Identity,
                                         bias=tiny[:, 0:1]).then_inc(mask_made, 1)
                    act.wait_ge(mask_made, g + 1)
                    if not first:
                        act.wait_ge(scattered, g * 2 - 2)
                    act.sem_inc(act_go, 1)
                    for k in range(G):
                        last = nc.scalar.activation(hotw[q % 2][:, k, :], hot[q][:, k, :], ACT.Copy,
                                                    scale=mask[:, q % 2, k:k + 1])
                    last.then_inc(hotw_made, 1)

                for q in range(R):
                    turn_evac(q, q, q < 2)
                    if q >= 1:
                        weigh(q - 1, q - 1, q < 3)
                with act.Fori(1, BODIES) as o:
                    for q in range(R):
                        turn_evac(o * R + q, q, False)
                        weigh(o * R + (q - 1), (q - 1) % R, False)
                weigh(GROUPS - 1, R - 1, False)

            @block.vector
            def _(dve):
                dve.memset(tiny[:, :], 1e-30)
                dve.memset(acc[:, :, 0:W], 0.0).then_inc(zeroed, 1)
                dve.wait_ge(w_in, 32)
                dve.wait_ge(steps_in, 32)
                dve.wait_ge(zeroed, R + 1)

                def start(g, q, older, tiles):
                    if g is not None and used(g, R):
                        dve.wait_ge(hotw_made, g - (R - 1))
                    for k in range(G):
                        if g is not None:
                            last = dve.tensor_scalar(hot[q][:, k, :], s.lane_b[:, :],
                                                     place_of[:, bass.ds(g * G + k, 1)], None, ALU.is_equal)
                            if k == G - 1:
                                last.then_inc(hot_made, 1)
                        if older is not None:
                            if k % 4 == 0:
                                dve.wait_ge(scattered, older * 2 + k // 4 + 1)
                            if used(older, 1) or k:
                                dve.wait_ge(added, older * 8 + k)
                            slot = acc[:, bass.ds(tiles[k], 1), 0:W]
                            dve.tensor_tensor(slot, slot, out[:, k // 4, k % 4:k % 4 + 1, 0:W],
                                              ALU.add).then_inc(added, 1)

                def finish(g, q, round_):
                    dve.wait_ge(rows_in[q], (round_ + 1) * (16 * G))
                    if used(g, 1):
                        dve.wait_ge(dotted, g)
                    for half in range(2):
                        dve.wait_ge(pre_made, g * 2 + half + 1)
                        dve.tensor_tensor(h[:, half], pre[:, half], bx[q][:, 4 * half:4 * half + 4, 0:D],
                                          ALU.add).then_inc(pre_used, 1)
                    if used(g, 2):
                        dve.wait_ge(sig_made, g - 1)
                    for half in range(2):
                        dve.wait_ge(pre_used, g * 2 + half + 1)
                        for k in range(4 * half, 4 * half + 4):
                            last = dve.scalar_tensor_tensor(h[:, half, k % 4, :], h[:, half, k % 4, :], 0.0, w2[:, :],
                                                            ALU.max, ALU.mult, accum_out=logit[:, q % 2, k:k + 1])
                    last.then_inc(dotted, 1)

                def tiles_for(g):
                    return load_values(nc, mybir.EngineType.DVE, tile_of[0:1, bass.ds(g * G, G)], TILES - 1)

                for q in range(R):
                    start(q, q, q - 3 if q >= 3 else None, tiles_for(0) if q >= 3 else None)
                    if q >= 1:
                        finish(q - 1, q - 1, 0)
                with dve.Fori(1, BODIES) as o:
                    for q in range(R):
                        start(o * R + q, q, o * R + (q - 3), tiles_for(o * R + (q - 3)))
                        finish(o * R + (q - 1), (q - 1) % R, o - 1 if q == 0 else o)
                start(None, None, GROUPS - 3, tiles_for(GROUPS - 3))
                finish(GROUPS - 1, R - 1, BODIES - 1)
                start(None, None, GROUPS - 2, tiles_for(GROUPS - 2))
                start(None, None, GROUPS - 1, tiles_for(GROUPS - 1))


def weights_stage(nc, s, ins):
    with ExitStack() as ctx:
        sb = lambda name, shape, dt: ctx.enter_context(nc.sbuf_tensor(name, shape, dt))
        ps = lambda name, shape: ctx.enter_context(nc.psum_tensor(name, shape, F32))
        sem = ctx.enter_context(stage_semaphores(nc))
        raw = sb("w1_raw", [P, 4, D], F32)
        total = sb("w1_total", [P, 4], F32)
        mean = sb("w1_mean", [P, 4], F32)
        w2 = sb("w2_raw", [P, D], F32)
        wih, whh = sb("wih_raw", [P, 3, D], F32), sb("whh_raw", [P, 3, D], F32)
        w2T, wihT = sb("w2T", [P, D], F32), sb("wihT", [P, 3 * D], F32)
        ln_b, b2 = sb("ln_b_col", [P, 1], F32), sb("b2_col", [P, 1], F32)
        u = sb("u", [P, 1], F32)
        fold, whhT = sb("fold", [P, 3 * D], F32), sb("whhT_sb", [P, 3 * D], F32)
        bi, bh = sb("b_ih_row", [1, 3 * D], F32), sb("b_hh_row", [1, 3 * D], F32)
        vrow, brow = sb("v_row", [1, 4 * D], F32), sb("b_row", [1, 4 * D], F32)
        wT_ps, hT_ps, m_ps = ps("wT_ps", [P, 4, D]), ps("hT_ps", [P, 4, D]), ps("m_ps", [P, 4, D])
        u_ps, v_ps = ps("u_ps", [P, 512]), ps("v_ps", [P, 512])
        w_in, zeroed, chain = sem("weights_in"), sem("w_zeroed"), sem("w_chain")
        turned, copied, folded, rows_done = sem("w_turned"), sem("w_copied"), sem("w_folded"), sem("rows_done")
        rows_out = sem("rows_out")
        row = lambda name: ins[name].rearrange("(a d) -> a d", a=1)
        with nc.Block() as block:
            @block.sync
            def _(sp):
                w1 = ins["L1_gnn_W1"]
                sp.wait_ge(zeroed, 1)
                sp.dma_start(raw[:, 0:2, :], w1[0:2 * D, :].rearrange("(j p) d -> p j d", p=P)).then_inc(w_in, 16)
                sp.dma_start(raw[0:DE, 2, :], w1[2 * D:2 * D + DE, :]).then_inc(w_in, 16)
                sp.dma_start(raw[0:1, 3, :], row("L1_gnn_b1")).then_inc(w_in, 16)
                sp.dma_start(w2[:, :], ins["L1_gnn_W2"]).then_inc(w_in, 16)
                sp.dma_start(wih[:, :, :], ins["L1_gnn_W_ih"].rearrange("(j p) d -> p j d", p=P)).then_inc(w_in, 16)
                sp.dma_start(whh[:, :, :], ins["L1_gnn_W_hh"].rearrange("(j p) d -> p j d", p=P)).then_inc(w_in, 16)
                sp.dma_start(ln_b[:, :], ins["L1_gnn_ln_b"].rearrange("(d a) -> d a", a=1)).then_inc(w_in, 16)
                sp.dma_start(b2[:, :], ins["L1_gnn_b2"].rearrange("(d a) -> d a", a=1)).then_inc(w_in, 16)
                sp.dma_start(bi[:, :], row("L1_gnn_b_ih")).then_inc(w_in, 16)
                sp.dma_start(bh[:, :], row("L1_gnn_b_hh")).then_inc(w_in, 16)
                sp.wait_ge(rows_done, 3)
                sp.dma_start(s.aug_w[0:1, :], vrow[:, :]).then_inc(rows_out, 16)
                sp.dma_start(s.aug_w[1:2, :], brow[:, :]).then_inc(rows_out, 16)
                sp.dma_start(s.wfold[:, :], fold[:, :]).then_inc(rows_out, 16)
                sp.dma_start(s.whh[:, :], whhT[:, :]).then_inc(rows_out, 16)
                sp.wait_ge(rows_out, 64)

            @block.tensor
            def _(pe):
                pe.wait_ge(w_in, 16 * 10)
                nc.tensor.transpose(wT_ps[:, 3, :], w2[:, :], s.ident_f[:, :])
                for j in range(3):
                    nc.tensor.transpose(wT_ps[:, j, :], wih[:, j, :], s.ident_f[:, :])
                for j in range(3):
                    last = nc.tensor.transpose(hT_ps[:, j, :], whh[:, j, :], s.ident_f[:, :])
                last.then_inc(turned, 1)
                nc.tensor.matmul(u_ps[:, 0:1], w2[:, :], ln_b[:, :], start=True, stop=True).then_inc(turned, 1)
                pe.wait_ge(copied, 4)
                nc.tensor.matmul(m_ps[:, 0:3, :], w2T[:, :], wihT[:, :], start=True, stop=True)
                nc.tensor.matmul(v_ps[0:1, 0:3 * D], u[:, :], wihT[:, :], start=True, stop=True).then_inc(folded, 1)

            @block.vector
            def _(dve):
                dve.memset(raw[:, 2:4, :], 0.0).then_inc(zeroed, 1)
                dve.memset(vrow[:, 3 * D:4 * D], 0.0)
                dve.wait_ge(w_in, 16 * 10)
                dve.reduce_sum(total[:, :], raw[:, :, :], axis=mybir.AxisListType.X).then_inc(chain, 1)
                dve.wait_ge(chain, 1)
                dve.tensor_scalar(mean[:, :], total[:, :], 1.0 / D, None, ALU.mult).then_inc(chain, 1)
                dve.wait_ge(chain, 2)
                for j in range(2):
                    dve.tensor_scalar(s.w1cd[:, j * D:(j + 1) * D], raw[:, j, :], mean[:, j:j + 1], None, ALU.subtract)
                dve.tensor_scalar(s.w1e[:, :], raw[0:DE, 2, :], mean[0:DE, 2:3], None, ALU.subtract)
                dve.memset(s.b1cd[:, D:2 * D], 0.0)
                dve.tensor_scalar(s.b1cd[:, 0:D], raw[0:1, 3, :], mean[0:1, 3:4], None, ALU.subtract)
                dve.wait_ge(turned, 1)
                dve.tensor_copy(w2T[:, :], wT_ps[:, 3, :]).then_inc(copied, 1)
                dve.tensor_copy(wihT[:, :], wT_ps[:, 0:3, :].rearrange("p j d -> p (j d)")).then_inc(copied, 1)
                dve.tensor_copy(whhT[:, :], hT_ps[:, 0:3, :].rearrange("p j d -> p (j d)")).then_inc(copied, 1)
                dve.wait_ge(turned, 2)
                dve.tensor_tensor(u[:, :], u_ps[:, 0:1], b2[:, :], ALU.add).then_inc(copied, 1)
                dve.tensor_tensor(brow[:, 0:2 * D], bi[:, 0:2 * D], bh[:, 0:2 * D], ALU.add)
                dve.tensor_copy(brow[:, 2 * D:3 * D], bi[:, 2 * D:3 * D])
                dve.tensor_copy(brow[:, 3 * D:4 * D], bh[:, 2 * D:3 * D]).then_inc(rows_done, 1)
                dve.wait_ge(folded, 1)
                dve.tensor_copy(fold[:, :], m_ps[:, 0:3, :].rearrange("p j d -> p (j d)")).then_inc(rows_done, 1)
                dve.tensor_copy(vrow[:, 0:3 * D], v_ps[0:1, 0:3 * D]).then_inc(rows_done, 1)


PAIRS = TILES // 2
assert TILES % 2 == 0 and PAIRS % 2 == 1


def run_pairs(engine, steps, lead, unroll=2):
    first = 4
    whole = (PAIRS - 1 - first) // unroll
    for i in range(first):
        steps(i, i % unroll, i // unroll)
    with engine.Fori(first // unroll, first // unroll + whole) as o:
        for u in range(unroll):
            steps(o * unroll + u, u, o)
    for i in range(first + unroll * whole, PAIRS + lead):
        steps(i, i % unroll, i // unroll)


def runs(i, back):
    return not isinstance(i, int) or 0 <= i - back < PAIRS


def past_first(i, n):
    return not isinstance(i, int) or i >= n


def node_stage0(nc, s, ins):
    with ExitStack() as ctx:
        sb = lambda name, shape, dt: ctx.enter_context(nc.sbuf_tensor(name, shape, dt))
        ps = lambda name, shape: ctx.enter_context(nc.psum_tensor(name, shape, F32))
        sem = ctx.enter_context(stage_semaphores(nc))
        x = [sb(f"n_x{i}", [P, 2, D], F32) for i in range(2)]
        wl, bl = sb("wl", [P, D], F32), sb("bl", [1, D], F32)
        has, half, den = sb("has", [P, TILES], F32), sb("half", [P, TILES], F32), sb("den", [P, TILES], F32)
        ka, kx = sb("ka", [P, TILES], F32), sb("kx", [P, TILES], F32)
        eps = sb("eps0", [P, 1], F32)
        scaled = [sb(f"scaled{i}", [P, 2, D], F32) for i in range(2)]
        mixed = [sb(f"mixed{i}", [P, 2, D], F32) for i in range(2)]
        mT = [sb(f"mT{i}", [P, 2, P], F32) for i in range(2)]
        y = [sb(f"y{i}", [P, 2, D], F32) for i in range(2)]
        stats, mv = sb("stats0", [P, 2, 2, 6], F32), sb("mv0", [P, 2, 2, 2], F32)
        std, rstd = sb("std0", [P, 2, 2], F32), sb("rstd0", [P, 2, 2], F32)
        x1 = [sb(f"x1_{i}", [P, 2, D], F32) for i in range(2)]
        x1T = [sb(f"x1T{i}", [P, 2, P], F32) for i in range(2)]
        cd = [sb(f"cd{i}", [P, 2, 2 * D], F32) for i in range(2)]
        rest = [sb(f"rest1_{i}", [P, 2, D], F32) for i in range(2)]
        mT_ps, y_ps, x1T_ps = ps("mT_ps", [P, 512]), ps("y_ps", [P, 2, 512]), ps("x1T_ps", [P, 512])
        cd_ps = ps("cd_ps", [P, 2, 2, 2 * D])
        w_in, x_pad = sem("wl_in"), sem("n_x_pad")
        x_in = [sem(f"n_x_in{i}") for i in range(2)]
        factors, chain = sem("factors"), sem("n_chain")
        scaled_made, mixed_made, mT_made, mT_evac, y_made = (
            sem("scaled_made"), sem("mixed_made"), sem("mT_made"), sem("mT_evac"), sem("y_made"))
        y_sum, var_made, std_made, rstd_made, x1_made = (
            sem("y_sum"), sem("var_made"), sem("std_made"), sem("rstd_made"), sem("x1_made"))
        stats_made = sem("stats_made")
        x1T_made, x1T_evac, cd_made, cd_evac = sem("x1T_made"), sem("x1T_evac"), sem("cd_made"), sem("cd_evac")
        hi_made, rest_made, mid_made, lo_made = sem("hi_made"), sem("rest_made"), sem("mid_made"), sem("lo_made")
        x1_out = [sem(f"x1_out{i}") for i in range(2)]
        c_out = [sem(f"c_out{i}") for i in range(2)]
        go, dve_go, sp_go = sem("n_go"), sem("n_dve_go"), sem("n_sp_go")
        acc = s.acc

        def pair(t, i):
            return t[:, bass.ds(i * 2, 2)]

        with nc.Block() as block:
            @block.sync
            def _(sp):
                sp.dma_start(wl[:, :], ins["L0_gnn_Wl"]).then_inc(w_in, 16)
                sp.dma_start(bl[:, :], ins["L0_gnn_bl"].rearrange("(a d) -> a d", a=1)).then_inc(w_in, 16)

                def rows_of(table, i):
                    return table[bass.ds(i * (2 * P), 2 * P), :].rearrange("(t p) d -> p t d", p=P)

                def move(i, store, parts, done):
                    table, tile = parts
                    if isinstance(i, int) and i == PAIRS - 1:
                        a = table[2 * i * P:(2 * i + 1) * P, :].rearrange("(t p) d -> p t d", p=P)
                        b = table[(TILES - 1) * P:N, :]
                        ends = ((a, tile[:, 0:1, :]), (b, tile[0:LASTROWS, 1, :]))
                    else:
                        ends = ((rows_of(table, i), tile),)
                    for d, t in ends:
                        sp.dma_start(*((d, t) if store else (t, d))).then_inc(done, 16)

                def steps(i, par, o):
                    if runs(i, 0):
                        if past_first(i, 2):
                            sp.wait_ge(y_sum, i - 1)
                            sp.sem_inc(sp_go, 1)
                        if isinstance(i, int) and i == PAIRS - 1:
                            sp.wait_ge(x_pad, 1)
                        move(i, False, (ins["x"], x[par][:, :, :]), x_in[par])
                    if runs(i, 1):
                        sp.wait_ge(x1_made, i)
                        sp.sem_inc(sp_go, 1)
                        move(i - 1, True, (s.x1, x1[1 - par][:, :, :]), x1_out[1 - par])
                    if runs(i, 2):
                        sp.wait_ge(cd_evac, i - 1)
                        sp.sem_inc(sp_go, 1)
                        move(i - 2, True, (s.c, cd[par][:, :, 0:D]), c_out[par])
                run_pairs(sp, steps, 2)
                for par in range(2):
                    n = len(range(par, PAIRS, 2)) + (par == (PAIRS - 1) % 2)
                    sp.wait_ge(x1_out[par], 16 * n)
                    sp.wait_ge(c_out[par], 16 * n)

            @block.gpsimd
            def _(pool):
                pool.wait_ge(y_sum, PAIRS - 2)
                nc.gpsimd.memset(x[(PAIRS - 1) % 2][:, 1, :], 0.0).then_inc(x_pad, 1)

            @block.scalar
            def _(act):
                act.wait_ge(factors, 1)

                def steps(i, par, o):
                    if runs(i, 0):
                        if past_first(i, 2):
                            act.wait_ge(mixed_made, i - 1)
                            act.sem_inc(go, 1)
                        for t in range(2):
                            last = nc.scalar.activation(scaled[par][:, t, :], acc[:, bass.ds(i * 2 + t, 1), 0:D],
                                                        ACT.Copy, scale=ka[:, bass.ds(i * 2 + t, 1)])
                        last.then_inc(scaled_made, 1)
                        act.wait_ge(mT_made, i + 1)
                        if past_first(i, 2):
                            act.wait_ge(y_made, i - 1)
                        act.sem_inc(go, 1)
                        nc.scalar.copy(mT[par][:, :, :], mT_ps[:, 0:2 * P]).then_inc(mT_evac, 1)
                    if runs(i, 1):
                        act.wait_ge(var_made, i)
                        act.sem_inc(go, 1)
                        nc.scalar.activation(std[:, 1 - par, :], mv[:, 1 - par, :, 1], ACT.Sqrt,
                                             bias=eps[:, 0:1]).then_inc(std_made, 1)
                    if runs(i, 2):
                        act.wait_ge(x1T_made, i - 1)
                        if past_first(i, 4):
                            act.wait_ge(cd_made, i - 3)
                        act.sem_inc(go, 1)
                        nc.scalar.copy(x1T[par][:, :, :], x1T_ps[:, 0:2 * P]).then_inc(x1T_evac, 1)
                        act.wait_ge(cd_made, i - 1)
                        if past_first(i, 4):
                            act.wait_ge(lo_made, i - 3)
                            act.wait_ge(c_out[par], o * 16 - 16)
                        act.sem_inc(go, 1)
                        nc.scalar.copy(cd[par][:, :, :], cd_ps[:, par]).then_inc(cd_evac, 1)
                        nc.scalar.copy(pair(s.split, i - 2)[:, :, 0, :], cd_ps[:, par, :, D:2 * D]).then_inc(hi_made, 1)
                        act.wait_ge(rest_made, i - 1)
                        act.sem_inc(go, 1)
                        nc.scalar.copy(pair(s.split, i - 2)[:, :, 1, :], rest[par][:, :, :]).then_inc(mid_made, 1)

                run_pairs(act, steps, 2)

            @block.tensor
            def _(pe):
                pe.wait_ge(w_in, 32)

                def steps(i, par, o):
                    if runs(i, 0):
                        pe.wait_ge(mixed_made, i + 1)
                        if past_first(i, 1):
                            pe.wait_ge(mT_evac, i)
                        for t in range(2):
                            last = nc.tensor.transpose(mT_ps[:, t * P:(t + 1) * P], mixed[par][:, t, :], s.ident_f[:, :])
                        last.then_inc(mT_made, 1)
                    if runs(i, 2):
                        pe.wait_ge(x1_made, i - 1)
                        if past_first(i, 3):
                            pe.wait_ge(x1T_evac, i - 2)
                        for t in range(2):
                            last = nc.tensor.transpose(x1T_ps[:, t * P:(t + 1) * P], x1[par][:, t, :], s.ident_f[:, :])
                        last.then_inc(x1T_made, 1)
                    if runs(i, 0):
                        pe.wait_ge(mT_evac, i + 1)
                        if past_first(i, 2):
                            pe.wait_ge(y_sum, i - 1)
                        for t in range(2):
                            nc.tensor.matmul(y_ps[:, par, t * D:(t + 1) * D], mT[par][:, t, :], wl[:, :],
                                             start=True, stop=False)
                            last = nc.tensor.matmul(y_ps[:, par, t * D:(t + 1) * D], s.ones_f[0:1, :], bl[:, :],
                                                    start=False, stop=True)
                        last.then_inc(y_made, 1)
                    if runs(i, 2):
                        pe.wait_ge(x1T_evac, i - 1)
                        if past_first(i, 4):
                            pe.wait_ge(hi_made, i - 3)
                        for t in range(2):
                            nc.tensor.matmul(cd_ps[:, par, t, :], x1T[par][:, t, :], s.w1cd[:, :],
                                             start=True, stop=False)
                            last = nc.tensor.matmul(cd_ps[:, par, t, :], s.ones_f[0:1, :], s.b1cd[:, :],
                                                    start=False, stop=True)
                        last.then_inc(cd_made, 1)
                run_pairs(pe, steps, 2)

            @block.vector
            def _(dve):
                sums = acc[:, :, D]
                dve.memset(eps[:, :], 1e-5)
                dve.tensor_scalar(half[:, :], sums, 0.0, 0.5, ALU.is_gt, ALU.mult).then_inc(chain, 1)
                dve.tensor_scalar(den[:, :], sums, 1e-9, None, ALU.add).then_inc(chain, 1)
                dve.wait_ge(chain, 2)
                dve.reciprocal(has[:, :], den[:, :]).then_inc(chain, 1)
                dve.tensor_scalar(kx[:, :], half[:, :], -1.0, 1.0, ALU.mult, ALU.add)
                dve.wait_ge(chain, 3)
                dve.tensor_tensor(ka[:, :], half[:, :], has[:, :], ALU.mult).then_inc(factors, 1)
                dve.wait_ge(factors, 1)

                def steps(i, par, o):
                    other = 1 - par
                    if runs(i, 0):
                        dve.wait_ge(scaled_made, i + 1)
                        last_one = isinstance(i, int) and i == PAIRS - 1
                        dve.wait_ge(x_in[par], o * 16 + 16 + 16 * last_one)
                        if past_first(i, 2):
                            dve.wait_ge(mT_made, i - 1)
                        for t in range(2):
                            last = dve.scalar_tensor_tensor(mixed[par][:, t, :], x[par][:, t, :],
                                                            kx[:, bass.ds(i * 2 + t, 1)], scaled[par][:, t, :],
                                                            ALU.mult, ALU.add)
                        last.then_inc(mixed_made, 1)
                    if runs(i, 1):
                        dve.wait_ge(std_made, i)
                        dve.reciprocal(rstd[:, other, :], std[:, other, :]).then_inc(rstd_made, 1)
                        dve.wait_ge(rstd_made, i)
                        if past_first(i, 3):
                            dve.wait_ge(x1T_made, i - 2)
                            dve.wait_ge(x1_out[other], o * 16 - 16 * other)
                        for t in range(2):
                            last = dve.tensor_scalar(x1[other][:, t, :], y[other][:, t, :], mv[:, other, t, 0:1],
                                                     rstd[:, other, t:t + 1], ALU.subtract, ALU.mult)
                        last.then_inc(x1_made, 1)
                    if runs(i, 0):
                        dve.wait_ge(y_made, i + 1)
                        dve.scalar_tensor_tensor(y[par][:, :, :].rearrange("p t d -> p (t d)"),
                                                 y_ps[:, par, 0:2 * D], 0.0,
                                                 x[par][:, :, :].rearrange("p t d -> p (t d)"),
                                                 ALU.max, ALU.add).then_inc(y_sum, 1)
                        dve.wait_ge(y_sum, i + 1)
                        for t in range(2):
                            last = dve.bn_stats(stats[:, par, t, :], y[par][:, t, :])
                        last.then_inc(stats_made, 1)
                        dve.wait_ge(stats_made, i + 1)
                        dve.sem_inc(dve_go, 1)
                        for t in range(2):
                            last = dve.bn_aggr(mv[:, par, t, :], stats[:, par, t, :])
                        last.then_inc(var_made, 1)
                    if runs(i, 2):
                        dve.wait_ge(hi_made, i - 1)
                        if past_first(i, 4):
                            dve.wait_ge(lo_made, i - 3)
                        dve.tensor_tensor(rest[par][:, :, :], cd[par][:, :, D:2 * D], pair(s.split, i - 2)[:, :, 0, :],
                                          ALU.subtract).then_inc(rest_made, 1)
                        dve.wait_ge(mid_made, i - 1)
                        dve.tensor_tensor(pair(s.split, i - 2)[:, :, 2, :], rest[par][:, :, :],
                                          pair(s.split, i - 2)[:, :, 1, :], ALU.subtract).then_inc(lo_made, 1)
                run_pairs(dve, steps, 2)


def loop_groups(engine, steps, lead):
    for q in range(R):
        steps(q, q, 0)
    with engine.Fori(1, BODIES) as o:
        for q in range(R):
            steps(o * R + q, q, o)
    for q in range(lead):
        steps(GROUPS + q, q, BODIES)


def has(g, back):
    return not isinstance(g, int) or 0 <= g - back < GROUPS


def used(g, n):
    return not isinstance(g, int) or g >= n


def edge_stage1(nc, s, ins):
    W = D + 1
    with ExitStack() as ctx:
        sb = lambda name, shape, dt: ctx.enter_context(nc.sbuf_tensor(name, shape, dt))
        ps = lambda name, shape, dt: ctx.enter_context(nc.psum_tensor(name, shape, dt))
        sem = ctx.enter_context(stage_semaphores(nc))
        step_rows, place_of = sb("step_rows1", [2, STEPS], I16), sb("places1", [P, STEPS], BF16)
        tile_of, edge_of = step_rows[0:1, :], step_rows[1:2, :]
        idx = [sb(f"idx1_{q}", [P, G], I32) for q in range(R)]
        crows = [sb(f"crows{q}", [P, G, D], F32) for q in range(R)]
        ef = [sb(f"ef{q}", [P, G, DE], F32) for q in range(R)]
        hot = [sb(f"hot1_{q}", [P, G, P], BF16) for q in range(R)]
        hotT = [sb(f"hotT1_{i}", [P, G, P], BF16) for i in range(2)]
        efT = [sb(f"efT{i}", [P, G // 2, P], F32) for i in range(2)]
        w1e2, gw2 = sb("w1e2", [P, 2, D], F32), sb("gate_w2", [P, 2], F32)
        hotw = [sb(f"hotw1_{i}", [P, G, P], F32) for i in range(2)]
        h = [sb(f"h1_{i}", [P, G, D], F32) for i in range(2)]
        z = [sb(f"z{i}", [P, G, W], F32) for i in range(2)]
        sq = sb("sq", [P, 4, D], BF16)
        ss, lnv, rstd = (sb(n, [P, 2, G], F32) for n in ("ss", "lnv", "rstd1"))
        eg, eg1, gate = (sb(n, [P, 2, G], F32) for n in ("eg", "eg1", "gate"))
        ln_g, neg_b, gb, eps = (sb("ln_g", [P, D], F32), sb("neg_b", [P, D], F32), sb("neg_gate_b", [P, 1], F32), sb("eps1", [P, 1], F32))
        hotT_ps = ps("hotT1_ps", [P, G, P], BF16)
        efT_ps = ps("efT_ps", [P, 4, P], F32)
        pre = ps("pre1", [P, 2, 4, D], F32)
        out = ps("scattered1", [P, 3, 512], F32)
        gate_ps = ps("gate_ps", [P, 512], F32)
        w_in, zeroed, steps_in, negated = sem("w1_in"), sem("zeroed1"), sem("steps1_in"), sem("negated")
        idx_in = [sem(f"idx1_in{q}") for q in range(R)]
        rows_in = [sem(f"c_in{q}") for q in range(R)]
        ef_in = [sem(f"ef_in{q}") for q in range(R)]
        hot_made, hot_turned, hotT_made = sem("hot1_made"), sem("hot1_turned"), sem("hotT1_made")
        ef_turned, efT_made = sem("ef_turned"), sem("efT_made")
        pre_made, pre_used, gate_made, gate_read = sem("pre1_made"), sem("pre1_used"), sem("gatel_made"), sem("gate_read")
        ss_made, ln_made, rstd_made = sem("ss_made"), sem("ln_made"), sem("rstd1_made")
        eg1_made, gates_made, hotw_made = sem("eg1_made"), sem("gates_made"), sem("hotw1_made")
        scaled, z_made = sem("z_scaled"), sem("z_made")
        scattered, added = sem("scattered1_up"), sem("added1")
        issue, act_go, pe_go, sp_go = sem("issue1"), sem("act_go1"), sem("pe_go1"), sem("sp_go1")
        acc = s.acc
        slot = [(k // 3, (k % 3) * W) for k in range(G)]

        with nc.Block() as block:
            @block.sync
            def _(sp):
                sp.dma_start(tile_of, s.tile_of[1][:, :]).then_inc(steps_in, 16)
                sp.dma_start(edge_of, s.edge_of[:, :]).then_inc(steps_in, 16)
                sp.dma_start(place_of[:, :], s.place_of[1][:, :]).then_inc(steps_in, 16)
                row = lambda name, n: ins[name].rearrange("(a d) -> a d", a=1).to_broadcast([P, n])
                sp.dma_start(ln_g[:, :], row("L1_gnn_ln_g", D)).then_inc(w_in, 16)
                sp.dma_start(neg_b[:, :], row("L1_gnn_ln_b", D)).then_inc(w_in, 16)
                sp.dma_start(gb[:, :], row("L1_gnn_gate_b", 1)).then_inc(w_in, 16)
                sp.wait_ge(zeroed, 1)
                for half in range(2):
                    there = slice(half * DE, (half + 1) * DE)
                    sp.dma_start(w1e2[there, half, :], s.w1e[:, :]).then_inc(w_in, 16)
                    sp.dma_start(gw2[there, half:half + 1], ins["L1_gnn_gate_w"]).then_inc(w_in, 16)
                sp.wait_ge(steps_in, 48)

                def load(g, q):
                    sp.dma_start(idx[q][:, :], s.gather_of[1][:, bass.ds(g * G, G)]).then_inc(idx_in[q], 16)
                    edges = load_values(nc, mybir.EngineType.SP, edge_of[0:1, bass.ds(g * G, G)], (E - P) // 64)
                    for k in range(G):
                        sp.dma_start(ef[q][:, k, :],
                                     ins["edge_attr_64"][bass.ds(edges[k] * 64, P), :]).then_inc(ef_in[q], 16)
                for q in range(R):
                    load(q, q)
                with sp.Fori(1, BODIES) as o:
                    for q in range(R):
                        sp.wait_ge(rows_in[q], o * (16 * G))
                        sp.sem_inc(sp_go, 1)
                        sp.wait_ge(ef_turned, (o - 1) * R + q + 1)
                        sp.sem_inc(sp_go, 1)
                        load(o * R + q, q)

            @block.gpsimd
            def _(pool):
                pool.wait_ge(zeroed, 1)
                for i in range(2):
                    nc.gpsimd.memset(z[i][:, :, D:W], 1.0).then_inc(zeroed, 1)

                def gather(q):
                    for k in range(G):
                        pool.indirect_dma_start(
                            out=crows[q][:, k, :], out_offset=None, in_=s.c[:, :],
                            in_offset=bass.IndirectOffsetOnAxis(ap=idx[q][:, k:k + 1], axis=0),
                        ).then_inc(rows_in[q], 16)
                for q in range(R):
                    pool.wait_ge(idx_in[q], 16)
                    gather(q)
                with pool.Fori(1, BODIES) as o:
                    for q in range(R):
                        pool.wait_ge(idx_in[q], o * 16 + 16)
                        pool.wait_ge(pre_used, (o - 1) * (2 * R) + 2 * q + 2)
                        pool.sem_inc(issue, 1)
                        gather(q)

            @block.tensor
            def _(pe):
                pe.wait_ge(steps_in, 48)
                pe.wait_ge(w_in, 16 * 7)
                pe.wait_ge(zeroed, 3)
                pe.wait_ge(added, 1)

                def steps(g, q, o):
                    if has(g, 1):
                        par = (q - 1) % 2
                        tiles = load_values(nc, mybir.EngineType.PE, tile_of[0:1, bass.ds((g - 1) * G, G)], TILES - 1)
                        pe.wait_ge(hotT_made, g)
                        pe.wait_ge(efT_made, g)
                        for half in range(2):
                            if used(g, 2):
                                pe.wait_ge(pre_used, g * 2 + half - 3)
                            for k in range(4):
                                for part in range(3):
                                    nc.tensor.matmul(pre[:, half, k, :], hotT[par][:, 4 * half + k, :],
                                                     s.split[:, bass.ds(tiles[4 * half + k], 1), part, :],
                                                     start=(part == 0), stop=False)
                                last = nc.tensor.matmul(pre[:, half, k, :], efT[par][:, 2 * half + k // 2, :],
                                                        w1e2[:, k % 2, :], start=False, stop=True)
                            last.then_inc(pre_made, 1)
                        if used(g, 2):
                            pe.wait_ge(gate_read, g - 1)
                        for k in range(G // 2):
                            last = nc.tensor.matmul(gate_ps[:, 2 * k:2 * k + 2], efT[par][:, k, :], gw2[:, :],
                                                    start=True, stop=True)
                        last.then_inc(gate_made, 1)
                    if has(g, 0):
                        pe.wait_ge(ef_in[q], o * (16 * G) + 16 * G)
                        if used(g, 1):
                            pe.wait_ge(efT_made, g)
                        for k in range(G // 2):
                            last = nc.tensor.transpose(efT_ps[:, k, :],
                                                       ef[q][:, 2 * k:2 * k + 2, :].rearrange("p a d -> p (a d)"),
                                                       s.ident_f[:, :])
                        last.then_inc(ef_turned, 1)
                        pe.wait_ge(hot_made, g + 1)
                        if used(g, 1):
                            pe.wait_ge(hotT_made, g)
                        for k in range(G):
                            last = nc.tensor.transpose(hotT_ps[:, k, :], hot[q][:, k, :], s.ident_b[:, :])
                        last.then_inc(hot_turned, 1)
                    if has(g, 3):
                        par = (q - 3) % 2
                        pe.wait_ge(hotw_made, g - 2)
                        for k in range(G):
                            if k % 4 == 0:
                                pe.wait_ge(z_made, g * 2 - 5 + k // 4)
                            bank, at = slot[k]
                            if used(g, 4) and at == 0:
                                pe.wait_ge(added, (g - 4) * G + min(k + 3, G) + 1)
                            last = nc.tensor.matmul(out[:, bank, at:at + W], hotw[par][:, k, :], z[par][:, k, :],
                                                    start=True, stop=True)
                            if k in (2, 5, 7):
                                last.then_inc(scattered, 1)
                loop_groups(pe, steps, 4)

            @block.scalar
            def _(act):
                act.preload_act_table_set("natural_log_exp_and_others")
                act.wait_ge(negated, 2)

                def steps(g, q, o):
                    par, other = q % 2, 1 - q % 2
                    if has(g, 2):
                        for half in range(2):
                            if used(g, 3) or half:
                                act.wait_ge(ss_made, g * 2 - 4 + half)
                            act.wait_ge(pre_used, g * 2 + half - 3)
                            act.sem_inc(act_go, 1)
                            for k in range(4 * half, 4 * half + 4):
                                last = nc.scalar.activation(sq[:, k % 4, :], h[par][:, k, :], ACT.Square,
                                                            accum_out=ss[:, par, k:k + 1])
                            last.then_inc(ss_made, 1)
                        act.wait_ge(ss_made, g * 2 - 2)
                        act.sem_inc(act_go, 1)
                        nc.scalar.activation(lnv[:, par, :], ss[:, par, :], ACT.Ln, bias=eps[:, 0:1],
                                             scale=1.0 / D).then_inc(ln_made, 1)
                    if has(g, 3):
                        act.wait_ge(gates_made, g - 2)
                        act.sem_inc(act_go, 1)
                        for k in range(G):
                            last = nc.scalar.activation(hotw[other][:, k, :], hot[(q - 3) % R][:, k, :], ACT.Copy,
                                                        scale=gate[:, other, k:k + 1])
                        last.then_inc(hotw_made, 1)
                    if has(g, 2):
                        act.wait_ge(ln_made, g - 1)
                        if used(g, 4):
                            act.wait_ge(scaled, g * 2 - 6)
                        act.sem_inc(act_go, 1)
                        nc.scalar.activation(rstd[:, par, :], lnv[:, par, :], ACT.Exp,
                                             scale=-0.5).then_inc(rstd_made, 1)
                    if has(g, 0):
                        act.wait_ge(ef_turned, g + 1)
                        if used(g, 2):
                            act.wait_ge(gate_made, g - 1)
                        act.sem_inc(act_go, 1)
                        nc.scalar.copy(efT[par][:, :, :], efT_ps[:, :, :]).then_inc(efT_made, 1)
                        act.wait_ge(hot_turned, g + 1)
                        act.sem_inc(act_go, 1)
                        nc.scalar.copy(hotT[par][:, :, :], hotT_ps[:, :, :]).then_inc(hotT_made, 1)
                    if has(g, 1):
                        act.wait_ge(gate_made, g)
                        if used(g, 3):
                            act.wait_ge(eg1_made, g - 2)
                        act.sem_inc(act_go, 1)
                        nc.scalar.activation(eg[:, other, :], gate_ps[:, 0:G], ACT.Exp, bias=gb[:, 0:1],
                                             scale=-1.0).then_inc(gate_read, 1)
                loop_groups(act, steps, 3)

            @block.vector
            def _(dve):
                dve.memset(w1e2[:, :, :], 0.0)
                dve.memset(gw2[:, :], 0.0).then_inc(zeroed, 1)
                dve.memset(eps[:, :], 1e-5)
                dve.memset(acc[:, :, D + 1:D + 2], 1.0)
                dve.memset(acc[:, :, 0:W], 0.0).then_inc(added, 1)
                dve.wait_ge(w_in, 16 * 7)
                dve.wait_ge(steps_in, 48)
                dve.tensor_scalar(neg_b[:, :], neg_b[:, :], -1.0, None, ALU.mult).then_inc(negated, 1)
                dve.tensor_scalar(gb[:, :], gb[:, :], -1.0, None, ALU.mult).then_inc(negated, 1)
                dve.wait_ge(negated, 2)
                dve.wait_ge(zeroed, 3)
                spread_b = neg_b[:, :].rearrange("p (a d) -> p a d", a=1).to_broadcast([P, 4, D])

                def steps(g, q, o):
                    par, other = q % 2, 1 - q % 2
                    if has(g, 0):
                        if used(g, R):
                            dve.wait_ge(hotw_made, g - (R - 1))
                        for k in range(G):
                            last = dve.tensor_scalar(hot[q][:, k, :], s.lane_b[:, :],
                                                     place_of[:, bass.ds(g * G + k, 1)], None, ALU.is_equal)
                        last.then_inc(hot_made, 1)
                    if has(g, 3):
                        dve.wait_ge(rstd_made, g - 2)
                    if has(g, 4):
                        tiles = load_values(nc, mybir.EngineType.DVE, tile_of[0:1, bass.ds((g - 4) * G, G)], TILES - 1)
                    for k in range(G):
                        if has(g, 3):
                            last = dve.scalar_tensor_tensor(z[other][:, k, 0:D], h[other][:, k, :],
                                                            rstd[:, other, k:k + 1], ln_g[:, :], ALU.mult, ALU.mult)
                            if k % 4 == 3:
                                last.then_inc(scaled, 1)
                        if has(g, 4):
                            bank, at = slot[k]
                            if at == 0:
                                dve.wait_ge(scattered, g * 3 + bank - 11)
                            dve.wait_ge(added, (g - 4) * G + k + 1)
                            place = acc[:, bass.ds(tiles[k], 1), 0:W]
                            dve.tensor_tensor(place, place, out[:, bank:bank + 1, at:at + W],
                                              ALU.add).then_inc(added, 1)
                        if has(g, 3) and k % 4 == 3:
                            half = k // 4
                            dve.wait_ge(scaled, g * 2 + half - 5)
                            part = z[other][:, 4 * half:4 * half + 4, 0:D]
                            dve.tensor_tensor(part, part, spread_b, ALU.max).then_inc(z_made, 1)
                    if has(g, 1):
                        p1 = (q - 1) % R
                        dve.wait_ge(rows_in[p1], o * (16 * G) + (0 if q == 0 else 16 * G))
                        if used(g, 3):
                            dve.wait_ge(scaled, g * 2 - 4)
                            dve.wait_ge(ss_made, g * 2 - 4)
                        for half in range(2):
                            dve.wait_ge(pre_made, g * 2 + half - 1)
                            dve.tensor_tensor(h[other][:, 4 * half:4 * half + 4, :], pre[:, half],
                                              crows[p1][:, 4 * half:4 * half + 4, :], ALU.add).then_inc(pre_used, 1)
                    if has(g, 2):
                        dve.wait_ge(gate_read, g - 1)
                        if used(g, 4):
                            dve.wait_ge(hotw_made, g - 3)
                        dve.tensor_scalar(eg1[:, par, :], eg[:, par, :], 1.0, None, ALU.add).then_inc(eg1_made, 1)
                        dve.wait_ge(eg1_made, g - 1)
                        dve.reciprocal(gate[:, par, :], eg1[:, par, :]).then_inc(gates_made, 1)
                loop_groups(dve, steps, 4)


def node_stage1(nc, s, ins, result):
    with ExitStack() as ctx:
        sb = lambda name, shape, dt: ctx.enter_context(nc.sbuf_tensor(name, shape, dt))
        ps = lambda name, shape: ctx.enter_context(nc.psum_tensor(name, shape, F32))
        sem = ctx.enter_context(stage_semaphores(nc))
        U = 4
        wfold, whh, aug_w = sb("wfold_sb", [P, 3 * D], F32), sb("whh_sb", [P, 3 * D], F32), sb("aug_sb", [2, 4 * D], F32)
        w_in = sem("gru_w_in")
        x = [sb(f"g_x{i}", [P, 2, D], F32) for i in range(U)]
        both = [sb(f"sums{i}", [P, 2, D + 2], F32) for i in range(2)]
        T = [sb(f"gT{i}", [P, 4, P], F32) for i in range(2)]
        augT = [sb(f"augT{i}", [2, 2, P], F32) for i in range(2)]
        rz = [sb(f"rz{i}", [P, 2, 2 * D], F32) for i in range(2)]
        t1, t2, new, diff, kept = ([sb(f"{n}{i}", [P, 2, D], F32) for i in range(2)]
                                   for n in ("t1_", "t2_", "new", "diff", "kept"))
        y = [sb(f"gy{i}", [P, 2, D], F32) for i in range(2)]
        stats, mv = sb("stats1", [P, 2, 2, 6], F32), sb("mv1", [P, TILES, 2], F32)
        std, rstd = sb("g_std", [P, TILES], F32), sb("g_rstd", [P, TILES], F32)
        eps = sb("g_eps", [P, 1], F32)
        T_ps, aug_ps = ps("T_ps", [P, 4, P]), ps("aug_ps", [P, 512])
        rz_ps, n_ps = ps("rz_ps", [P, 2, 2, 2 * D]), ps("n_ps", [P, 2, 2, 2 * D])
        x_pad = sem("g_x_pad")
        x_in = [sem(f"g_x_in{i}") for i in range(U)]
        both_made, T_made, T_evac, rz_made, n_made = (
            sem("both_made"), sem("T_made"), sem("T_evac"), sem("rz_made"), sem("n_made"))
        gates, t1_made, t2_made, new_made, diff_made, zd_made = (
            sem("g_gates"), sem("t1_made"), sem("t2_made"), sem("new_made"), sem("diff_made"), sem("zd_made"))
        kept_made, y_made, stats_made, var_made, std_made, rstd_made, o_made = (
            sem("kept_made"), sem("gy_made"), sem("g_stats"), sem("g_var"), sem("g_std_made"), sem("g_rstd_made"),
            sem("o_made"))
        stored, go, eps_made = sem("stored_out"), sem("g_go"), sem("g_eps_made")
        dve_go, aggr_made, sp_go = sem("g_dve_go"), sem("g_aggr_made"), sem("g_sp_go")
        mv2 = sb("mv_pair", [P, 2, 2, 2], F32)
        acc = s.acc
        CHUNK = 14
        STORES = TILES // CHUNK
        assert STORES * CHUNK == TILES

        with nc.Block() as block:
            @block.sync
            def _(sp):
                for t, w in ((wfold, s.wfold), (whh, s.whh), (aug_w, s.aug_w)):
                    sp.dma_start(t[:, :], w[:, :]).then_inc(w_in, 16)

                def steps(i, u, o):
                    if past_first(i, U):
                        sp.wait_ge(y_made, i - (U - 1))
                        sp.sem_inc(sp_go, 1)
                    if isinstance(i, int) and i == PAIRS - 1:
                        sp.wait_ge(x_pad, 1)
                        a = s.x1[2 * i * P:(2 * i + 1) * P, :].rearrange("(t p) d -> p t d", p=P)
                        sp.dma_start(x[u][:, 0:1, :], a).then_inc(x_in[u], 16)
                        sp.dma_start(x[u][0:LASTROWS, 1, :], s.x1[(TILES - 1) * P:N, :]).then_inc(x_in[u], 16)
                    else:
                        a = s.x1[bass.ds(i * (2 * P), 2 * P), :].rearrange("(t p) d -> p t d", p=P)
                        sp.dma_start(x[u][:, :, :], a).then_inc(x_in[u], 16)
                run_pairs(sp, steps, 0, U)
                for c in range(STORES):
                    sp.wait_ge(o_made, c + 1)
                    full = CHUNK if c < STORES - 1 else CHUNK - 1
                    view = result[c * CHUNK * P:(c * CHUNK + full) * P, :].rearrange("(t p) d -> p t d", p=P)
                    sp.dma_start(view, acc[:, c * CHUNK:c * CHUNK + full, 0:D]).then_inc(stored, 16)
                sp.dma_start(result[(TILES - 1) * P:N, :], acc[0:LASTROWS, TILES - 1, 0:D]).then_inc(stored, 16)
                sp.wait_ge(stored, 16 * (STORES + 1))

            @block.gpsimd
            def _(pool):
                def steps(i, u, o):
                    if past_first(i, 2):
                        pool.wait_ge(T_made, i - 1)
                    nc.gpsimd.tensor_copy(both[u % 2][:, :, :], acc[:, bass.ds(i * 2, 2), :]).then_inc(both_made, 1)
                    if isinstance(i, int) and i == PAIRS - 1:
                        pool.wait_ge(y_made, PAIRS - U)
                        nc.gpsimd.memset(x[u][:, 1, :], 0.0).then_inc(x_pad, 1)
                run_pairs(pool, steps, 0, U)

            @block.tensor
            def _(pe):
                pe.wait_ge(w_in, 48)

                def steps(i, u, o):
                    par = u % 2
                    last_one = isinstance(i, int) and i == PAIRS - 1
                    pe.wait_ge(x_in[u], o * 16 + 16 + 16 * last_one)
                    pe.wait_ge(both_made, i + 1)
                    if past_first(i, 1):
                        pe.wait_ge(T_evac, i * 2)
                    for t in range(2):
                        nc.tensor.transpose(T_ps[:, t, :], both[par][:, t, 0:D], s.ident_f[:, :])
                        nc.tensor.transpose(T_ps[:, 2 + t, :], x[u][:, t, :], s.ident_f[:, :])
                        last = nc.tensor.transpose(aug_ps[0:2, t * P:(t + 1) * P], both[par][:, t, D:D + 2],
                                                   s.ident_f[:, :])
                    last.then_inc(T_made, 1)
                    pe.wait_ge(T_evac, i * 2 + 2)
                    if past_first(i, 2):
                        pe.wait_ge(gates, i - 1)
                    for t in range(2):
                        nc.tensor.matmul(rz_ps[:, par, t, :], T[par][:, t, :], wfold[:, 0:2 * D],
                                         start=True, stop=False)
                        nc.tensor.matmul(rz_ps[:, par, t, :], T[par][:, 2 + t, :], whh[:, 0:2 * D],
                                         start=False, stop=False)
                        last = nc.tensor.matmul(rz_ps[:, par, t, :], augT[par][:, t, :], aug_w[:, 0:2 * D],
                                                start=False, stop=True)
                    last.then_inc(rz_made, 1)
                    if past_first(i, 2):
                        pe.wait_ge(t2_made, i - 1)
                    for t in range(2):
                        for side, part, weight in ((0, T[par][:, t, :], wfold), (1, T[par][:, 2 + t, :], whh)):
                            half = n_ps[:, par, t, side * D:(side + 1) * D]
                            nc.tensor.matmul(half, part, weight[:, 2 * D:3 * D], start=True, stop=False)
                            last = nc.tensor.matmul(half, augT[par][:, t, :],
                                                    aug_w[:, (2 + side) * D:(3 + side) * D],
                                                    start=False, stop=True)
                    last.then_inc(n_made, 1)
                run_pairs(pe, steps, 0, U)

            @block.scalar
            def _(act):
                def steps(i, u, o):
                    par, other = u % 2, 1 - u % 2
                    if runs(i, 0):
                        act.wait_ge(T_made, i + 1)
                        if past_first(i, 2):
                            act.wait_ge(n_made, i - 1)
                        act.sem_inc(go, 1)
                        nc.scalar.copy(T[par][:, :, :], T_ps[:, :, :]).then_inc(T_evac, 1)
                        nc.scalar.copy(augT[par][:, :, :], aug_ps[0:2, 0:2 * P]).then_inc(T_evac, 1)
                    if runs(i, 1):
                        act.wait_ge(rz_made, i)
                        if past_first(i, 3):
                            act.wait_ge(zd_made, i - 2)
                        act.sem_inc(go, 1)
                        nc.scalar.activation(rz[other][:, :, :], rz_ps[:, other], ACT.Sigmoid).then_inc(gates, 1)
                        act.wait_ge(t2_made, i)
                        if past_first(i, 3):
                            act.wait_ge(kept_made, i - 2)
                        act.sem_inc(go, 1)
                        nc.scalar.activation(new[other][:, :, :], t2[other][:, :, :], ACT.Tanh).then_inc(new_made, 1)
                run_pairs(act, steps, 1, U)
                act.wait_ge(var_made, PAIRS)
                act.wait_ge(eps_made, 1)
                nc.scalar.activation(std[:, :], mv[:, :, 1], ACT.Sqrt, bias=eps[:, 0:1]).then_inc(std_made, 1)

            @block.vector
            def _(dve):
                dve.memset(eps[:, :], 1e-5).then_inc(eps_made, 1)

                def steps(i, u, o):
                    par, other = u % 2, 1 - u % 2
                    if runs(i, 1):
                        dve.wait_ge(gates, i)
                        dve.wait_ge(n_made, i)
                        dve.tensor_tensor(t1[other][:, :, :], rz[other][:, :, 0:D], n_ps[:, other, :, D:2 * D],
                                          ALU.mult).then_inc(t1_made, 1)
                        dve.wait_ge(t1_made, i)
                        if past_first(i, 3):
                            dve.wait_ge(new_made, i - 2)
                        dve.tensor_tensor(t2[other][:, :, :], t1[other][:, :, :], n_ps[:, other, :, 0:D],
                                          ALU.add).then_inc(t2_made, 1)
                    if runs(i, 2):
                        xi = x[(u - 2) % U]
                        dve.wait_ge(new_made, i - 1)
                        dve.tensor_tensor(diff[par][:, :, :], xi[:, :, :], new[par][:, :, :],
                                          ALU.subtract).then_inc(diff_made, 1)
                        dve.tensor_tensor(kept[par][:, :, :], xi[:, :, :], new[par][:, :, :],
                                          ALU.add).then_inc(kept_made, 1)
                        dve.wait_ge(diff_made, i - 1)
                        dve.tensor_tensor(diff[par][:, :, :], rz[par][:, :, D:2 * D], diff[par][:, :, :],
                                          ALU.mult).then_inc(zd_made, 1)
                        dve.wait_ge(zd_made, i - 1)
                        dve.tensor_tensor(acc[:, bass.ds((i - 2) * 2, 2), 0:D], kept[par][:, :, :],
                                          diff[par][:, :, :], ALU.add).then_inc(y_made, 1)
                        dve.wait_ge(y_made, i - 1)
                        dve.sem_inc(dve_go, 1)
                        for t in range(2):
                            last = dve.bn_stats(stats[:, par, t, :], acc[:, bass.ds((i - 2) * 2 + t, 1), 0:D])
                        last.then_inc(stats_made, 1)
                        dve.wait_ge(stats_made, i - 1)
                        dve.sem_inc(dve_go, 1)
                        for t in range(2):
                            last = dve.bn_aggr(mv2[:, par, t, :], stats[:, par, t, :])
                        last.then_inc(aggr_made, 1)
                        dve.wait_ge(aggr_made, i - 1)
                        dve.tensor_copy(mv[:, bass.ds((i - 2) * 2, 2), :], mv2[:, par]).then_inc(var_made, 1)
                run_pairs(dve, steps, 2, U)
                dve.wait_ge(std_made, 1)
                dve.reciprocal(rstd[:, :], std[:, :]).then_inc(rstd_made, 1)
                dve.wait_ge(rstd_made, 1)
                dve.wait_ge(var_made, PAIRS)
                with dve.Fori(0, STORES) as c:
                    for t in range(CHUNK):
                        place = acc[:, bass.ds(c * CHUNK + t, 1), 0:D]
                        last = dve.tensor_scalar(place, place, mv[:, bass.ds(c * CHUNK + t, 1), 0:1],
                                                 rstd[:, bass.ds(c * CHUNK + t, 1)], ALU.subtract, ALU.mult)
                    last.then_inc(o_made, 1)


_INS = ['x', 'src', 'dst', 'edge_attr_64', 'L0_gnn_W1', 'L0_gnn_b1', 'L0_gnn_W2', 'L0_gnn_b2', 'L0_gnn_Wl',
        'L0_gnn_bl', 'L1_gnn_W1', 'L1_gnn_b1', 'L1_gnn_ln_g', 'L1_gnn_ln_b', 'L1_gnn_W2', 'L1_gnn_b2',
        'L1_gnn_gate_w', 'L1_gnn_gate_b', 'L1_gnn_W_ih', 'L1_gnn_b_ih', 'L1_gnn_W_hh', 'L1_gnn_b_hh']


def program(nc, ins, out):
    with ExitStack() as ctx:
        s = Shared()
        sb = lambda name, shape, dt: ctx.enter_context(nc.sbuf_tensor(name, shape, dt))
        sem = lambda name: ctx.enter_context(nc.semaphore(name))
        s.lane_b = sb("lane_b", [P, P], BF16)
        s.ident_b, s.ident_f = sb("ident_b", [P, P], BF16), sb("ident_f", [P, P], F32)
        s.ones_f = sb("ones_f", [1, P], F32)
        s.tile_of = [nc.dram_tensor(f"tile_of{l}", (1, STEPS), I16).ap() for l in range(2)]
        s.edge_of = nc.dram_tensor("edge_of", (1, STEPS), I16).ap()
        s.gather_of = [nc.dram_tensor(f"gather_of{l}", (P, STEPS), I32).ap() for l in range(2)]
        s.place_of = [nc.dram_tensor(f"place_of{l}", (P, STEPS), BF16).ap() for l in range(2)]
        s.const_i, s.const_f = sem("const_i"), sem("const_f")
        s.keys0 = nc.dram_tensor("keys0", (KEYROWS, P), I32).ap()
        s.keys1 = nc.dram_tensor("keys1", (STEPS, P), I32).ap()
        s.bx = nc.dram_tensor("bx", (N, 2 * D), F32).ap()
        s.x1 = nc.dram_tensor("x1", (N, D), F32).ap()
        s.c = nc.dram_tensor("c", (N, D), F32).ap()
        s.split = sb("split", [P, TILES, 3, D], BF16)
        s.w1cd, s.b1cd, s.w1e = sb("w1cd", [P, 2 * D], F32), sb("b1cd", [1, 2 * D], F32), sb("w1e", [DE, D], F32)
        s.wfold, s.whh, s.aug_w = (nc.dram_tensor(n, (r, c * D), F32).ap()
                                   for n, r, c in (("wfold", P, 3), ("whhT", P, 3), ("aug_w", 2, 4)))
        with ExitStack() as early:
            brief = lambda name, shape, dt: early.enter_context(nc.sbuf_tensor(name, shape, dt))
            s.lane_i, s.part_i = brief("lane_i", [P, P], I32), brief("part_i", [P, P], I32)
            s.lane_f, s.part_f = brief("lane_f", [P, P], F32), brief("part_f", [P, P], F32)
            s.ones_b = brief("ones_b", [P, P], BF16)
            s.chunk_i, s.chunk_f = brief("chunk_i", [P, BLOCKS], I32), brief("chunk_f", [P, BLOCKS], F32)
            s.bit, s.sign, s.flip = brief("bit", [P, 8], I32), brief("sign", [P, 9], F32), brief("flip", [P, 8], F32)
            s.step_i = early.enter_context(nc.sbuf_tensor("step_i", [P, STEPS], I32))
            s.step_f = early.enter_context(nc.sbuf_tensor("step_f", [P, STEPS], F32))
            constants_stage(nc, s, ins)
            weights_stage(nc, s, ins)
            prepare_stage(nc, s, ins)
            schedule_stage(nc, s, 0)
            schedule_stage(nc, s, 1)
        with ExitStack() as late:
            s.acc = late.enter_context(nc.sbuf_tensor("acc", [P, TILES, D + 2], F32))
            edge_stage0(nc, s, ins)
            node_stage0(nc, s, ins)
            edge_stage1(nc, s, ins)
            node_stage1(nc, s, ins, out)


def kernel(**inputs):
    import numpy as _np
    import concourse.bacc as _bacc
    from concourse import mybir as _mybir
    from concourse.bass_utils import run_bass_kernel_spmd as _run

    nc = _bacc.Bacc("TRN2", target_bir_lowering=False, num_devices=1)
    arrays, args = {}, {}
    for name in _INS:
        a = _np.ascontiguousarray(inputs[name])
        arrays[f"in_{name}"] = a
        args[name] = nc.dram_tensor(f"in_{name}", a.shape, _mybir.dt.from_np(a.dtype), kind="ExternalInput").ap()
    out = nc.dram_tensor("out_0", (N, D), _mybir.dt.float32, kind="ExternalOutput").ap()
    program(nc, args, out)
    r = _run(nc, [arrays], core_ids=[0])
    return r.results[0]["out_0"]
```

```python
from contextlib import ExitStack, contextmanager

import concourse.bass as bass
from concourse import mybir
from concourse.alu_op_type import AluOpType as ALU

ACT = mybir.ActivationFunctionType
F32 = mybir.dt.float32
BF16 = mybir.dt.bfloat16
I32 = mybir.dt.int32
I16 = mybir.dt.int16

P = 128
N = 12500
E = 200000
D = 128
DE = 64
TILES = -(-N // P)
LASTROWS = N - (TILES - 1) * P
CHUNKS = -(-E // P)
BLOCKS = -(-(CHUNKS + TILES - 1) // P)
STEPS = BLOCKS * P
G = 8
R = 4
GROUPS = STEPS // G
BODIES = GROUPS // R
KEYROWS = 2048
ROW = KEYROWS * P // P
EP = 125
EC = E // EP
BASE = 1 << 28
LOW = (1 << 14) - 1
PAD = BASE | (LOW << 14)
assert N <= LOW and EP * EC == E and BODIES * R * G == STEPS and E % P == 64


def load_values(nc, engine, ap, most):
    _, values = nc.values_load_multi_w_load_instructions(
        ap, engines=(engine,), min_val=0, max_val=most,
        skip_runtime_bounds_check_because="the schedule bounds them")
    return values


@contextmanager
def part_semaphores(nc):
    held = []

    def sem(name):
        held.append(nc.alloc_semaphore(name))
        return held[-1]
    yield sem
    nc.all_engine_barrier()
    nc.clear_and_free_semaphores(held)
    nc.all_engine_barrier()


class Shared:
    pass


def constants_stage(nc, s, ins):
    with nc.Block() as block:
        @block.gpsimd
        def _(pool):
            nc.gpsimd.iota(s.lane_i[:, :], [[1, P]], base=0, channel_multiplier=0).then_inc(s.const_i, 1)
            nc.gpsimd.iota(s.part_i[:, :], [[0, P]], base=0, channel_multiplier=1).then_inc(s.const_i, 1)
            nc.gpsimd.iota(s.step_i[:, :], [[1, STEPS]], base=0, channel_multiplier=0).then_inc(s.const_i, 1)
            nc.gpsimd.iota(s.chunk_i[:, :], [[1, BLOCKS]], base=0,
                           channel_multiplier=BLOCKS).then_inc(s.const_i, 1)

        @block.vector
        def _(dve):
            dve.memset(s.ones_b[:, :], 1.0)
            dve.memset(s.ones_f[:, :], 1.0)
            dve.memset(s.ones_r[:, :], 1.0)
            dve.wait_ge(s.const_i, 4)
            dve.tensor_copy(s.lane_b[:, :], s.lane_i[:, :])
            dve.tensor_copy(s.step_f[:, :], s.step_i[:, :])
            dve.tensor_copy(s.chunk_f[:, :], s.chunk_i[:, :])
            dve.tensor_copy(s.part_f[:, :], s.part_i[:, :])
            dve.tensor_copy(s.lane_f[:, :], s.lane_i[:, :]).then_inc(s.const_f, 1)
            dve.wait_ge(s.const_f, 1)
            dve.tensor_tensor(s.ident_b[:, :], s.lane_f[:, :], s.part_f[:, :], ALU.is_equal)
            dve.tensor_tensor(s.ident_f[:, :], s.lane_f[:, :], s.part_f[:, :], ALU.is_equal)
            for j in range(7):
                dve.tensor_scalar(s.bit[:, j:j + 1], s.part_i[:, 0:1], j, 1,
                                  ALU.logical_shift_right, ALU.bitwise_and).then_inc(s.const_f, 1)
            dve.wait_ge(s.const_f, 8)
            dve.tensor_scalar(s.sign[:, 1:8], s.bit[:, 0:7], -2.0, 1.0, ALU.mult, ALU.add)
            dve.memset(s.sign[:, 0:1], 1.0)
            dve.memset(s.sign[:, 8:9], 1.0).then_inc(s.const_f, 1)
            dve.wait_ge(s.const_f, 9)
            dve.tensor_tensor(s.flip[:, 0:8], s.sign[:, 0:8], s.sign[:, 1:9], ALU.mult)


def sort_plan():
    plan = []
    k = 2
    while k <= ROW * P:
        if k >= ROW:
            plan.append(("flip", (k // ROW).bit_length() - 1))
        if k > ROW:
            plan.append(("turn",))
            d = k // 2
            while d >= ROW:
                plan.append(("cross", d // ROW))
                d //= 2
            plan.append(("turn",))
        d = min(k // 2, ROW // 2)
        while d >= 1:
            plan.append(("row", k, d))
            d //= 2
        k *= 2
    counts, total = [], 2
    for e in plan:
        total += {"flip": 1, "turn": 0, "cross": 2, "row": 2 if e[0] != "row" or e[1] >= ROW else 4}[e[0]]
        counts.append(total)
    return plan, counts, [(i + 1) % 2 for i in range(len(plan))]


def sort_on_vector(dve, keys, flip, sort_dve, sort_evac):
    plan, counts, _ = sort_plan()
    at, done, turns = 0, 2, 0

    def exchange(lo, hi, a, b):
        dve.tensor_tensor(lo, a, b, ALU.min).then_inc(sort_dve, 1)
        dve.tensor_tensor(hi, a, b, ALU.max).then_inc(sort_dve, 1)

    for i, e in enumerate(plan):
        a, b = keys[at], keys[1 - at]
        at = 1 - at
        if e[0] == "turn":
            turns += 1
            continue
        dve.wait_ge(sort_dve, done)
        if turns:
            dve.wait_ge(sort_evac, 4 * turns)
        if e[0] == "flip":
            dve.tensor_scalar(b[:, :], a[:, :], flip[:, e[1]:e[1] + 1], None, ALU.mult).then_inc(sort_dve, 1)
        elif e[0] == "cross":
            x, y = (v[:, :].rearrange("c (b r two d) -> c b r two d", two=2, d=e[1], b=16) for v in (a, b))
            exchange(y[:, :, :, 0, :], y[:, :, :, 1, :], x[:, :, :, 0, :], x[:, :, :, 1, :])
        elif e[1] >= ROW:
            x, y = (v[:, :].rearrange("p (r two d) -> p r two d", two=2, d=e[2]) for v in (a, b))
            exchange(y[:, :, 0, :], y[:, :, 1, :], x[:, :, 0, :], x[:, :, 1, :])
        else:
            x, y = (v[:, :].rearrange("p (m s r two d) -> p m s r two d", s=2, two=2, d=e[2],
                                      r=e[1] // (2 * e[2])) for v in (a, b))
            exchange(y[:, :, 0, :, 0, :], y[:, :, 0, :, 1, :], x[:, :, 0, :, 0, :], x[:, :, 0, :, 1, :])
            exchange(y[:, :, 1, :, 1, :], y[:, :, 1, :, 0, :], x[:, :, 1, :, 0, :], x[:, :, 1, :, 1, :])
        done = counts[i]


def sort_on_tensor(nc, pe, keys, turn, ident, sort_dve, sort_turn, sort_evac):
    plan, counts, left_in = sort_plan()
    turns = 0
    for i, e in enumerate(plan):
        if e[0] == "turn":
            pe.wait_ge(sort_dve, counts[i])
            source = keys[1 - left_in[i]]
            for q in range(4):
                if turns >= 1:
                    pe.wait_ge(sort_evac, 4 * (turns - 1) + q + 1)
                for b in range(4 * q, 4 * q + 4):
                    last = nc.tensor.transpose(turn[:, b, :], source[:, b * P:(b + 1) * P], ident[:, :])
                last.then_inc(sort_turn, 1)
            turns += 1


def sort_on_scalar(nc, act, keys, turn, sort_turn, sort_evac):
    plan, _, left_in = sort_plan()
    turns = 0
    for i, e in enumerate(plan):
        if e[0] == "turn":
            turns += 1
            for q in range(4):
                act.wait_ge(sort_turn, 4 * (turns - 1) + q + 1)
                nc.scalar.copy(keys[left_in[i]][:, q * 512:(q + 1) * 512],
                               turn[:, 4 * q:4 * q + 4, :]).then_inc(sort_evac, 1)


def prepare_stage(nc, s, ins):
    with ExitStack() as ctx:
        sb = lambda name, shape, dt: ctx.enter_context(nc.sbuf_tensor(name, shape, dt))
        sem = s.sem
        keys = [sb("keys_even", [P, ROW], F32), sb("keys_odd", [P, ROW], F32)]
        src_i = sb("src_i", [P, EC], I32)
        dst_i = sb("dst_i", [P, EC], I32)
        dkey = sb("dkey", [P, EC], I32)
        dst_next = sb("dst_next", [P, EC], I32)
        padkey = sb("padkey", [P, P], I32)
        xs = sb("xs", [P, 4, 2, D], F32)
        w0 = sb("w0", [P, 2 * D], F32)
        b0 = sb("b0", [1, D], F32)
        xT = sb("xT", [P, 2, 2 * P], F32)
        ab = sb("ab", [P, 4, 2, 2 * D], F32)
        rest = sb("rest", [P, 2, 2, D], F32)
        turn = ctx.enter_context(nc.psum_tensor("turn", [P, 16, P], F32))
        xtp = ctx.enter_context(nc.psum_tensor("xtp", [P, 2, 4, P], F32))
        abp = ctx.enter_context(nc.psum_tensor("abp", [P, 2, 2, 2 * D], F32))
        edges_in, w_in, x_pad = sem("edges_in"), sem("w_in"), sem("x_pad")
        x_in = [sem(f"x_in{i}") for i in range(4)]
        sort_dve, sort_turn, sort_evac = sem("sort_dve"), sem("sort_turn"), sem("sort_evac")
        dkey_made, keys_out = sem("dkey_made"), sem("keys_out")
        next_clear, next_in = sem("next_clear"), sem("next_in")
        xT_made, xT_evac, ab_made, ab_evac = sem("xT_made"), sem("xT_evac"), sem("ab_made"), sem("ab_evac")
        split_done = sem("split_done")
        b_out = [sem(f"b_out{i}") for i in range(4)]
        x_copied = sem("x_copied")
        NG = TILES // 2

        with nc.Block() as block:
            @block.sync
            def _(sp):
                sp.dma_start(src_i[0:EP, :], ins["src"].rearrange("(p c) -> p c", c=EC)).then_inc(edges_in, 16)
                sp.dma_start(dst_i[0:EP, :], ins["dst"].rearrange("(p c) -> p c", c=EC)).then_inc(edges_in, 16)
                sp.wait_ge(next_clear, 1)
                sp.dma_start(dst_next[0:EP - 1, :],
                             ins["dst"][1:1 + (EP - 1) * EC].rearrange("(p c) -> p c", c=EC)).then_inc(next_in, 16)
                sp.dma_start(dst_next[EP - 1:EP, 0:EC - 1],
                             ins["dst"][1 + (EP - 1) * EC:E].rearrange("(a c) -> a c", a=1)).then_inc(next_in, 16)
                sp.dma_start(w0[:, 0:D], ins["L0_gnn_W1"][0:D, :]).then_inc(w_in, 16)
                sp.dma_start(w0[:, D:2 * D], ins["L0_gnn_W1"][D:2 * D, :]).then_inc(w_in, 16)
                sp.dma_start(b0[:, :], ins["L0_gnn_b1"].rearrange("(a d) -> a d", a=1)).then_inc(w_in, 16)
                def load_x(i):
                    if i >= 4:
                        sp.wait_ge(xT_made, i - 3)
                    full = 2 if i < NG - 1 else 1
                    xt = ins["x"][2 * i * P:(2 * i + full) * P, :].rearrange("(t p) d -> p t d", p=P)
                    sp.dma_start(xs[:, i % 4, 0:full, :], xt).then_inc(x_in[i % 4], 16)
                    if full == 1:
                        sp.wait_ge(x_pad, 1)
                        sp.dma_start(xs[0:LASTROWS, i % 4, 1, :],
                                     ins["x"][(TILES - 1) * P:N, :]).then_inc(x_in[i % 4], 16)
                for i in range(4):
                    load_x(i)
                sp.dma_start(s.bx[0:N, D:2 * D], ins["x"][:, :]).then_inc(x_copied, 16)
                sp.wait_ge(dkey_made, 2)
                flat = s.keys1.rearrange("r e -> (r e)")
                whole = (E // P) * P
                cut = whole - (EP - 1) * EC
                sp.dma_start(flat[0:(EP - 1) * EC].rearrange("(p c) -> p c", c=EC),
                             dkey[0:EP - 1, :]).then_inc(keys_out, 16)
                sp.dma_start(flat[(EP - 1) * EC:whole].rearrange("(a c) -> a c", a=1),
                             dkey[EP - 1:EP, 0:cut]).then_inc(keys_out, 16)
                sp.dma_start(flat[whole:whole + 64].rearrange("(a c) -> a c", a=1),
                             padkey[0:1, 0:64]).then_inc(keys_out, 16)
                sp.dma_start(flat[whole + 64:whole + P].rearrange("(a c) -> a c", a=1),
                             dkey[EP - 1:EP, cut:EC]).then_inc(keys_out, 16)
                sp.dma_start(s.keys1[CHUNKS:STEPS, :], padkey[0:STEPS - CHUNKS, :]).then_inc(keys_out, 16)
                for i in range(NG):
                    if i + 4 < NG:
                        load_x(i + 4)
                    sp.wait_ge(ab_evac, i + 1)
                    full = 2 if i < NG - 1 else 1
                    out = s.bx[2 * i * P:(2 * i + full) * P, 0:D].rearrange("(t p) d -> p t d", p=P)
                    sp.dma_start(out, ab[:, i % 4, 0:full, D:2 * D]).then_inc(b_out[i % 4], 16)
                    if full == 1:
                        sp.dma_start(s.bx[(TILES - 1) * P:N, 0:D],
                                     ab[0:LASTROWS, i % 4, 1, D:2 * D]).then_inc(b_out[i % 4], 16)
                for i in range(4):
                    sp.wait_ge(b_out[i], 16 * (len(range(i, NG, 4)) + (i == (NG - 1) % 4)))
                _, counts, left_in = sort_plan()
                sp.wait_ge(sort_dve, counts[-1])
                sp.dma_start(s.keys0.rearrange("(p c) e -> p (c e)", p=P),
                             keys[left_in[-1]].bitcast(I32)[:, :]).then_inc(keys_out, 16)
                sp.wait_ge(x_copied, 16)
                sp.wait_ge(keys_out, 16 * 6)

            @block.gpsimd
            def _(pool):
                for i in range(NG):
                    tab = s.split[:, 2 * i:2 * i + 2, :, :]
                    if i == NG - 4:
                        pool.wait_ge(xT_made, NG - 4)
                        nc.gpsimd.memset(xs[:, (NG - 1) % 4, 1, :], 0.0).then_inc(x_pad, 1)
                    pool.wait_ge(ab_evac, i + 1)
                    if i >= 2:
                        pool.wait_ge(split_done, 3 * (i - 1))
                    nc.gpsimd.tensor_tensor(rest[:, i % 2], ab[:, i % 4, :, 0:D], tab[:, :, 0, :],
                                            ALU.subtract).then_inc(split_done, 1)
                    pool.wait_ge(split_done, 3 * i + 1)
                    nc.gpsimd.tensor_copy(tab[:, :, 1, :], rest[:, i % 2]).then_inc(split_done, 1)
                    pool.wait_ge(split_done, 3 * i + 2)
                    nc.gpsimd.tensor_tensor(tab[:, :, 2, :], rest[:, i % 2], tab[:, :, 1, :],
                                            ALU.subtract).then_inc(split_done, 1)

            @block.scalar
            def _(act):
                for i in range(NG + 1):
                    if i < NG:
                        act.wait_ge(xT_made, i + 1)
                        if i >= 2:
                            act.wait_ge(ab_made, i - 1)
                        nc.scalar.copy(xT[:, i % 2, :], xtp[:, i % 2, 0:2]).then_inc(xT_evac, 1)
                    if i >= 1:
                        j = i - 1
                        act.wait_ge(ab_made, j + 1)
                        if j >= 4:
                            act.wait_ge(b_out[j % 4], 16 * (j // 4))
                            act.wait_ge(split_done, 3 * (j - 3))
                        nc.scalar.copy(s.split[:, 2 * j:2 * j + 2, 0, :], abp[:, j % 2, :, 0:D])
                        nc.scalar.copy(ab[:, j % 4], abp[:, j % 2]).then_inc(ab_evac, 1)
                sort_on_scalar(nc, act, keys, turn, sort_turn, sort_evac)

            @block.tensor
            def _(pe):
                pe.wait_ge(w_in, 48)
                for i in range(NG + 1):
                    if i < NG:
                        if i >= 2:
                            pe.wait_ge(xT_evac, i - 1)
                        pe.wait_ge(x_in[i % 4], 16 * (i // 4 + 1 + (i == NG - 1)))
                        for t in range(2):
                            last = nc.tensor.transpose(xtp[:, i % 2, t, :], xs[:, i % 4, t, :], s.ident_f[:, :])
                        last.then_inc(xT_made, 1)
                    if i >= 1:
                        j = i - 1
                        pe.wait_ge(xT_evac, j + 1)
                        if j >= 2:
                            pe.wait_ge(ab_evac, j - 1)
                        for t in range(2):
                            for side in range(2):
                                half = abp[:, j % 2, t, side * D:(side + 1) * D]
                                last = nc.tensor.matmul(half, xT[:, j % 2, t * P:(t + 1) * P],
                                                        w0[:, side * D:(side + 1) * D],
                                                        start=True, stop=(side == 1))
                                if side == 0:
                                    nc.tensor.matmul(half, s.ones_f[0:1, :], b0[:, :], start=False, stop=True)
                        last.then_inc(ab_made, 1)
                sort_on_tensor(nc, pe, keys, turn, s.ident_f, sort_dve, sort_turn, sort_evac)

            @block.vector
            def _(dve):
                dve.memset(dst_next[:, :], LOW)
                dve.memset(s.falls[:, :], 0.0).then_inc(next_clear, 1)
                dve.memset(padkey[:, :], PAD)
                dve.memset(keys[0].bitcast(I32)[:, :], PAD).then_inc(sort_dve, 1)
                dve.wait_ge(edges_in, 32)
                dve.tensor_scalar(src_i[0:EP, :], src_i[0:EP, :], 0, None, ALU.bitwise_or)
                dve.tensor_scalar(dkey[0:EP, :], dst_i[0:EP, :], 14, BASE, ALU.logical_shift_left,
                                  ALU.bitwise_or).then_inc(dkey_made, 1)
                dve.wait_ge(dkey_made, 1)
                dve.tensor_tensor(dkey[0:EP, :], dkey[0:EP, :], src_i[0:EP, :],
                                  ALU.bitwise_or).then_inc(dkey_made, 1)
                dve.wait_ge(dkey_made, 2)
                dve.tensor_scalar(src_i[0:EP, :], src_i[0:EP, :], 14, BASE, ALU.logical_shift_left,
                                  ALU.bitwise_or).then_inc(dkey_made, 1)
                dve.wait_ge(dkey_made, 3)
                dve.wait_ge(sort_dve, 1)
                dve.tensor_tensor(keys[0].bitcast(I32)[0:EP, 0:EC], src_i[0:EP, :], dst_i[0:EP, :],
                                  ALU.bitwise_or).then_inc(sort_dve, 1)
                dve.wait_ge(next_in, 32)
                dve.wait_ge(next_clear, 1)
                dve.wait_ge(dkey_made, 3)
                dve.scalar_tensor_tensor(dst_next[0:EP, :], dst_next[0:EP, :], 0, dst_i[0:EP, :],
                                         ALU.add, ALU.is_lt, accum_out=s.falls[0:EP, :])
                sort_on_vector(dve, keys, s.flip, sort_dve, sort_evac)


def regroup_stage(nc, s, ins):
    with ExitStack() as ctx:
        sb = lambda name, shape, dt: ctx.enter_context(nc.sbuf_tensor(name, shape, dt))
        sem = s.sem
        keys = [sb("by_tile_even", [P, ROW], F32), sb("by_tile_odd", [P, ROW], F32)]
        src_i, dst_i, number = (sb(n, [P, EC], I32) for n in ("src_again", "dst_again", "edge_number"))
        tile = sb("edge_tile", [P, EC], I32)
        edge, key, features = sb("edge_idx", [P, 1], I32), sb("edge_key_rows", [P, 1], I32), sb("ef_rows", [P, DE], F32)
        turn = ctx.enter_context(nc.psum_tensor("turn_again", [P, 16, P], F32))
        count = ctx.enter_context(nc.psum_tensor("falls_counted", [P, 512], F32))
        counted, flag_made, edges_in = sem("falls_counted_up"), sem("flag_made"), sem("edges_again")
        numbered, keyed, key_out = sem("numbered"), sem("keyed"), sem("key_out")
        sort_dve, sort_turn, sort_evac = sem("by_tile_dve"), sem("by_tile_turn"), sem("by_tile_evac")
        order_out, edge_in, fetched, moved = sem("order_out"), sem("edge_in"), sem("fetched"), sem("moved")
        go_sp, go_pool = sem("regroup_sp_go"), sem("regroup_pool_go")
        _, counts, left_in = sort_plan()

        def unsorted(engine, kind):
            engine.wait_ge(flag_made, 1)
            return load_values(nc, kind, s.unsorted[0:1, 0:1], 1)[0]

        with nc.Block() as block:
            @block.sync
            def _(sp):
                with sp.If(unsorted(sp, mybir.EngineType.SP)):
                    sp.dma_start(src_i[0:EP, :], ins["src"].rearrange("(p c) -> p c", c=EC)).then_inc(edges_in, 16)
                    sp.dma_start(dst_i[0:EP, :], ins["dst"].rearrange("(p c) -> p c", c=EC)).then_inc(edges_in, 16)
                    sp.wait_ge(keyed, 4)
                    sp.dma_start(s.edge_key.rearrange("(p c) a -> p (c a)", c=EC), dst_i[0:EP, :]).then_inc(key_out, 16)
                    sp.wait_ge(key_out, 16)
                    sp.wait_ge(sort_dve, counts[-1] + 1)
                    sp.dma_start(s.order.rearrange("(p c) a -> p (c a)", p=P),
                                 keys[1 - left_in[-1]].bitcast(I32)[:, :]).then_inc(order_out, 16)
                    sp.wait_ge(order_out, 16)
                    flat = s.keys1.rearrange("r e -> (r e)").rearrange("(n a) -> n a", a=1)
                    with sp.Fori(0, CHUNKS - 1) as c:
                        sp.dma_start(edge[:, :], s.order[bass.ds(c * P, P), :]).then_inc(edge_in, 16)
                        sp.wait_ge(fetched, c * 32 + 32)
                        sp.sem_inc(go_sp, 1)
                        sp.dma_start(flat[bass.ds(c * P, P), :], key[:, :]).then_inc(moved, 16)
                        sp.dma_start(s.grouped_features[bass.ds(c * P, P), :], features[:, :]).then_inc(moved, 16)
                        sp.wait_ge(moved, c * 32 + 32)
                        sp.sem_inc(go_sp, 1)
                    sp.dma_start(edge[:, :], s.order[E - P:E, :]).then_inc(edge_in, 16)
                    sp.wait_ge(fetched, CHUNKS * 32)
                    sp.dma_start(flat[CHUNKS * P - 64:CHUNKS * P, :], key[64:P, :]).then_inc(moved, 16)
                    sp.dma_start(s.grouped_features[E - P:E, :], features[:, :]).then_inc(moved, 16)
                    sp.wait_ge(moved, CHUNKS * 32)

            @block.gpsimd
            def _(pool):
                with pool.If(unsorted(pool, mybir.EngineType.Pool)):
                    nc.gpsimd.iota(number[:, :], [[1, EC]], base=BASE, channel_multiplier=EC).then_inc(numbered, 1)
                    pool.wait_ge(key_out, 16)
                    with pool.Fori(0, CHUNKS) as c:
                        pool.wait_ge(edge_in, c * 16 + 16)
                        pool.sem_inc(go_pool, 1)
                        for rows, table in ((key, s.edge_key), (features, ins["edge_attr_64"])):
                            pool.indirect_dma_start(
                                out=rows[:, :], out_offset=None, in_=table[:, :],
                                in_offset=bass.IndirectOffsetOnAxis(ap=edge[:, 0:1], axis=0),
                            ).then_inc(fetched, 16)

            @block.tensor
            def _(pe):
                nc.tensor.matmul(count[0:1, 0:1], s.falls[:, :], s.sign[:, 0:1],
                                 start=True, stop=True).then_inc(counted, 1)
                with pe.If(unsorted(pe, mybir.EngineType.PE)):
                    sort_on_tensor(nc, pe, keys, turn, s.ident_f, sort_dve, sort_turn, sort_evac)

            @block.scalar
            def _(act):
                with act.If(unsorted(act, mybir.EngineType.Activation)):
                    sort_on_scalar(nc, act, keys, turn, sort_turn, sort_evac)

            @block.vector
            def _(dve):
                dve.wait_ge(counted, 1)
                dve.tensor_scalar(s.unsorted[:, :], count[0:1, 0:1], 1.0, None, ALU.min).then_inc(flag_made, 1)
                with dve.If(unsorted(dve, mybir.EngineType.DVE)):
                    dve.memset(keys[0].bitcast(I32)[:, :], BASE | ((1 << 25) - 1)).then_inc(sort_dve, 1)
                    dve.wait_ge(edges_in, 32)
                    dve.tensor_scalar(tile[0:EP, :], dst_i[0:EP, :], 7, 18, ALU.logical_shift_right,
                                      ALU.logical_shift_left).then_inc(keyed, 1)
                    dve.wait_ge(keyed, 1)
                    dve.wait_ge(numbered, 1)
                    dve.wait_ge(sort_dve, 1)
                    dve.tensor_tensor(keys[0].bitcast(I32)[0:EP, 0:EC], tile[0:EP, :], number[0:EP, :],
                                      ALU.bitwise_or).then_inc(sort_dve, 1)
                    dve.tensor_scalar(dst_i[0:EP, :], dst_i[0:EP, :], 14, BASE, ALU.logical_shift_left,
                                      ALU.bitwise_or).then_inc(keyed, 1)
                    dve.wait_ge(keyed, 2)
                    dve.tensor_tensor(dst_i[0:EP, :], dst_i[0:EP, :], src_i[0:EP, :],
                                      ALU.bitwise_or).then_inc(keyed, 2)
                    sort_on_vector(dve, keys, s.flip, sort_dve, sort_evac)
                    dve.wait_ge(sort_dve, counts[-1])
                    dve.tensor_scalar(keys[1 - left_in[-1]].bitcast(I32)[:, :],
                                      keys[left_in[-1]].bitcast(I32)[:, :], (1 << 18) - 1, None,
                                      ALU.bitwise_and).then_inc(sort_dve, 1)


def schedule_stage(nc, s, l):
    keys = (s.keys0, s.keys1)[l]
    with ExitStack() as ctx:
        sb = lambda name, shape, dt: ctx.enter_context(nc.sbuf_tensor(f"{name}_{l}", shape, dt))
        sem = lambda name: s.sem(f"{name}_{l}")
        lastkey = sb("lastkey", [P, BLOCKS], I32)
        ends_i = sb("ends_i", [P, BLOCKS], I32)
        ends = sb("ends", [P, BLOCKS], F32)
        past = sb("past", [P, BLOCKS, STEPS], BF16)
        chunk_of = sb("chunk_of", [P, BLOCKS], I32)
        rows = sb("rows", [P, BLOCKS, P], I32)
        stepkey = sb("stepkey", [P, STEPS], F32)
        side = sb("side", [P, STEPS], I32)
        trow = sb("trow", [P, STEPS], F32)
        crow = sb("crow", [1, STEPS], F32)
        tile_i, edge_i = sb("tile_i", [1, STEPS], I16), sb("edge_i", [1, STEPS], I16)
        gather_i = sb("gather_i", [P, STEPS], I32)
        place = sb("place", [P, STEPS], BF16)
        counted = ctx.enter_context(nc.psum_tensor(f"counted_{l}", [P, 4, 512], F32))
        listed = ctx.enter_context(nc.psum_tensor(f"listed_{l}", [P, 512], F32))
        turned = ctx.enter_context(nc.psum_tensor(f"keys_turned_{l}", [P, 2, 4, P], F32))
        last_in, chain, counted_up, past_made = sem("last_in"), sem("chain"), sem("counted_up"), sem("past_made")
        rows_in, turned_up, evac, chunk_made = sem("rows_in"), sem("turned_up"), sem("evac"), sem("chunk_made")
        tiles_made, made, stored = sem("tiles_made"), sem("made"), sem("stored")
        widths = [min(512, STEPS - 512 * b) for b in range(-(-STEPS // 512))]
        quads = [(b, min(b + 4, BLOCKS)) for b in range(0, BLOCKS, 4)]
        with nc.Block() as block:
            @block.sync
            def _(sp):
                view = keys[0:STEPS, :].rearrange("(p j) e -> p j e", j=BLOCKS)[:, :, P - 1:P]
                with nc.allow_non_contiguous_dma(reason="one key of each chunk"):
                    sp.dma_start(lastkey[:, :].rearrange("p (j a) -> p j a", a=1), view).then_inc(last_in, 16)
                sp.wait_ge(tiles_made, 1 + l)
                sp.dma_start(s.tile_of[l][:, :], tile_i[:, :]).then_inc(stored, 16)
                if l == 1:
                    sp.dma_start(s.edge_of[:, :], edge_i[:, :]).then_inc(stored, 16)
                sp.wait_ge(made, 2)
                sp.dma_start(s.gather_of[l][:, :], gather_i[:, :]).then_inc(stored, 16)
                sp.dma_start(s.place_of[l][:, :], place[:, :]).then_inc(stored, 16)
                sp.wait_ge(stored, 16 * (3 + l))

            @block.gpsimd
            def _(pool):
                pool.wait_ge(chunk_made, 1)
                for b in range(BLOCKS):
                    pool.indirect_dma_start(
                        out=rows[:, b, :], out_offset=None, in_=keys[:, :],
                        in_offset=bass.IndirectOffsetOnAxis(ap=chunk_of[:, b:b + 1], axis=0),
                    ).then_inc(rows_in, 16)

            @block.tensor
            def _(pe):
                pe.wait_ge(past_made, 1)
                for b in range(BLOCKS):
                    for j in range(BLOCKS):
                        last = nc.tensor.matmul(listed[:, b:b + 1], past[:, j, b * P:(b + 1) * P],
                                                s.ones_b[:, 0:1], start=(j == 0), stop=(j == BLOCKS - 1))
                last.then_inc(counted_up, 1)
                for b, w in enumerate(widths):
                    for j in range(BLOCKS):
                        last = nc.tensor.matmul(counted[:, b, 0:w], s.ones_b[:, :], past[:, j, b * 512:b * 512 + w],
                                                start=(j == 0), stop=(j == BLOCKS - 1))
                last.then_inc(counted_up, 1)
                pe.wait_ge(rows_in, 16 * BLOCKS)
                for n, (b, e) in enumerate(quads):
                    if n >= 2:
                        pe.wait_ge(evac, n - 1)
                    for k in range(b, e):
                        last = nc.tensor.transpose(turned[:, n % 2, k - b, :], rows.bitcast(F32)[:, k, :],
                                                   s.ident_f[:, :])
                    last.then_inc(turned_up, 1)

            @block.vector
            def _(dve):
                dve.wait_ge(last_in, 16)
                dve.tensor_scalar(ends_i[:, :], lastkey[:, :], 21, 127,
                                  ALU.logical_shift_right, ALU.bitwise_and).then_inc(chain, 1)
                dve.wait_ge(chain, 1)
                dve.tensor_scalar(ends[:, :], ends_i[:, :], float(TILES - 1), None, ALU.min).then_inc(chain, 1)
                dve.wait_ge(chain, 2)
                dve.tensor_tensor(ends[:, :], ends[:, :], s.chunk_f[:, :], ALU.add).then_inc(chain, 1)
                dve.wait_ge(chain, 3)
                for j in range(BLOCKS):
                    last = dve.tensor_scalar(past[:, j, :], s.step_f[:, :], ends[:, j:j + 1], None, ALU.is_gt)
                last.then_inc(past_made, 1)
                dve.wait_ge(counted_up, 1)
                dve.tensor_copy(chunk_of[:, :], listed[:, 0:BLOCKS]).then_inc(chunk_made, 1)
                dve.wait_ge(counted_up, 2)
                for b, w in enumerate(widths):
                    cut = slice(b * 512, b * 512 + w)
                    last = dve.tensor_tensor(trow[:, cut], s.step_f[:, cut], counted[:, b, 0:w], ALU.subtract)
                    if l == 1:
                        last = dve.tensor_scalar(crow[:, cut], counted[0:1, b, 0:w], 2.0, float((E - P) // 64),
                                                 ALU.mult, ALU.min)
                last.then_inc(chain, 1)
                dve.wait_ge(chain, 4)
                dve.tensor_copy(tile_i[:, :], trow[0:1, :]).then_inc(tiles_made, 1)
                if l == 1:
                    dve.tensor_copy(edge_i[:, :], crow[:, :]).then_inc(tiles_made, 1)
                for n, (b, e) in enumerate(quads):
                    dve.wait_ge(turned_up, n + 1)
                    dve.tensor_copy(stepkey[:, b * P:e * P],
                                    turned[:, n % 2].rearrange("p k e -> p (k e)")[:, 0:(e - b) * P]).then_inc(evac, 1)
                dve.wait_ge(evac, len(quads))
                dve.tensor_scalar(gather_i[:, :], stepkey.bitcast(I32)[:, :], LOW, None,
                                  ALU.bitwise_and).then_inc(made, 1)
                dve.tensor_scalar(side[:, :], stepkey.bitcast(I32)[:, :], 14, LOW,
                                  ALU.logical_shift_right, ALU.bitwise_and).then_inc(chain, 1)
                dve.wait_ge(chain, 5)
                dve.scalar_tensor_tensor(place[:, :], trow[:, :], -float(P), side[:, :],
                                         ALU.mult, ALU.add).then_inc(made, 1)


def edge_stage0(nc, s, ins):
    W = D + 1
    with ExitStack() as ctx:
        sb = lambda name, shape, dt: ctx.enter_context(nc.sbuf_tensor(name, shape, dt))
        ps = lambda name, shape, dt: ctx.enter_context(nc.psum_tensor(name, shape, dt))
        sem = s.sem
        idx = [sb(f"idx{q}", [P, G], I32) for q in range(R)]
        bx = [sb(f"bxrows{q}", [P, G, 2 * D + 1], F32) for q in range(R)]
        hot = [sb(f"hot{q}", [P, G, P], BF16) for q in range(R)]
        hotT = [sb(f"hotT{i}", [P, G, P], BF16) for i in range(2)]
        hotw = [sb(f"hotw{i}", [P, G, P], F32) for i in range(2)]
        h = sb("h", [P, 2, 4, D], F32)
        logit = sb("logit", [P, 2, G], F32)
        sig = sb("sig", [P, 2, G], F32)
        mask = sb("mask", [P, 2, G], F32)
        w2 = sb("w2", [P, D], F32)
        b2 = sb("b2", [P, 1], F32)
        tiny = sb("tiny", [P, 1], F32)
        hotT_ps = ps("hotT_ps", [P, G, P], BF16)
        pre = ps("pre", [P, 2, 4, D], F32)
        out = ps("scattered", [P, 2, 4, 256], F32)
        w_in, zeroed = sem("w2_in"), sem("zeroed")
        idx_in = [sem(f"idx_in{q}") for q in range(R)]
        rows_in = [sem(f"bx_in{q}") for q in range(R)]
        hot_made, hot_turned, hotT_made = sem("hot_made"), sem("hot_turned"), sem("hotT_made")
        pre_made, pre_used, dotted = sem("pre_made"), sem("pre_used"), sem("dotted")
        sig_made, mask_made, hotw_made = sem("sig_made"), sem("mask_made"), sem("hotw_made")
        scattered, added = sem("scattered_up"), sem("added")
        issue, act_go = sem("issue"), sem("act_go")
        tile_of, place_of = sb("tile_row", [1, STEPS], I16), sb("places", [P, STEPS], BF16)
        gather_of, acc = s.gather_of[0], s.acc
        steps_in = sem("steps_in")

        with nc.Block() as block:
            @block.sync
            def _(sp):
                sp.dma_start(tile_of[:, :], s.tile_of[0][:, :]).then_inc(steps_in, 16)
                sp.dma_start(place_of[:, :], s.place_of[0][:, :]).then_inc(steps_in, 16)
                with nc.allow_non_contiguous_dma(reason="a row for every partition"):
                    sp.dma_start(w2[:, :], ins["L0_gnn_W2"].rearrange("d a -> a d").to_broadcast([P, D])
                                 ).then_inc(w_in, 16)
                    sp.dma_start(b2[:, :], ins["L0_gnn_b2"].rearrange("(a d) -> a d", a=1).to_broadcast([P, 1])
                                 ).then_inc(w_in, 16)

                def load_idx(g, q, round_):
                    sp.dma_start(idx[q][:, :], gather_of[:, bass.ds(g * G, G)]).then_inc(idx_in[q], 16)
                for q in range(R):
                    load_idx(q, q, 0)
                with sp.Fori(1, BODIES) as o:
                    for q in range(R):
                        sp.wait_ge(rows_in[q], o * (16 * G))
                        load_idx(o * R + q, q, o)

            @block.gpsimd
            def _(pool):
                for q in range(R):
                    nc.gpsimd.memset(bx[q][:, :, 2 * D:2 * D + 1], 1.0).then_inc(zeroed, 1)

                def gather(q):
                    for k in range(G):
                        pool.indirect_dma_start(
                            out=bx[q][:, k, 0:2 * D], out_offset=None, in_=s.bx[:, :],
                            in_offset=bass.IndirectOffsetOnAxis(ap=idx[q][:, k:k + 1], axis=0),
                        ).then_inc(rows_in[q], 16)
                for q in range(R):
                    pool.wait_ge(idx_in[q], 16)
                    gather(q)
                with pool.Fori(1, BODIES) as o:
                    for q in range(R):
                        pool.wait_ge(idx_in[q], o * 16 + 16)
                        pool.wait_ge(scattered, (o - 1) * (2 * R) + 2 * q + 2)
                        pool.sem_inc(issue, 1)
                        gather(q)

            @block.tensor
            def _(pe):
                def turn(g, q, first):
                    pe.wait_ge(hot_made, g + 1)
                    if not first:
                        pe.wait_ge(hotT_made, g)
                    for k in range(G):
                        last = nc.tensor.transpose(hotT_ps[:, k, :], hot[q][:, k, :], s.ident_b[:, :])
                    last.then_inc(hot_turned, 1)

                def products(g, q, first):
                    tiles = load_values(nc, mybir.EngineType.PE, tile_of[0:1, bass.ds(g * G, G)], TILES - 1)
                    pe.wait_ge(hotT_made, g + 1)
                    for half in range(2):
                        if not first:
                            pe.wait_ge(pre_used, g * 2 + half - 1)
                        for k in range(4):
                            for part in range(3):
                                last = nc.tensor.matmul(pre[:, half, k, :], hotT[q % 2][:, 4 * half + k, :],
                                                        s.split[:, bass.ds(tiles[4 * half + k], 1), part, :],
                                                        start=(part == 0), stop=(part == 2))
                        last.then_inc(pre_made, 1)

                def scatter(g, q, first):
                    pe.wait_ge(hotw_made, g + 1)
                    for half in range(2):
                        if not first:
                            pe.wait_ge(added, g * 8 + 4 * half - 4)
                        for k in range(4):
                            last = nc.tensor.matmul(out[:, half, k, 0:W], hotw[q % 2][:, 4 * half + k, :],
                                                    bx[q][:, 4 * half + k, D:D + W], start=True, stop=True)
                        last.then_inc(scattered, 1)

                pe.wait_ge(zeroed, R)
                pe.wait_ge(steps_in, 32)
                for q in range(R):
                    if q >= 1:
                        products(q - 1, q - 1, q == 1)
                    turn(q, q, q == 0)
                    if q >= 2:
                        scatter(q - 2, q - 2, q == 2)
                with pe.Fori(1, BODIES) as o:
                    for q in range(R):
                        products(o * R + (q - 1), (q - 1) % R, False)
                        turn(o * R + q, q, False)
                        scatter(o * R + (q - 2), (q - 2) % R, False)
                products(GROUPS - 1, R - 1, False)
                scatter(GROUPS - 2, R - 2, False)
                scatter(GROUPS - 1, R - 1, False)

            @block.scalar
            def _(act):
                act.wait_ge(w_in, 32)
                act.wait_ge(zeroed, R + 1)

                def turn_evac(g, q, first):
                    act.wait_ge(hot_turned, g + 1)
                    if not first:
                        act.wait_ge(pre_made, g * 2 - 2)
                    act.sem_inc(act_go, 1)
                    nc.scalar.copy(hotT[q % 2][:, :, :], hotT_ps[:, :, :]).then_inc(hotT_made, 1)

                def weigh(g, q, first):
                    act.wait_ge(dotted, g + 1)
                    act.sem_inc(act_go, 1)
                    nc.scalar.activation(sig[:, q % 2, :], logit[:, q % 2, :], ACT.Sigmoid,
                                         bias=b2[:, 0:1]).then_inc(sig_made, 1)
                    act.wait_ge(sig_made, g + 1)
                    act.sem_inc(act_go, 1)
                    nc.scalar.activation(mask[:, q % 2, :], sig[:, q % 2, :], ACT.Identity,
                                         bias=tiny[:, 0:1]).then_inc(mask_made, 1)
                    act.wait_ge(mask_made, g + 1)
                    if not first:
                        act.wait_ge(scattered, g * 2 - 2)
                    act.sem_inc(act_go, 1)
                    for k in range(G):
                        last = nc.scalar.activation(hotw[q % 2][:, k, :], hot[q][:, k, :], ACT.Copy,
                                                    scale=mask[:, q % 2, k:k + 1])
                    last.then_inc(hotw_made, 1)

                for q in range(R):
                    turn_evac(q, q, q < 2)
                    if q >= 1:
                        weigh(q - 1, q - 1, q < 3)
                with act.Fori(1, BODIES) as o:
                    for q in range(R):
                        turn_evac(o * R + q, q, False)
                        weigh(o * R + (q - 1), (q - 1) % R, False)
                weigh(GROUPS - 1, R - 1, False)

            @block.vector
            def _(dve):
                dve.memset(tiny[:, :], 1e-30)
                dve.memset(acc[:, :, 0:W], 0.0).then_inc(zeroed, 1)
                dve.wait_ge(w_in, 32)
                dve.wait_ge(steps_in, 32)
                dve.wait_ge(zeroed, R + 1)

                def start(g, q, older, tiles):
                    if g is not None and used(g, R):
                        dve.wait_ge(hotw_made, g - (R - 1))
                    for k in range(G):
                        if g is not None:
                            last = dve.tensor_scalar(hot[q][:, k, :], s.lane_b[:, :],
                                                     place_of[:, bass.ds(g * G + k, 1)], None, ALU.is_equal)
                            if k == G - 1:
                                last.then_inc(hot_made, 1)
                        if older is not None:
                            if k % 4 == 0:
                                dve.wait_ge(scattered, older * 2 + k // 4 + 1)
                            if used(older, 1) or k:
                                dve.wait_ge(added, older * 8 + k)
                            slot = acc[:, bass.ds(tiles[k], 1), 0:W]
                            dve.tensor_tensor(slot, slot, out[:, k // 4, k % 4:k % 4 + 1, 0:W],
                                              ALU.add).then_inc(added, 1)

                def finish(g, q, round_):
                    dve.wait_ge(rows_in[q], (round_ + 1) * (16 * G))
                    if used(g, 1):
                        dve.wait_ge(dotted, g)
                    for half in range(2):
                        dve.wait_ge(pre_made, g * 2 + half + 1)
                        dve.tensor_tensor(h[:, half], pre[:, half], bx[q][:, 4 * half:4 * half + 4, 0:D],
                                          ALU.add).then_inc(pre_used, 1)
                    if used(g, 2):
                        dve.wait_ge(sig_made, g - 1)
                    for half in range(2):
                        dve.wait_ge(pre_used, g * 2 + half + 1)
                        for k in range(4 * half, 4 * half + 4):
                            last = dve.scalar_tensor_tensor(h[:, half, k % 4, :], h[:, half, k % 4, :], 0.0, w2[:, :],
                                                            ALU.max, ALU.mult, accum_out=logit[:, q % 2, k:k + 1])
                    last.then_inc(dotted, 1)

                def tiles_for(g):
                    return load_values(nc, mybir.EngineType.DVE, tile_of[0:1, bass.ds(g * G, G)], TILES - 1)

                for q in range(R):
                    start(q, q, q - 3 if q >= 3 else None, tiles_for(0) if q >= 3 else None)
                    if q >= 1:
                        finish(q - 1, q - 1, 0)
                with dve.Fori(1, BODIES) as o:
                    for q in range(R):
                        start(o * R + q, q, o * R + (q - 3), tiles_for(o * R + (q - 3)))
                        finish(o * R + (q - 1), (q - 1) % R, o - 1 if q == 0 else o)
                start(None, None, GROUPS - 3, tiles_for(GROUPS - 3))
                finish(GROUPS - 1, R - 1, BODIES - 1)
                start(None, None, GROUPS - 2, tiles_for(GROUPS - 2))
                start(None, None, GROUPS - 1, tiles_for(GROUPS - 1))


def weights_stage(nc, s, ins):
    with ExitStack() as ctx:
        sb = lambda name, shape, dt: ctx.enter_context(nc.sbuf_tensor(name, shape, dt))
        ps = lambda name, shape: ctx.enter_context(nc.psum_tensor(name, shape, F32))
        sem = s.sem
        raw = sb("w1_raw", [P, 4, D], F32)
        total = sb("w1_total", [P, 4], F32)
        mean = sb("w1_mean", [P, 4], F32)
        w2 = sb("w2_raw", [P, D], F32)
        wih, whh = sb("wih_raw", [P, 3, D], F32), sb("whh_raw", [P, 3, D], F32)
        w2T, wihT = sb("w2T", [P, D], F32), sb("wihT", [P, 3 * D], F32)
        ln_b, b2 = sb("ln_b_col", [P, 1], F32), sb("b2_col", [P, 1], F32)
        u = sb("u", [P, 1], F32)
        fold, whhT = sb("fold", [P, 3 * D], F32), sb("whhT_sb", [P, 3 * D], F32)
        bi, bh = sb("b_ih_row", [1, 3 * D], F32), sb("b_hh_row", [1, 3 * D], F32)
        wT_ps, hT_ps, m_ps = ps("wT_ps", [P, 4, D]), ps("hT_ps", [P, 4, D]), ps("m_ps", [P, 4, D])
        u_ps, v_ps = ps("u_ps", [P, 512]), ps("v_ps", [P, 512])
        w_in, zeroed, chain = sem("weights_in"), sem("w_zeroed"), sem("w_chain")
        turned, copied, folded, rows_done = sem("w_turned"), sem("w_copied"), sem("w_folded"), sem("rows_done")
        rows_out, split_up = sem("rows_out"), sem("rows_split")
        long = sb("long_rows", [1, 10 * D], F32)
        parts, rest = sb("row_parts", [1, 3, 10 * D], BF16), sb("row_rest", [1, 10 * D], F32)
        row = lambda name: ins[name].rearrange("(a d) -> a d", a=1)
        with nc.Block() as block:
            @block.sync
            def _(sp):
                w1 = ins["L1_gnn_W1"]
                sp.wait_ge(zeroed, 1)
                sp.dma_start(raw[:, 0:2, :], w1[0:2 * D, :].rearrange("(j p) d -> p j d", p=P)).then_inc(w_in, 16)
                sp.dma_start(raw[0:DE, 2, :], w1[2 * D:2 * D + DE, :]).then_inc(w_in, 16)
                sp.dma_start(raw[0:1, 3, :], row("L1_gnn_b1")).then_inc(w_in, 16)
                sp.dma_start(w2[:, :], ins["L1_gnn_W2"]).then_inc(w_in, 16)
                sp.dma_start(wih[:, :, :], ins["L1_gnn_W_ih"].rearrange("(j p) d -> p j d", p=P)).then_inc(w_in, 16)
                sp.dma_start(whh[:, :, :], ins["L1_gnn_W_hh"].rearrange("(j p) d -> p j d", p=P)).then_inc(w_in, 16)
                sp.dma_start(ln_b[:, :], ins["L1_gnn_ln_b"].rearrange("(d a) -> d a", a=1)).then_inc(w_in, 16)
                sp.dma_start(b2[:, :], ins["L1_gnn_b2"].rearrange("(d a) -> d a", a=1)).then_inc(w_in, 16)
                sp.dma_start(bi[:, :], row("L1_gnn_b_ih")).then_inc(w_in, 16)
                sp.dma_start(bh[:, :], row("L1_gnn_b_hh")).then_inc(w_in, 16)
                sp.dma_start(long[:, 8 * D:9 * D], row("L0_gnn_bl")).then_inc(w_in, 16)
                sp.wait_ge(rows_done, 3)
                sp.wait_ge(split_up, 4)
                for part in range(3):
                    sp.dma_start(s.row_parts[part:part + 1, :], parts[:, part, :]).then_inc(rows_out, 16)
                sp.dma_start(s.wfold[:, :], fold[:, :]).then_inc(rows_out, 16)
                sp.dma_start(s.whh[:, :], whhT[:, :]).then_inc(rows_out, 16)
                sp.wait_ge(rows_out, 16 * 5)

            @block.tensor
            def _(pe):
                pe.wait_ge(w_in, 16 * 11)
                nc.tensor.transpose(wT_ps[:, 3, :], w2[:, :], s.ident_f[:, :])
                for j in range(3):
                    nc.tensor.transpose(wT_ps[:, j, :], wih[:, j, :], s.ident_f[:, :])
                for j in range(3):
                    last = nc.tensor.transpose(hT_ps[:, j, :], whh[:, j, :], s.ident_f[:, :])
                last.then_inc(turned, 1)
                nc.tensor.matmul(u_ps[:, 0:1], w2[:, :], ln_b[:, :], start=True, stop=True).then_inc(turned, 1)
                pe.wait_ge(copied, 4)
                nc.tensor.matmul(m_ps[:, 0:3, :], w2T[:, :], wihT[:, :], start=True, stop=True)
                nc.tensor.matmul(v_ps[0:1, 0:3 * D], u[:, :], wihT[:, :], start=True, stop=True).then_inc(folded, 1)

            @block.vector
            def _(dve):
                dve.memset(raw[:, 2:4, :], 0.0).then_inc(zeroed, 1)
                dve.memset(long[:, 3 * D:4 * D], 0.0)
                dve.wait_ge(w_in, 16 * 11)
                dve.reduce_sum(total[:, :], raw[:, :, :], axis=mybir.AxisListType.X).then_inc(chain, 1)
                dve.wait_ge(chain, 1)
                dve.tensor_scalar(mean[:, :], total[:, :], 1.0 / D, None, ALU.mult).then_inc(chain, 1)
                dve.wait_ge(chain, 2)
                for j in range(2):
                    dve.tensor_scalar(s.w1cd[:, j * D:(j + 1) * D], raw[:, j, :], mean[:, j:j + 1], None, ALU.subtract)
                dve.tensor_scalar(s.w1e[:, :], raw[0:DE, 2, :], mean[0:DE, 2:3], None, ALU.subtract)
                dve.tensor_scalar(long[:, 9 * D:10 * D], raw[0:1, 3, :], mean[0:1, 3:4], None, ALU.subtract)
                dve.wait_ge(turned, 1)
                dve.tensor_copy(w2T[:, :], wT_ps[:, 3, :]).then_inc(copied, 1)
                dve.tensor_copy(wihT[:, :], wT_ps[:, 0:3, :].rearrange("p j d -> p (j d)")).then_inc(copied, 1)
                dve.tensor_copy(whhT[:, :], hT_ps[:, 0:3, :].rearrange("p j d -> p (j d)")).then_inc(copied, 1)
                dve.wait_ge(turned, 2)
                dve.tensor_tensor(u[:, :], u_ps[:, 0:1], b2[:, :], ALU.add).then_inc(copied, 1)
                dve.tensor_tensor(long[:, 4 * D:6 * D], bi[:, 0:2 * D], bh[:, 0:2 * D], ALU.add)
                dve.tensor_copy(long[:, 6 * D:7 * D], bi[:, 2 * D:3 * D])
                dve.tensor_copy(long[:, 7 * D:8 * D], bh[:, 2 * D:3 * D]).then_inc(rows_done, 1)
                dve.wait_ge(folded, 1)
                dve.tensor_copy(fold[:, :], m_ps[:, 0:3, :].rearrange("p j d -> p (j d)")).then_inc(rows_done, 1)
                dve.tensor_copy(long[:, 0:3 * D], v_ps[0:1, 0:3 * D]).then_inc(rows_done, 1)
                dve.wait_ge(rows_done, 3)
                dve.tensor_copy(parts[:, 0, :], long[:, :]).then_inc(split_up, 1)
                dve.wait_ge(split_up, 1)
                dve.tensor_tensor(rest[:, :], long[:, :], parts[:, 0, :], ALU.subtract).then_inc(split_up, 1)
                dve.wait_ge(split_up, 2)
                dve.tensor_copy(parts[:, 1, :], rest[:, :]).then_inc(split_up, 1)
                dve.wait_ge(split_up, 3)
                dve.tensor_tensor(parts[:, 2, :], rest[:, :], parts[:, 1, :], ALU.subtract).then_inc(split_up, 1)


PAIRS = TILES // 2
assert TILES % 2 == 0 and PAIRS % 2 == 1


def run_pairs(engine, steps, lead, first=4, unroll=4):
    whole = (PAIRS - 1 - first) // unroll
    for i in range(first):
        steps(i, i % unroll, i // unroll)
    with engine.Fori(first // unroll, first // unroll + whole) as o:
        for u in range(unroll):
            steps(o * unroll + u, u, o)
    for i in range(first + unroll * whole, PAIRS + lead):
        steps(i, i % unroll, i // unroll)


def runs(i, back):
    return not isinstance(i, int) or 0 <= i - back < PAIRS


def past_first(i, n):
    return not isinstance(i, int) or i >= n


def node_stage0(nc, s, ins):
    U = 4
    LEAD, FIRST = 8, 12
    with ExitStack() as ctx:
        sb = lambda name, shape, dt: ctx.enter_context(nc.sbuf_tensor(name, shape, dt))
        ps = lambda name, shape: ctx.enter_context(nc.psum_tensor(name, shape, F32))
        sem = s.sem
        ring = lambda name, shape: [sb(f"{name}{i}", shape, F32) for i in range(U)]
        wl, bias = sb("wl", [P, D], F32), sb("bias_parts", [3, 2 * D], BF16)
        has, half, den = sb("has", [P, TILES], F32), sb("half", [P, TILES], F32), sb("den", [P, TILES], F32)
        ka, kx = sb("ka", [P, TILES], F32), sb("kx", [P, TILES], F32)
        eps = sb("eps0", [P, 1], F32)
        x, scaled, mixed, mT = (ring(n, [P, 2, D]) for n in ("n_x", "scaled", "mixed", "mT"))
        y, x1, x1T, c, rest = (ring(n, [P, 2, D]) for n in ("y", "x1_", "x1T", "c_rows", "rest1_"))
        stats, mv = ring("stats0", [P, 2, 6]), ring("mv0", [P, 2, 2])
        std, rstd = ring("std0", [P, 2]), ring("rstd0", [P, 2])
        mT_ps, y_ps, x1T_ps = ps("mT_ps", [P, 2, 512]), ps("y_ps", [P, 2, 512]), ps("x1T_ps", [P, 2, 512])
        cd_ps = ps("cd_ps", [P, 2, 2, 2 * D])
        w_in, x_pad = sem("wl_in"), sem("n_x_pad")
        x_in = [sem(f"n_x_in{i}") for i in range(U)]
        x1_out = [sem(f"x1_out{i}") for i in range(U)]
        c_out = [sem(f"c_out{i}") for i in range(U)]
        factors, chain = sem("factors"), sem("n_chain")
        scaled_made, mixed_made, mT_made, mT_evac, y_made = (
            sem("scaled_made"), sem("mixed_made"), sem("mT_made"), sem("mT_evac"), sem("y_made"))
        y_sum, stats_made, var_made, std_made, rstd_made, x1_made = (
            sem("y_sum"), sem("stats_made"), sem("var_made"), sem("std_made"), sem("rstd_made"), sem("x1_made"))
        x1T_made, x1T_evac, cd_made, c_evac = sem("x1T_made"), sem("x1T_evac"), sem("cd_made"), sem("c_evac")
        hi_made, rest_made, mid_made, lo_made = sem("hi_made"), sem("rest_made"), sem("mid_made"), sem("lo_made")
        go, dve_go, sp_go = sem("n_go"), sem("n_dve_go"), sem("n_sp_go")
        acc = s.acc

        def split(i, part):
            return s.split[:, bass.ds(i * 2, 2), part, :]

        with nc.Block() as block:
            @block.sync
            def _(sp):
                sp.dma_start(wl[:, :], ins["L0_gnn_Wl"]).then_inc(w_in, 16)
                sp.dma_start(bias[:, :], s.row_parts[:, 8 * D:10 * D]).then_inc(w_in, 16)

                def rows_of(table, i):
                    return table[bass.ds(i * (2 * P), 2 * P), :].rearrange("(t p) d -> p t d", p=P)

                def move(i, store, table, tile, done):
                    if isinstance(i, int) and i == PAIRS - 1:
                        a = table[2 * i * P:(2 * i + 1) * P, :].rearrange("(t p) d -> p t d", p=P)
                        b = table[(TILES - 1) * P:N, :]
                        ends = ((a, tile[:, 0:1, :]), (b, tile[0:LASTROWS, 1, :]))
                    else:
                        ends = ((rows_of(table, i), tile[:, :, :]),)
                    for d, t in ends:
                        sp.dma_start(*((d, t) if store else (t, d))).then_inc(done, 16)

                def steps(i, u, o):
                    if runs(i, 0):
                        if past_first(i, 4):
                            sp.wait_ge(y_sum, i - 3)
                            sp.sem_inc(sp_go, 1)
                        if isinstance(i, int) and i == PAIRS - 1:
                            sp.wait_ge(x_pad, 1)
                        move(i, False, ins["x"], x[u], x_in[u])
                    if runs(i, 5):
                        sp.wait_ge(x1_made, i - 4)
                        sp.sem_inc(sp_go, 1)
                        move(i - 5, True, s.x1, x1[(u - 5) % U], x1_out[(u - 5) % U])
                    if runs(i, 7):
                        sp.wait_ge(c_evac, i - 6)
                        sp.sem_inc(sp_go, 1)
                        move(i - 7, True, s.c, c[(u - 7) % U], c_out[(u - 7) % U])
                run_pairs(sp, steps, LEAD, FIRST)
                for u in range(U):
                    n = len(range(u, PAIRS, U)) + (u == (PAIRS - 1) % U)
                    sp.wait_ge(x1_out[u], 16 * n)
                    sp.wait_ge(c_out[u], 16 * n)

            @block.gpsimd
            def _(pool):
                pool.wait_ge(y_sum, PAIRS - U)
                nc.gpsimd.memset(x[(PAIRS - 1) % U][:, 1, :], 0.0).then_inc(x_pad, 1)

            @block.scalar
            def _(act):
                act.wait_ge(factors, 1)

                def steps(i, u, o):
                    if runs(i, 0):
                        if past_first(i, 4):
                            act.wait_ge(mixed_made, i - 3)
                            act.sem_inc(go, 1)
                        for t in range(2):
                            last = nc.scalar.activation(scaled[u][:, t, :], acc[:, bass.ds(i * 2 + t, 1), 0:D],
                                                        ACT.Copy, scale=ka[:, bass.ds(i * 2 + t, 1)])
                        last.then_inc(scaled_made, 1)
                    if runs(i, 3):
                        v = (u - 3) % U
                        act.wait_ge(var_made, i - 2)
                        if past_first(i, 7):
                            act.wait_ge(rstd_made, i - 6)
                        act.sem_inc(go, 1)
                        nc.scalar.activation(std[v][:, :], mv[v][:, :, 1], ACT.Sqrt,
                                             bias=eps[:, 0:1]).then_inc(std_made, 1)
                    if runs(i, 1):
                        v = (u - 1) % U
                        act.wait_ge(mT_made, i)
                        if past_first(i, 5):
                            act.wait_ge(y_made, i - 4)
                        act.sem_inc(go, 1)
                        nc.scalar.copy(mT[v][:, :, :], mT_ps[:, (u - 1) % 2, 0:2 * P]).then_inc(mT_evac, 1)
                    if runs(i, 4):
                        act.wait_ge(x1T_made, i - 3)
                        if past_first(i, 8):
                            act.wait_ge(cd_made, i - 7)
                        act.sem_inc(go, 1)
                        nc.scalar.copy(x1T[u][:, :, :], x1T_ps[:, u % 2, 0:2 * P]).then_inc(x1T_evac, 1)
                    if runs(i, 5):
                        v = (u - 5) % U
                        act.wait_ge(cd_made, i - 4)
                        if past_first(i, 9):
                            act.wait_ge(c_out[v], (o - (2 if u >= 1 else 3)) * 16 + 16)
                        act.sem_inc(go, 1)
                        nc.scalar.copy(c[v][:, :, :], cd_ps[:, v % 2, :, 0:D]).then_inc(c_evac, 1)
                        nc.scalar.copy(split(i - 5, 0), cd_ps[:, v % 2, :, D:2 * D]).then_inc(hi_made, 1)
                    if runs(i, 7):
                        act.wait_ge(rest_made, i - 6)
                        act.sem_inc(go, 1)
                        nc.scalar.copy(split(i - 7, 1), rest[(u - 7) % U][:, :, :]).then_inc(mid_made, 1)

                run_pairs(act, steps, LEAD, FIRST)

            @block.tensor
            def _(pe):
                pe.wait_ge(w_in, 32)

                def steps(i, u, o):
                    if runs(i, 1):
                        v = (u - 1) % U
                        pe.wait_ge(mixed_made, i)
                        if past_first(i, 3):
                            pe.wait_ge(mT_evac, i - 2)
                        for t in range(2):
                            last = nc.tensor.transpose(mT_ps[:, v % 2, t * P:(t + 1) * P], mixed[v][:, t, :],
                                                       s.ident_f[:, :])
                        last.then_inc(mT_made, 1)
                    if runs(i, 2):
                        v = (u - 2) % U
                        pe.wait_ge(mT_evac, i - 1)
                        if past_first(i, 4):
                            pe.wait_ge(y_sum, i - 3)
                        for t in range(2):
                            there = y_ps[:, v % 2, t * D:(t + 1) * D]
                            nc.tensor.matmul(there, mT[v][:, t, :], wl[:, :], start=True, stop=False)
                            last = nc.tensor.matmul(there, s.ones_r[:, :], bias[:, 0:D], start=False, stop=True)
                        last.then_inc(y_made, 1)
                    if runs(i, 4):
                        pe.wait_ge(x1_made, i - 3)
                        if past_first(i, 6):
                            pe.wait_ge(x1T_evac, i - 5)
                        for t in range(2):
                            last = nc.tensor.transpose(x1T_ps[:, u % 2, t * P:(t + 1) * P], x1[u][:, t, :],
                                                       s.ident_f[:, :])
                        last.then_inc(x1T_made, 1)
                    if runs(i, 5):
                        v = (u - 5) % U
                        pe.wait_ge(x1T_evac, i - 4)
                        if past_first(i, 7):
                            pe.wait_ge(rest_made, i - 6)
                            pe.wait_ge(c_evac, i - 6)
                        for t in range(2):
                            for side in range(2):
                                there = cd_ps[:, v % 2, t, side * D:(side + 1) * D]
                                last = nc.tensor.matmul(there, x1T[v][:, t, :], s.w1cd[:, side * D:(side + 1) * D],
                                                        start=True, stop=(side == 1))
                                if side == 0:
                                    nc.tensor.matmul(there, s.ones_r[:, :], bias[:, D:2 * D], start=False, stop=True)
                        last.then_inc(cd_made, 1)
                run_pairs(pe, steps, LEAD, FIRST)

            @block.vector
            def _(dve):
                sums = acc[:, :, D]
                dve.memset(eps[:, :], 1e-5)
                dve.tensor_scalar(half[:, :], sums, 0.0, 0.5, ALU.is_gt, ALU.mult).then_inc(chain, 1)
                dve.tensor_scalar(den[:, :], sums, 1e-9, None, ALU.add).then_inc(chain, 1)
                dve.wait_ge(chain, 2)
                dve.reciprocal(has[:, :], den[:, :]).then_inc(chain, 1)
                dve.tensor_scalar(kx[:, :], half[:, :], -1.0, 1.0, ALU.mult, ALU.add)
                dve.wait_ge(chain, 3)
                dve.tensor_tensor(ka[:, :], half[:, :], has[:, :], ALU.mult).then_inc(factors, 1)
                dve.wait_ge(factors, 1)

                def steps(i, u, o):
                    if runs(i, 2):
                        v = (u - 2) % U
                        dve.wait_ge(y_made, i - 1)
                        if past_first(i, 6):
                            dve.wait_ge(x1_made, i - 5)
                        dve.scalar_tensor_tensor(y[v][:, :, :].rearrange("p t d -> p (t d)"),
                                                 y_ps[:, v % 2, 0:2 * D], 0.0,
                                                 x[v][:, :, :].rearrange("p t d -> p (t d)"),
                                                 ALU.max, ALU.add).then_inc(y_sum, 1)
                    if runs(i, 3):
                        v = (u - 3) % U
                        dve.wait_ge(std_made, i - 2)
                        dve.reciprocal(rstd[v][:, :], std[v][:, :]).then_inc(rstd_made, 1)
                    if runs(i, 2):
                        v = (u - 2) % U
                        dve.wait_ge(y_sum, i - 1)
                        for t in range(2):
                            last = dve.bn_stats(stats[v][:, t, :], y[v][:, t, :])
                        last.then_inc(stats_made, 1)
                    if runs(i, 3):
                        v = (u - 3) % U
                        dve.wait_ge(rstd_made, i - 2)
                        if past_first(i, 7):
                            dve.wait_ge(x1T_made, i - 6)
                            dve.wait_ge(x1_out[v], (o - (1 if u == 3 else 2)) * 16 + 16)
                        for t in range(2):
                            last = dve.tensor_scalar(x1[v][:, t, :], y[v][:, t, :], mv[v][:, t, 0:1],
                                                     rstd[v][:, t:t + 1], ALU.subtract, ALU.mult)
                        last.then_inc(x1_made, 1)
                    if runs(i, 2):
                        v = (u - 2) % U
                        dve.wait_ge(stats_made, i - 1)
                        dve.sem_inc(dve_go, 1)
                        for t in range(2):
                            last = dve.bn_aggr(mv[v][:, t, :], stats[v][:, t, :])
                        last.then_inc(var_made, 1)
                    if runs(i, 0):
                        dve.wait_ge(scaled_made, i + 1)
                        last_one = isinstance(i, int) and i == PAIRS - 1
                        dve.wait_ge(x_in[u], o * 16 + 16 + 16 * last_one)
                        if past_first(i, 4):
                            dve.wait_ge(mT_made, i - 3)
                        for t in range(2):
                            last = dve.scalar_tensor_tensor(mixed[u][:, t, :], x[u][:, t, :],
                                                            kx[:, bass.ds(i * 2 + t, 1)], scaled[u][:, t, :],
                                                            ALU.mult, ALU.add)
                        last.then_inc(mixed_made, 1)
                    if runs(i, 6):
                        v = (u - 6) % U
                        dve.wait_ge(hi_made, i - 5)
                        if past_first(i, 10):
                            dve.wait_ge(lo_made, i - 9)
                        dve.tensor_tensor(rest[v][:, :, :], cd_ps[:, v % 2, :, D:2 * D], split(i - 6, 0),
                                          ALU.subtract).then_inc(rest_made, 1)
                    if runs(i, 8):
                        dve.wait_ge(mid_made, i - 7)
                        dve.tensor_tensor(split(i - 8, 2), rest[u][:, :, :], split(i - 8, 1),
                                          ALU.subtract).then_inc(lo_made, 1)
                run_pairs(dve, steps, LEAD, FIRST)


def loop_groups(engine, steps, lead):
    for q in range(R):
        steps(q, q, 0)
    with engine.Fori(1, BODIES) as o:
        for q in range(R):
            steps(o * R + q, q, o)
    for q in range(lead):
        steps(GROUPS + q, q, BODIES)


def has(g, back):
    return not isinstance(g, int) or 0 <= g - back < GROUPS


def used(g, n):
    return not isinstance(g, int) or g >= n


def edge_stage1(nc, s, ins):
    W = D + 1
    with ExitStack() as ctx:
        sb = lambda name, shape, dt: ctx.enter_context(nc.sbuf_tensor(name, shape, dt))
        ps = lambda name, shape, dt: ctx.enter_context(nc.psum_tensor(name, shape, dt))
        sem = s.sem
        step_rows, place_of = sb("step_rows1", [2, STEPS], I16), sb("places1", [P, STEPS], BF16)
        tile_of, edge_of = step_rows[0:1, :], step_rows[1:2, :]
        idx = [sb(f"idx1_{q}", [P, G], I32) for q in range(R)]
        crows = [sb(f"crows{q}", [P, G, D], F32) for q in range(R)]
        ef = [sb(f"ef{q}", [P, G, DE], F32) for q in range(R)]
        hot = [sb(f"hot1_{q}", [P, G, P], BF16) for q in range(R)]
        hotT = [sb(f"hotT1_{i}", [P, G, P], BF16) for i in range(2)]
        efT = [sb(f"efT{i}", [P, G // 2, P], F32) for i in range(2)]
        w1e2, gw2 = sb("w1e2", [P, 2, D], F32), sb("gate_w2", [P, 2], F32)
        hotw = [sb(f"hotw1_{i}", [P, G, P], F32) for i in range(2)]
        h = [sb(f"h1_{i}", [P, G, D], F32) for i in range(2)]
        z = [sb(f"z{i}", [P, G, W], F32) for i in range(2)]
        sq = sb("sq", [P, 4, D], BF16)
        ss, lnv, rstd = (sb(n, [P, 2, G], F32) for n in ("ss", "lnv", "rstd1"))
        eg, eg1, gate = (sb(n, [P, 2, G], F32) for n in ("eg", "eg1", "gate"))
        ln_g, neg_b, gb, eps = (sb("ln_g", [P, D], F32), sb("neg_b", [P, D], F32), sb("neg_gate_b", [P, 1], F32), sb("eps1", [P, 1], F32))
        hotT_ps = ps("hotT1_ps", [P, G, P], BF16)
        efT_ps = ps("efT_ps", [P, 4, P], F32)
        pre = ps("pre1", [P, 2, 4, D], F32)
        out = ps("scattered1", [P, 3, 512], F32)
        gate_ps = ps("gate_ps", [P, 512], F32)
        w_in, zeroed, steps_in, negated = sem("w1_in"), sem("zeroed1"), sem("steps1_in"), sem("negated")
        idx_in = [sem(f"idx1_in{q}") for q in range(R)]
        rows_in = [sem(f"c_in{q}") for q in range(R)]
        ef_in = [sem(f"ef_in{q}") for q in range(R)]
        hot_made, hot_turned, hotT_made = sem("hot1_made"), sem("hot1_turned"), sem("hotT1_made")
        ef_turned, efT_made = sem("ef_turned"), sem("efT_made")
        pre_made, pre_used, gate_made, gate_read = sem("pre1_made"), sem("pre1_used"), sem("gatel_made"), sem("gate_read")
        ss_made, ln_made, rstd_made = sem("ss_made"), sem("ln_made"), sem("rstd1_made")
        eg1_made, gates_made, hotw_made = sem("eg1_made"), sem("gates_made"), sem("hotw1_made")
        scaled, z_made = sem("z_scaled"), sem("z_made")
        scattered, added = sem("scattered1_up"), sem("added1")
        issue, act_go, pe_go, sp_go = sem("issue1"), sem("act_go1"), sem("pe_go1"), sem("sp_go1")
        acc = s.acc
        slot = [(k // 3, (k % 3) * W) for k in range(G)]

        with nc.Block() as block:
            @block.sync
            def _(sp):
                sp.dma_start(tile_of, s.tile_of[1][:, :]).then_inc(steps_in, 16)
                sp.dma_start(edge_of, s.edge_of[:, :]).then_inc(steps_in, 16)
                sp.dma_start(place_of[:, :], s.place_of[1][:, :]).then_inc(steps_in, 16)
                row = lambda name, n: ins[name].rearrange("(a d) -> a d", a=1).to_broadcast([P, n])
                sp.dma_start(ln_g[:, :], row("L1_gnn_ln_g", D)).then_inc(w_in, 16)
                sp.dma_start(neg_b[:, :], row("L1_gnn_ln_b", D)).then_inc(w_in, 16)
                sp.dma_start(gb[:, :], row("L1_gnn_gate_b", 1)).then_inc(w_in, 16)
                sp.wait_ge(zeroed, 1)
                for half in range(2):
                    there = slice(half * DE, (half + 1) * DE)
                    sp.dma_start(w1e2[there, half, :], s.w1e[:, :]).then_inc(w_in, 16)
                    sp.dma_start(gw2[there, half:half + 1], ins["L1_gnn_gate_w"]).then_inc(w_in, 16)
                sp.wait_ge(steps_in, 48)

                def load(g, q, features):
                    sp.dma_start(idx[q][:, :], s.gather_of[1][:, bass.ds(g * G, G)]).then_inc(idx_in[q], 16)
                    edges = load_values(nc, mybir.EngineType.SP, edge_of[0:1, bass.ds(g * G, G)], (E - P) // 64)
                    for k in range(G):
                        sp.dma_start(ef[q][:, k, :],
                                     features[bass.ds(edges[k] * 64, P), :]).then_inc(ef_in[q], 16)

                def load_all(features):
                    for q in range(R):
                        load(q, q, features)
                    with sp.Fori(1, BODIES) as o:
                        for q in range(R):
                            sp.wait_ge(rows_in[q], o * (16 * G))
                            sp.sem_inc(sp_go, 1)
                            sp.wait_ge(ef_turned, (o - 1) * R + q + 1)
                            sp.sem_inc(sp_go, 1)
                            load(o * R + q, q, features)
                regrouped = load_values(nc, mybir.EngineType.SP, s.unsorted[0:1, 0:1], 1)[0]
                with sp.If(regrouped):
                    load_all(s.grouped_features)
                with sp.Else():
                    load_all(ins["edge_attr_64"])

            @block.gpsimd
            def _(pool):
                pool.wait_ge(zeroed, 1)
                for i in range(2):
                    nc.gpsimd.memset(z[i][:, :, D:W], 1.0).then_inc(zeroed, 1)

                def gather(q):
                    for k in range(G):
                        pool.indirect_dma_start(
                            out=crows[q][:, k, :], out_offset=None, in_=s.c[:, :],
                            in_offset=bass.IndirectOffsetOnAxis(ap=idx[q][:, k:k + 1], axis=0),
                        ).then_inc(rows_in[q], 16)
                for q in range(R):
                    pool.wait_ge(idx_in[q], 16)
                    gather(q)
                with pool.Fori(1, BODIES) as o:
                    for q in range(R):
                        pool.wait_ge(idx_in[q], o * 16 + 16)
                        pool.wait_ge(pre_used, (o - 1) * (2 * R) + 2 * q + 2)
                        pool.sem_inc(issue, 1)
                        gather(q)

            @block.tensor
            def _(pe):
                pe.wait_ge(steps_in, 48)
                pe.wait_ge(w_in, 16 * 7)
                pe.wait_ge(zeroed, 3)
                pe.wait_ge(added, 1)

                def steps(g, q, o):
                    if has(g, 1):
                        par = (q - 1) % 2
                        tiles = load_values(nc, mybir.EngineType.PE, tile_of[0:1, bass.ds((g - 1) * G, G)], TILES - 1)
                        pe.wait_ge(hotT_made, g)
                        pe.wait_ge(efT_made, g)
                        for half in range(2):
                            if used(g, 2):
                                pe.wait_ge(pre_used, g * 2 + half - 3)
                            for k in range(4):
                                for part in range(3):
                                    nc.tensor.matmul(pre[:, half, k, :], hotT[par][:, 4 * half + k, :],
                                                     s.split[:, bass.ds(tiles[4 * half + k], 1), part, :],
                                                     start=(part == 0), stop=False)
                                last = nc.tensor.matmul(pre[:, half, k, :], efT[par][:, 2 * half + k // 2, :],
                                                        w1e2[:, k % 2, :], start=False, stop=True)
                            last.then_inc(pre_made, 1)
                        if used(g, 2):
                            pe.wait_ge(gate_read, g - 1)
                        for k in range(G // 2):
                            last = nc.tensor.matmul(gate_ps[:, 2 * k:2 * k + 2], efT[par][:, k, :], gw2[:, :],
                                                    start=True, stop=True)
                        last.then_inc(gate_made, 1)
                    if has(g, 0):
                        pe.wait_ge(ef_in[q], o * (16 * G) + 16 * G)
                        if used(g, 1):
                            pe.wait_ge(efT_made, g)
                        for k in range(G // 2):
                            last = nc.tensor.transpose(efT_ps[:, k, :],
                                                       ef[q][:, 2 * k:2 * k + 2, :].rearrange("p a d -> p (a d)"),
                                                       s.ident_f[:, :])
                        last.then_inc(ef_turned, 1)
                        pe.wait_ge(hot_made, g + 1)
                        if used(g, 1):
                            pe.wait_ge(hotT_made, g)
                        for k in range(G):
                            last = nc.tensor.transpose(hotT_ps[:, k, :], hot[q][:, k, :], s.ident_b[:, :])
                        last.then_inc(hot_turned, 1)
                    if has(g, 3):
                        par = (q - 3) % 2
                        pe.wait_ge(hotw_made, g - 2)
                        for k in range(G):
                            if k % 4 == 0:
                                pe.wait_ge(z_made, g * 2 - 5 + k // 4)
                            bank, at = slot[k]
                            if used(g, 4) and at == 0:
                                pe.wait_ge(added, (g - 4) * G + min(k + 3, G) + 1)
                            last = nc.tensor.matmul(out[:, bank, at:at + W], hotw[par][:, k, :], z[par][:, k, :],
                                                    start=True, stop=True)
                            if k in (2, 5, 7):
                                last.then_inc(scattered, 1)
                loop_groups(pe, steps, 4)

            @block.scalar
            def _(act):
                act.preload_act_table_set("natural_log_exp_and_others")
                act.wait_ge(negated, 2)

                def steps(g, q, o):
                    par, other = q % 2, 1 - q % 2
                    if has(g, 2):
                        for half in range(2):
                            if used(g, 3) or half:
                                act.wait_ge(ss_made, g * 2 - 4 + half)
                            act.wait_ge(pre_used, g * 2 + half - 3)
                            act.sem_inc(act_go, 1)
                            for k in range(4 * half, 4 * half + 4):
                                last = nc.scalar.activation(sq[:, k % 4, :], h[par][:, k, :], ACT.Square,
                                                            accum_out=ss[:, par, k:k + 1])
                            last.then_inc(ss_made, 1)
                        act.wait_ge(ss_made, g * 2 - 2)
                        act.sem_inc(act_go, 1)
                        nc.scalar.activation(lnv[:, par, :], ss[:, par, :], ACT.Ln, bias=eps[:, 0:1],
                                             scale=1.0 / D).then_inc(ln_made, 1)
                    if has(g, 3):
                        act.wait_ge(gates_made, g - 2)
                        act.sem_inc(act_go, 1)
                        for k in range(G):
                            last = nc.scalar.activation(hotw[other][:, k, :], hot[(q - 3) % R][:, k, :], ACT.Copy,
                                                        scale=gate[:, other, k:k + 1])
                        last.then_inc(hotw_made, 1)
                    if has(g, 2):
                        act.wait_ge(ln_made, g - 1)
                        if used(g, 4):
                            act.wait_ge(scaled, g * 2 - 6)
                        act.sem_inc(act_go, 1)
                        nc.scalar.activation(rstd[:, par, :], lnv[:, par, :], ACT.Exp,
                                             scale=-0.5).then_inc(rstd_made, 1)
                    if has(g, 0):
                        act.wait_ge(ef_turned, g + 1)
                        if used(g, 2):
                            act.wait_ge(gate_made, g - 1)
                        act.sem_inc(act_go, 1)
                        nc.scalar.copy(efT[par][:, :, :], efT_ps[:, :, :]).then_inc(efT_made, 1)
                        act.wait_ge(hot_turned, g + 1)
                        act.sem_inc(act_go, 1)
                        nc.scalar.copy(hotT[par][:, :, :], hotT_ps[:, :, :]).then_inc(hotT_made, 1)
                    if has(g, 1):
                        act.wait_ge(gate_made, g)
                        if used(g, 3):
                            act.wait_ge(eg1_made, g - 2)
                        act.sem_inc(act_go, 1)
                        nc.scalar.activation(eg[:, other, :], gate_ps[:, 0:G], ACT.Exp, bias=gb[:, 0:1],
                                             scale=-1.0).then_inc(gate_read, 1)
                loop_groups(act, steps, 3)

            @block.vector
            def _(dve):
                dve.memset(w1e2[:, :, :], 0.0)
                dve.memset(gw2[:, :], 0.0).then_inc(zeroed, 1)
                dve.memset(eps[:, :], 1e-5)
                dve.memset(acc[:, :, 0:W], 0.0).then_inc(added, 1)
                dve.wait_ge(w_in, 16 * 7)
                dve.wait_ge(steps_in, 48)
                dve.tensor_scalar(neg_b[:, :], neg_b[:, :], -1.0, None, ALU.mult).then_inc(negated, 1)
                dve.tensor_scalar(gb[:, :], gb[:, :], -1.0, None, ALU.mult).then_inc(negated, 1)
                dve.wait_ge(negated, 2)
                dve.wait_ge(zeroed, 3)
                spread_b = neg_b[:, :].rearrange("p (a d) -> p a d", a=1).to_broadcast([P, 4, D])

                def steps(g, q, o):
                    par, other = q % 2, 1 - q % 2
                    if has(g, 0):
                        if used(g, R):
                            dve.wait_ge(hotw_made, g - (R - 1))
                        for k in range(G):
                            last = dve.tensor_scalar(hot[q][:, k, :], s.lane_b[:, :],
                                                     place_of[:, bass.ds(g * G + k, 1)], None, ALU.is_equal)
                        last.then_inc(hot_made, 1)
                    if has(g, 3):
                        dve.wait_ge(rstd_made, g - 2)
                    if has(g, 4):
                        tiles = load_values(nc, mybir.EngineType.DVE, tile_of[0:1, bass.ds((g - 4) * G, G)], TILES - 1)
                    for k in range(G):
                        if has(g, 3):
                            last = dve.scalar_tensor_tensor(z[other][:, k, 0:D], h[other][:, k, :],
                                                            rstd[:, other, k:k + 1], ln_g[:, :], ALU.mult, ALU.mult)
                            if k % 4 == 3:
                                last.then_inc(scaled, 1)
                        if has(g, 4):
                            bank, at = slot[k]
                            if at == 0:
                                dve.wait_ge(scattered, g * 3 + bank - 11)
                            dve.wait_ge(added, (g - 4) * G + k + 1)
                            place = acc[:, bass.ds(tiles[k], 1), 0:W]
                            dve.tensor_tensor(place, place, out[:, bank:bank + 1, at:at + W],
                                              ALU.add).then_inc(added, 1)
                        if has(g, 3) and k % 4 == 3:
                            half = k // 4
                            dve.wait_ge(scaled, g * 2 + half - 5)
                            part = z[other][:, 4 * half:4 * half + 4, 0:D]
                            dve.tensor_tensor(part, part, spread_b, ALU.max).then_inc(z_made, 1)
                    if has(g, 1):
                        p1 = (q - 1) % R
                        dve.wait_ge(rows_in[p1], o * (16 * G) + (0 if q == 0 else 16 * G))
                        if used(g, 3):
                            dve.wait_ge(scaled, g * 2 - 4)
                            dve.wait_ge(ss_made, g * 2 - 4)
                        for half in range(2):
                            dve.wait_ge(pre_made, g * 2 + half - 1)
                            dve.tensor_tensor(h[other][:, 4 * half:4 * half + 4, :], pre[:, half],
                                              crows[p1][:, 4 * half:4 * half + 4, :], ALU.add).then_inc(pre_used, 1)
                    if has(g, 2):
                        dve.wait_ge(gate_read, g - 1)
                        if used(g, 4):
                            dve.wait_ge(hotw_made, g - 3)
                        dve.tensor_scalar(eg1[:, par, :], eg[:, par, :], 1.0, None, ALU.add).then_inc(eg1_made, 1)
                        dve.wait_ge(eg1_made, g - 1)
                        dve.reciprocal(gate[:, par, :], eg1[:, par, :]).then_inc(gates_made, 1)
                loop_groups(dve, steps, 4)


def node_stage1(nc, s, ins, result):
    with ExitStack() as ctx:
        sb = lambda name, shape, dt: ctx.enter_context(nc.sbuf_tensor(name, shape, dt))
        ps = lambda name, shape: ctx.enter_context(nc.psum_tensor(name, shape, F32))
        sem = s.sem
        U, FIRST, LEAD = 6, 6, 4
        wfold, whh = sb("wfold_sb", [P, 3 * D], F32), sb("whh_sb", [P, 3 * D], F32)
        AUG = 12
        aug_w, aug = sb("aug_w", [AUG, 4 * D], BF16), sb("aug", [P, TILES, AUG], BF16)
        pair_aug = [sb(f"pair_aug{i}", [P, 2, AUG], BF16) for i in range(2)]
        s_rest = sb("s_rest", [P, TILES], F32)
        w_in = sem("gru_w_in")
        x = [sb(f"g_x{i}", [P, 2, D], F32) for i in range(U)]
        both = [sb(f"sums{i}", [P, 2, D], F32) for i in range(2)]
        T = [sb(f"gT{i}", [P, 4, P], F32) for i in range(2)]
        augT = [sb(f"augT{i}", [AUG, 2, P], BF16) for i in range(2)]
        rz = [sb(f"rz{i}", [P, 2, 2 * D], F32) for i in range(2)]
        t1, t2, new, diff, kept = ([sb(f"{n}{i}", [P, 2, D], F32) for i in range(2)]
                                   for n in ("t1_", "t2_", "new", "diff", "kept"))
        y = [sb(f"gy{i}", [P, 2, D], F32) for i in range(2)]
        stats, mv = sb("stats1", [P, 2, 2, 6], F32), sb("mv1", [P, TILES, 2], F32)
        std, rstd = sb("g_std", [P, TILES], F32), sb("g_rstd", [P, TILES], F32)
        eps = sb("g_eps", [P, 1], F32)
        T_ps = ps("T_ps", [P, 2, 4, P])
        aug_ps = ctx.enter_context(nc.psum_tensor("aug_ps", [P, 2, 1024], BF16))
        rz_ps, n_ps = ps("rz_ps", [P, 2, 2, 2 * D]), ps("n_ps", [P, 2, 2, 2 * D])
        x_pad = sem("g_x_pad")
        x_in = [sem(f"g_x_in{i}") for i in range(U)]
        both_made, T_made, T_evac, rz_made, n_made = (
            sem("both_made"), sem("T_made"), sem("T_evac"), sem("rz_made"), sem("n_made"))
        gates, t1_made, t2_made, new_made, diff_made, zd_made = (
            sem("g_gates"), sem("t1_made"), sem("t2_made"), sem("new_made"), sem("diff_made"), sem("zd_made"))
        kept_made, y_made, stats_made, var_made, std_made, rstd_made, o_made = (
            sem("kept_made"), sem("gy_made"), sem("g_stats"), sem("g_var"), sem("g_std_made"), sem("g_rstd_made"),
            sem("o_made"))
        stored, go, eps_made = sem("stored_out"), sem("g_go"), sem("g_eps_made")
        dve_go, aggr_made, sp_go, aug_made = sem("g_dve_go"), sem("g_aggr_made"), sem("g_sp_go"), sem("aug_made")
        mv2 = sb("mv_pair", [P, 2, 2, 2], F32)
        acc = s.acc
        CHUNK = 14
        STORES = TILES // CHUNK
        assert STORES * CHUNK == TILES

        with nc.Block() as block:
            @block.sync
            def _(sp):
                for t, w in ((wfold, s.wfold), (whh, s.whh)):
                    sp.dma_start(t[:, :], w[:, :]).then_inc(w_in, 16)
                for a in range(3):
                    sp.dma_start(aug_w[3 * a:3 * a + 3, :], s.row_parts[:, 0:4 * D]).then_inc(w_in, 16)
                sp.dma_start(aug_w[9:12, :], s.row_parts[:, 4 * D:8 * D]).then_inc(w_in, 16)

                def steps(i, u, o):
                    if past_first(i, U):
                        sp.wait_ge(y_made, i - (U - 1))
                        sp.sem_inc(sp_go, 1)
                    if isinstance(i, int) and i == PAIRS - 1:
                        sp.wait_ge(x_pad, 1)
                        a = s.x1[2 * i * P:(2 * i + 1) * P, :].rearrange("(t p) d -> p t d", p=P)
                        sp.dma_start(x[u][:, 0:1, :], a).then_inc(x_in[u], 16)
                        sp.dma_start(x[u][0:LASTROWS, 1, :], s.x1[(TILES - 1) * P:N, :]).then_inc(x_in[u], 16)
                    else:
                        a = s.x1[bass.ds(i * (2 * P), 2 * P), :].rearrange("(t p) d -> p t d", p=P)
                        sp.dma_start(x[u][:, :, :], a).then_inc(x_in[u], 16)
                run_pairs(sp, steps, 0, FIRST, U)
                for c in range(STORES):
                    sp.wait_ge(o_made, c + 1)
                    full = CHUNK if c < STORES - 1 else CHUNK - 1
                    view = result[c * CHUNK * P:(c * CHUNK + full) * P, :].rearrange("(t p) d -> p t d", p=P)
                    sp.dma_start(view, acc[:, c * CHUNK:c * CHUNK + full, 0:D]).then_inc(stored, 16)
                sp.dma_start(result[(TILES - 1) * P:N, :], acc[0:LASTROWS, TILES - 1, 0:D]).then_inc(stored, 16)
                sp.wait_ge(stored, 16 * (STORES + 1))

            @block.gpsimd
            def _(pool):
                pool.wait_ge(aug_made, 8)

                def steps(i, u, o):
                    if past_first(i, 2):
                        pool.wait_ge(T_made, i - 1)
                    nc.gpsimd.tensor_copy(both[u % 2][:, :, :], acc[:, bass.ds(i * 2, 2), 0:D])
                    nc.gpsimd.tensor_copy(pair_aug[u % 2][:, :, :], aug[:, bass.ds(i * 2, 2), :]).then_inc(both_made, 1)
                    if isinstance(i, int) and i == PAIRS - 1:
                        pool.wait_ge(y_made, PAIRS - U)
                        nc.gpsimd.memset(x[u][:, 1, :], 0.0).then_inc(x_pad, 1)
                run_pairs(pool, steps, 0, FIRST, U)

            @block.tensor
            def _(pe):
                pe.wait_ge(w_in, 16 * 6)

                def steps(i, u, o):
                    par, other = u % 2, 1 - u % 2
                    if runs(i, 1):
                        v = (u - 1) % U
                        last_one = isinstance(i, int) and i == PAIRS
                        pe.wait_ge(x_in[v], (o + (1 if u >= 1 else 0)) * 16 + 16 * last_one)
                        pe.wait_ge(both_made, i)
                        if past_first(i, 3):
                            pe.wait_ge(T_evac, (i - 2) * 2)
                        for t in range(2):
                            nc.tensor.transpose(T_ps[:, other, t, :], both[other][:, t, :], s.ident_f[:, :])
                            nc.tensor.transpose(T_ps[:, other, 2 + t, :], x[v][:, t, :], s.ident_f[:, :])
                            last = nc.tensor.transpose(aug_ps[0:AUG, other, t * P:(t + 1) * P],
                                                       pair_aug[other][:, t, :], s.ident_b[:, :])
                        last.then_inc(T_made, 1)
                    if runs(i, 2):
                        pe.wait_ge(T_evac, i * 2 - 2)
                        if past_first(i, 4):
                            pe.wait_ge(gates, i - 3)
                        for t in range(2):
                            nc.tensor.matmul(rz_ps[:, par, t, :], T[par][:, t, :], wfold[:, 0:2 * D],
                                             start=True, stop=False)
                            nc.tensor.matmul(rz_ps[:, par, t, :], T[par][:, 2 + t, :], whh[:, 0:2 * D],
                                             start=False, stop=False)
                            last = nc.tensor.matmul(rz_ps[:, par, t, :], augT[par][:, t, :], aug_w[:, 0:2 * D],
                                                    start=False, stop=True)
                        last.then_inc(rz_made, 1)
                        if past_first(i, 4):
                            pe.wait_ge(t2_made, i - 3)
                        for t in range(2):
                            for side, part, weight in ((0, T[par][:, t, :], wfold), (1, T[par][:, 2 + t, :], whh)):
                                there = n_ps[:, par, t, side * D:(side + 1) * D]
                                nc.tensor.matmul(there, part, weight[:, 2 * D:3 * D], start=True, stop=False)
                                last = nc.tensor.matmul(there, augT[par][:, t, :],
                                                        aug_w[:, (2 + side) * D:(3 + side) * D],
                                                        start=False, stop=True)
                        last.then_inc(n_made, 1)
                run_pairs(pe, steps, LEAD, FIRST, U)

            @block.scalar
            def _(act):
                def steps(i, u, o):
                    par, other = u % 2, 1 - u % 2
                    if runs(i, 3):
                        act.wait_ge(rz_made, i - 2)
                        if past_first(i, 5):
                            act.wait_ge(zd_made, i - 4)
                        act.sem_inc(go, 1)
                        nc.scalar.activation(rz[other][:, :, :], rz_ps[:, other], ACT.Sigmoid).then_inc(gates, 1)
                    if runs(i, 1):
                        act.wait_ge(T_made, i)
                        if past_first(i, 3):
                            act.wait_ge(n_made, i - 2)
                        act.sem_inc(go, 1)
                        nc.scalar.copy(T[other][:, :, :], T_ps[:, other]).then_inc(T_evac, 1)
                        nc.scalar.copy(augT[other][:, :, :], aug_ps[0:AUG, other, 0:2 * P]).then_inc(T_evac, 1)
                    if runs(i, 3):
                        act.wait_ge(t2_made, i - 2)
                        if past_first(i, 5):
                            act.wait_ge(kept_made, i - 4)
                        act.sem_inc(go, 1)
                        nc.scalar.activation(new[other][:, :, :], t2[other][:, :, :], ACT.Tanh).then_inc(new_made, 1)
                run_pairs(act, steps, LEAD, FIRST, U)
                act.wait_ge(var_made, PAIRS)
                act.wait_ge(eps_made, 1)
                nc.scalar.activation(std[:, :], mv[:, :, 1], ACT.Sqrt, bias=eps[:, 0:1]).then_inc(std_made, 1)

            @block.vector
            def _(dve):
                dve.memset(eps[:, :], 1e-5).then_inc(eps_made, 1)
                sums = acc[:, :, D]
                dve.tensor_copy(aug[:, :, 0], sums).then_inc(aug_made, 1)
                dve.wait_ge(aug_made, 1)
                dve.tensor_tensor(s_rest[:, :], sums, aug[:, :, 0], ALU.subtract).then_inc(aug_made, 1)
                dve.wait_ge(aug_made, 2)
                dve.tensor_copy(aug[:, :, 3], s_rest[:, :]).then_inc(aug_made, 1)
                dve.wait_ge(aug_made, 3)
                dve.tensor_tensor(aug[:, :, 6], s_rest[:, :], aug[:, :, 3], ALU.subtract).then_inc(aug_made, 1)
                dve.wait_ge(aug_made, 4)
                for a in range(3):
                    again = aug[:, :, 3 * a:3 * a + 1].to_broadcast([P, TILES, 2])
                    dve.tensor_copy(aug[:, :, 3 * a + 1:3 * a + 3], again).then_inc(aug_made, 1)
                dve.memset(aug[:, :, 9:12], 1.0).then_inc(aug_made, 1)

                def steps(i, u, o):
                    par, other = u % 2, 1 - u % 2
                    if runs(i, 4):
                        xi = x[(u - 4) % U]
                        dve.wait_ge(new_made, i - 3)
                        dve.tensor_tensor(diff[par][:, :, :], xi[:, :, :], new[par][:, :, :],
                                          ALU.subtract).then_inc(diff_made, 1)
                        dve.tensor_tensor(kept[par][:, :, :], xi[:, :, :], new[par][:, :, :],
                                          ALU.add).then_inc(kept_made, 1)
                    if runs(i, 3):
                        dve.wait_ge(gates, i - 2)
                        dve.wait_ge(n_made, i - 2)
                        dve.tensor_tensor(t1[other][:, :, :], rz[other][:, :, 0:D], n_ps[:, other, :, D:2 * D],
                                          ALU.mult).then_inc(t1_made, 1)
                    if runs(i, 4):
                        dve.wait_ge(diff_made, i - 3)
                        dve.tensor_tensor(diff[par][:, :, :], rz[par][:, :, D:2 * D], diff[par][:, :, :],
                                          ALU.mult).then_inc(zd_made, 1)
                    if runs(i, 3):
                        dve.wait_ge(t1_made, i - 2)
                        if past_first(i, 5):
                            dve.wait_ge(new_made, i - 4)
                        dve.tensor_tensor(t2[other][:, :, :], t1[other][:, :, :], n_ps[:, other, :, 0:D],
                                          ALU.add).then_inc(t2_made, 1)
                    if runs(i, 4):
                        dve.wait_ge(zd_made, i - 3)
                        dve.tensor_tensor(acc[:, bass.ds((i - 4) * 2, 2), 0:D], kept[par][:, :, :],
                                          diff[par][:, :, :], ALU.add).then_inc(y_made, 1)
                        dve.wait_ge(y_made, i - 3)
                        dve.sem_inc(dve_go, 1)
                        for t in range(2):
                            last = dve.bn_stats(stats[:, par, t, :], acc[:, bass.ds((i - 4) * 2 + t, 1), 0:D])
                        last.then_inc(stats_made, 1)
                        dve.wait_ge(stats_made, i - 3)
                        dve.sem_inc(dve_go, 1)
                        for t in range(2):
                            last = dve.bn_aggr(mv2[:, par, t, :], stats[:, par, t, :])
                        last.then_inc(aggr_made, 1)
                        dve.wait_ge(aggr_made, i - 3)
                        dve.tensor_copy(mv[:, bass.ds((i - 4) * 2, 2), :], mv2[:, par]).then_inc(var_made, 1)
                run_pairs(dve, steps, LEAD, FIRST, U)
                dve.wait_ge(std_made, 1)
                dve.reciprocal(rstd[:, :], std[:, :]).then_inc(rstd_made, 1)
                dve.wait_ge(rstd_made, 1)
                dve.wait_ge(var_made, PAIRS)
                with dve.Fori(0, STORES) as c:
                    for t in range(CHUNK):
                        place = acc[:, bass.ds(c * CHUNK + t, 1), 0:D]
                        last = dve.tensor_scalar(place, place, mv[:, bass.ds(c * CHUNK + t, 1), 0:1],
                                                 rstd[:, bass.ds(c * CHUNK + t, 1)], ALU.subtract, ALU.mult)
                    last.then_inc(o_made, 1)


_INS = ['x', 'src', 'dst', 'edge_attr_64', 'L0_gnn_W1', 'L0_gnn_b1', 'L0_gnn_W2', 'L0_gnn_b2', 'L0_gnn_Wl',
        'L0_gnn_bl', 'L1_gnn_W1', 'L1_gnn_b1', 'L1_gnn_ln_g', 'L1_gnn_ln_b', 'L1_gnn_W2', 'L1_gnn_b2',
        'L1_gnn_gate_w', 'L1_gnn_gate_b', 'L1_gnn_W_ih', 'L1_gnn_b_ih', 'L1_gnn_W_hh', 'L1_gnn_b_hh']


def program(nc, ins, out):
    with ExitStack() as ctx:
        s = Shared()
        sb = lambda name, shape, dt: ctx.enter_context(nc.sbuf_tensor(name, shape, dt))
        sem = lambda name: ctx.enter_context(nc.semaphore(name))
        s.lane_b = sb("lane_b", [P, P], BF16)
        s.ident_b, s.ident_f = sb("ident_b", [P, P], BF16), sb("ident_f", [P, P], F32)
        s.ones_f = sb("ones_f", [1, P], F32)
        s.tile_of = [nc.dram_tensor(f"tile_of{l}", (1, STEPS), I16).ap() for l in range(2)]
        s.edge_of = nc.dram_tensor("edge_of", (1, STEPS), I16).ap()
        s.gather_of = [nc.dram_tensor(f"gather_of{l}", (P, STEPS), I32).ap() for l in range(2)]
        s.place_of = [nc.dram_tensor(f"place_of{l}", (P, STEPS), BF16).ap() for l in range(2)]
        s.const_i, s.const_f = sem("const_i"), sem("const_f")
        s.keys0 = nc.dram_tensor("keys0", (KEYROWS, P), I32).ap()
        s.keys1 = nc.dram_tensor("keys1", (STEPS, P), I32).ap()
        s.falls, s.unsorted = sb("falls", [P, 1], F32), sb("unsorted", [1, 1], I32)
        s.edge_key = nc.dram_tensor("edge_key", (E, 1), I32).ap()
        s.order = nc.dram_tensor("order", (KEYROWS * P, 1), I32).ap()
        s.grouped_features = nc.dram_tensor("grouped_features", (E, DE), F32).ap()
        s.bx = nc.dram_tensor("bx", (N, 2 * D), F32).ap()
        s.x1 = nc.dram_tensor("x1", (N, D), F32).ap()
        s.c = nc.dram_tensor("c", (N, D), F32).ap()
        s.split = sb("split", [P, TILES, 3, D], BF16)
        s.w1cd, s.w1e = sb("w1cd", [P, 2 * D], F32), sb("w1e", [DE, D], F32)
        s.wfold, s.whh = (nc.dram_tensor(n, (P, 3 * D), F32).ap() for n in ("wfold", "whhT"))
        s.row_parts = nc.dram_tensor("row_parts_table", (3, 10 * D), BF16).ap()
        s.ones_r = sb("ones_r", [3, P], BF16)
        with ExitStack() as early:
            s.sem = early.enter_context(part_semaphores(nc))
            brief = lambda name, shape, dt: early.enter_context(nc.sbuf_tensor(name, shape, dt))
            s.lane_i, s.part_i = brief("lane_i", [P, P], I32), brief("part_i", [P, P], I32)
            s.lane_f, s.part_f = brief("lane_f", [P, P], F32), brief("part_f", [P, P], F32)
            s.ones_b = brief("ones_b", [P, P], BF16)
            s.chunk_i, s.chunk_f = brief("chunk_i", [P, BLOCKS], I32), brief("chunk_f", [P, BLOCKS], F32)
            s.bit, s.sign, s.flip = brief("bit", [P, 8], I32), brief("sign", [P, 9], F32), brief("flip", [P, 8], F32)
            s.step_i = early.enter_context(nc.sbuf_tensor("step_i", [P, STEPS], I32))
            s.step_f = early.enter_context(nc.sbuf_tensor("step_f", [P, STEPS], F32))
            constants_stage(nc, s, ins)
            weights_stage(nc, s, ins)
            prepare_stage(nc, s, ins)
            regroup_stage(nc, s, ins)
            schedule_stage(nc, s, 0)
            schedule_stage(nc, s, 1)
        with ExitStack() as late:
            s.acc = late.enter_context(nc.sbuf_tensor("acc", [P, TILES, D + 1], F32))
            with part_semaphores(nc) as s.sem:
                edge_stage0(nc, s, ins)
                node_stage0(nc, s, ins)
            s.sem = lambda name: late.enter_context(nc.semaphore(name))
            edge_stage1(nc, s, ins)
            node_stage1(nc, s, ins, out)


def kernel(**inputs):
    import numpy as _np
    import concourse.bacc as _bacc
    from concourse import mybir as _mybir
    from concourse.bass_utils import run_bass_kernel_spmd as _run

    nc = _bacc.Bacc("TRN2", target_bir_lowering=False, num_devices=1)
    arrays, args = {}, {}
    for name in _INS:
        a = _np.ascontiguousarray(inputs[name])
        arrays[f"in_{name}"] = a
        args[name] = nc.dram_tensor(f"in_{name}", a.shape, _mybir.dt.from_np(a.dtype), kind="ExternalInput").ap()
    out = nc.dram_tensor("out_0", (N, D), _mybir.dt.float32, kind="ExternalOutput").ap()
    program(nc, args, out)
    r = _run(nc, [arrays], core_ids=[0])
    return r.results[0]["out_0"]
```

```python
from contextlib import ExitStack, contextmanager

import concourse.bass as bass
from concourse import mybir
from concourse.alu_op_type import AluOpType as ALU

ACT = mybir.ActivationFunctionType
F32 = mybir.dt.float32
BF16 = mybir.dt.bfloat16
I32 = mybir.dt.int32
I16 = mybir.dt.int16

P = 128
N = 12500
E = 200000
D = 128
DE = 64
TILES = -(-N // P)
LASTROWS = N - (TILES - 1) * P
CHUNKS = -(-E // P)
BLOCKS = -(-(CHUNKS + TILES - 1) // P)
STEPS = BLOCKS * P
G = 8
R = 4
GROUPS = STEPS // G
BODIES = GROUPS // R
ROW = 2048
KEYROWS = ROW
EP = 125
EC = E // EP
BASE = 1 << 28
LOW = (1 << 14) - 1
PAD = BASE | (LOW << 14)
assert N <= LOW and EP * EC == E and BODIES * R * G == STEPS and E % P == 64


def spread_places(place_of, g):
    return place_of[:, bass.ds(g * G, G)].rearrange("p (k a) -> p k a", a=1).to_broadcast([P, G, P])


def load_values(nc, engine, ap, most):
    _, values = nc.values_load_multi_w_load_instructions(
        ap, engines=(engine,), min_val=0, max_val=most,
        skip_runtime_bounds_check_because="the schedule bounds them")
    return values


@contextmanager
def part_semaphores(nc):
    held = []

    def sem(name):
        held.append(nc.alloc_semaphore(name))
        return held[-1]
    yield sem
    nc.all_engine_barrier()
    nc.clear_and_free_semaphores(held)
    nc.all_engine_barrier()


class Shared:
    pass


def constants_stage(nc, s, ins):
    with nc.Block() as block:
        @block.gpsimd
        def _(pool):
            nc.gpsimd.iota(s.lane_i[:, :], [[1, P]], base=0, channel_multiplier=0).then_inc(s.const_i, 1)
            nc.gpsimd.iota(s.part_i[:, :], [[0, P]], base=0, channel_multiplier=1).then_inc(s.const_i, 1)
            nc.gpsimd.iota(s.step_i[:, :], [[1, STEPS]], base=0, channel_multiplier=0).then_inc(s.const_i, 1)
            nc.gpsimd.iota(s.lane_step_i[:, :], [[P, BLOCKS]], base=0,
                           channel_multiplier=1).then_inc(s.const_i, 1)

        @block.vector
        def _(dve):
            dve.memset(s.ones_b[:, :], 1.0)
            dve.memset(s.ones_f[:, :], 1.0)
            dve.memset(s.ones_r[:, :], 1.0)
            dve.wait_ge(s.const_i, 4)
            dve.tensor_copy(s.lane_b[:, :], s.lane_i[:, :])
            dve.tensor_copy(s.step_f[:, :], s.step_i[:, :])
            dve.tensor_copy(s.lane_step[:, :], s.lane_step_i[:, :])
            dve.tensor_copy(s.part_f[:, :], s.part_i[:, :])
            dve.tensor_copy(s.lane_f[:, :], s.lane_i[:, :]).then_inc(s.const_f, 1)
            dve.wait_ge(s.const_f, 1)
            dve.tensor_tensor(s.ident_b[:, :], s.lane_f[:, :], s.part_f[:, :], ALU.is_equal)
            dve.tensor_tensor(s.ident_f[:, :], s.lane_f[:, :], s.part_f[:, :], ALU.is_equal)
            for j in range(7):
                dve.tensor_scalar(s.bit[:, j:j + 1], s.part_i[:, 0:1], j, 1,
                                  ALU.logical_shift_right, ALU.bitwise_and).then_inc(s.const_f, 1)
            dve.wait_ge(s.const_f, 8)
            dve.tensor_scalar(s.sign[:, 1:8], s.bit[:, 0:7], -2.0, 1.0, ALU.mult, ALU.add)
            dve.memset(s.sign[:, 0:1], 1.0)
            dve.memset(s.sign[:, 8:9], 1.0).then_inc(s.const_f, 1)
            dve.wait_ge(s.const_f, 9)
            dve.tensor_tensor(s.flip[:, 0:8], s.sign[:, 0:8], s.sign[:, 1:9], ALU.mult)


def weights_work(nc, s, ins, ctx, turn):
    sb = lambda name, shape, dt: ctx.enter_context(nc.sbuf_tensor(name, shape, dt))
    sem = s.sem
    raw = sb("w1_raw", [P, 4, D], F32)
    total = sb("w1_total", [P, 4], F32)
    mean = sb("w1_mean", [P, 4], F32)
    w2 = sb("w2_raw", [P, D], F32)
    wih, whh = sb("wih_raw", [P, 3, D], F32), sb("whh_raw", [P, 3, D], F32)
    w2T, wihT = sb("w2T", [P, D], F32), sb("wihT", [P, 3 * D], F32)
    ln_b, b2 = sb("ln_b_col", [P, 1], F32), sb("b2_col", [P, 1], F32)
    u = sb("u", [P, 1], F32)
    fold, whhT = sb("fold", [P, 3 * D], F32), sb("whhT_sb", [P, 3 * D], F32)
    bi, bh = sb("b_ih_row", [1, 3 * D], F32), sb("b_hh_row", [1, 3 * D], F32)
    wT_ps, hT_ps, m_ps = turn[:, 0:4, :], turn[:, 4:8, :], turn[:, 8:11, :]
    u_ps, v_ps = turn[:, 11, :], turn[:, 12:15, :]
    w_in, zeroed, chain = sem("weights_in"), sem("w_zeroed"), sem("w_chain")
    turned, copied, folded, rows_done = sem("w_turned"), sem("w_copied"), sem("w_folded"), sem("rows_done")
    rows_out, split_up = sem("rows_out"), sem("rows_split")
    long = sb("long_rows", [1, 10 * D], F32)
    parts, rest = sb("row_parts", [1, 3, 10 * D], BF16), sb("row_rest", [1, 10 * D], F32)
    row = lambda name: ins[name].rearrange("(a d) -> a d", a=1)

    def load(sp):
        w1 = ins["L1_gnn_W1"]
        sp.wait_ge(zeroed, 1)
        sp.dma_start(raw[:, 0:2, :], w1[0:2 * D, :].rearrange("(j p) d -> p j d", p=P)).then_inc(w_in, 16)
        sp.dma_start(raw[0:DE, 2, :], w1[2 * D:2 * D + DE, :]).then_inc(w_in, 16)
        sp.dma_start(raw[0:1, 3, :], row("L1_gnn_b1")).then_inc(w_in, 16)
        sp.dma_start(w2[:, :], ins["L1_gnn_W2"]).then_inc(w_in, 16)
        sp.dma_start(wih[:, :, :], ins["L1_gnn_W_ih"].rearrange("(j p) d -> p j d", p=P)).then_inc(w_in, 16)
        sp.dma_start(whh[:, :, :], ins["L1_gnn_W_hh"].rearrange("(j p) d -> p j d", p=P)).then_inc(w_in, 16)
        sp.dma_start(ln_b[:, :], ins["L1_gnn_ln_b"].rearrange("(d a) -> d a", a=1)).then_inc(w_in, 16)
        sp.dma_start(b2[:, :], ins["L1_gnn_b2"].rearrange("(d a) -> d a", a=1)).then_inc(w_in, 16)
        sp.dma_start(bi[:, :], row("L1_gnn_b_ih")).then_inc(w_in, 16)
        sp.dma_start(bh[:, :], row("L1_gnn_b_hh")).then_inc(w_in, 16)
        sp.dma_start(long[:, 8 * D:9 * D], row("L0_gnn_bl")).then_inc(w_in, 16)

    def store(sp):
        sp.wait_ge(rows_done, 3)
        sp.wait_ge(split_up, 4)
        for part in range(3):
            sp.dma_start(s.row_parts[part:part + 1, :], parts[:, part, :]).then_inc(rows_out, 16)
        sp.dma_start(s.wfold[:, :], fold[:, :]).then_inc(rows_out, 16)
        sp.dma_start(s.whh[:, :], whhT[:, :]).then_inc(rows_out, 16)
        sp.wait_ge(rows_out, 16 * 5)

    def turn_weights(pe):
        pe.wait_ge(w_in, 16 * 11)
        nc.tensor.transpose(wT_ps[:, 3, :], w2[:, :], s.ident_f[:, :])
        for j in range(3):
            nc.tensor.transpose(wT_ps[:, j, :], wih[:, j, :], s.ident_f[:, :])
        for j in range(3):
            last = nc.tensor.transpose(hT_ps[:, j, :], whh[:, j, :], s.ident_f[:, :])
        last.then_inc(turned, 1)
        nc.tensor.matmul(u_ps[:, 0:1], w2[:, :], ln_b[:, :], start=True, stop=True).then_inc(turned, 1)

    def fold_weights(pe):
        pe.wait_ge(copied, 4)
        nc.tensor.matmul(m_ps[:, :, :], w2T[:, :], wihT[:, :], start=True, stop=True)
        nc.tensor.matmul(v_ps[0:1, :, :], u[:, :], wihT[:, :], start=True, stop=True).then_inc(folded, 1)

    def clear(dve):
        dve.memset(raw[:, 2:4, :], 0.0).then_inc(zeroed, 1)
        dve.memset(long[:, 3 * D:4 * D], 0.0)

    def centre(dve):
        dve.wait_ge(w_in, 16 * 11)
        dve.reduce_sum(total[:, :], raw[:, :, :], axis=mybir.AxisListType.X).then_inc(chain, 1)
        dve.wait_ge(chain, 1)
        dve.tensor_scalar(mean[:, :], total[:, :], 1.0 / D, None, ALU.mult).then_inc(chain, 1)
        dve.wait_ge(chain, 2)
        for j in range(2):
            dve.tensor_scalar(s.w1cd[:, j * D:(j + 1) * D], raw[:, j, :], mean[:, j:j + 1], None, ALU.subtract)
        dve.tensor_scalar(s.w1e[:, :], raw[0:DE, 2, :], mean[0:DE, 2:3], None, ALU.subtract)
        dve.tensor_scalar(long[:, 9 * D:10 * D], raw[0:1, 3, :], mean[0:1, 3:4], None, ALU.subtract)

    def copy_turned(dve):
        dve.wait_ge(turned, 1)
        dve.tensor_copy(w2T[:, :], wT_ps[:, 3, :]).then_inc(copied, 1)
        dve.tensor_copy(wihT[:, :], wT_ps[:, 0:3, :].rearrange("p j d -> p (j d)")).then_inc(copied, 1)
        dve.tensor_copy(whhT[:, :], hT_ps[:, 0:3, :].rearrange("p j d -> p (j d)")).then_inc(copied, 1)
        dve.wait_ge(turned, 2)
        dve.tensor_tensor(u[:, :], u_ps[:, 0:1], b2[:, :], ALU.add).then_inc(copied, 1)
        dve.tensor_tensor(long[:, 4 * D:6 * D], bi[:, 0:2 * D], bh[:, 0:2 * D], ALU.add)
        dve.tensor_copy(long[:, 6 * D:7 * D], bi[:, 2 * D:3 * D])
        dve.tensor_copy(long[:, 7 * D:8 * D], bh[:, 2 * D:3 * D]).then_inc(rows_done, 1)

    def split_rows(dve):
        dve.wait_ge(folded, 1)
        dve.tensor_copy(fold[:, :], m_ps[:, :, :].rearrange("p j d -> p (j d)")).then_inc(rows_done, 1)
        dve.tensor_copy(long[:, 0:3 * D], v_ps[0:1, :, :].rearrange("a j d -> a (j d)")).then_inc(rows_done, 1)
        dve.wait_ge(rows_done, 3)
        dve.tensor_copy(parts[:, 0, :], long[:, :]).then_inc(split_up, 1)
        dve.wait_ge(split_up, 1)
        dve.tensor_tensor(rest[:, :], long[:, :], parts[:, 0, :], ALU.subtract).then_inc(split_up, 1)
        dve.wait_ge(split_up, 2)
        dve.tensor_copy(parts[:, 1, :], rest[:, :]).then_inc(split_up, 1)
        dve.wait_ge(split_up, 3)
        dve.tensor_tensor(parts[:, 2, :], rest[:, :], parts[:, 1, :], ALU.subtract).then_inc(split_up, 1)

    return load, store, turn_weights, fold_weights, clear, {1: centre, 8: copy_turned, 24: split_rows}


QUARTER = ROW // 4


def sort_plan():
    passes = []
    k = 2
    while k <= ROW * P:
        if k >= ROW:
            passes.append(("flip", (k // ROW).bit_length() - 1))
        if k > ROW:
            apart, d = [], k // 2
            while d >= ROW:
                apart.append(d // ROW)
                d //= 2
            passes.append(("across", apart))
        d = min(k // 2, ROW // 2)
        while d >= 1:
            passes.append(("row", k, d))
            d //= 2
        k *= 2
    plan, total, at = [], 2, 0
    for e in passes:
        adds = 4 if e[0] == "flip" else 8 * len(e[1]) if e[0] == "across" else 2 if e[1] >= ROW else 4
        left = (at + 2 + len(e[1])) % 2 if e[0] == "across" else 1 - at
        plan.append((e, total, adds, at, left))
        total, at = total + adds, left
    return plan


def sorted_at():
    _, before, adds, _, left = sort_plan()[-1]
    return before + adds, left


def quarter(t, q):
    return t[:, q * QUARTER:(q + 1) * QUARTER]


def sort_on_vector(dve, keys, flip, sort_dve, sort_evac, beside={}):
    def exchange(lo, hi, a, b):
        dve.tensor_tensor(lo, a, b, ALU.min).then_inc(sort_dve, 1)
        dve.tensor_tensor(hi, a, b, ALU.max).then_inc(sort_dve, 1)

    turned = 0
    for n, (e, before, adds, at, left) in enumerate(sort_plan()):
        if n in beside:
            beside[n](dve)
        if e[0] == "across":
            for q in range(4):
                dve.wait_ge(sort_evac, turned + q + 1)
                now = 1 - at
                for m, d in enumerate(e[1]):
                    if m:
                        dve.wait_ge(sort_dve, before + q * 2 * len(e[1]) + 2 * m)
                    x, y = (quarter(v, q).rearrange("c (r two d) -> c r two d", two=2, d=d)
                            for v in (keys[now], keys[1 - now]))
                    exchange(y[:, :, 0, :], y[:, :, 1, :], x[:, :, 0, :], x[:, :, 1, :])
                    now = 1 - now
            turned += 8
            continue
        a, b = keys[at], keys[1 - at]
        dve.wait_ge(sort_dve, before)
        if turned:
            dve.wait_ge(sort_evac, turned)
        if e[0] == "flip":
            for q in range(4):
                dve.tensor_scalar(quarter(b, q), quarter(a, q), flip[:, e[1]:e[1] + 1], None,
                                  ALU.mult).then_inc(sort_dve, 1)
        elif e[1] >= ROW:
            x, y = (v[:, :].rearrange("p (r two d) -> p r two d", two=2, d=e[2]) for v in (a, b))
            exchange(y[:, :, 0, :], y[:, :, 1, :], x[:, :, 0, :], x[:, :, 1, :])
        else:
            width = min(-(-EC // (2 * e[1])) * 2 * e[1], ROW)
            x, y = (v[:, 0:width].rearrange("p (m s r two d) -> p m s r two d", s=2, two=2, d=e[2],
                                      r=e[1] // (2 * e[2])) for v in (a, b))
            exchange(y[:, :, 0, :, 0, :], y[:, :, 0, :, 1, :], x[:, :, 0, :, 0, :], x[:, :, 0, :, 1, :])
            exchange(y[:, :, 1, :, 1, :], y[:, :, 1, :, 0, :], x[:, :, 1, :, 0, :], x[:, :, 1, :, 1, :])


def sort_on_tensor(nc, pe, keys, turn, ident, sort_dve, sort_turn, sort_evac):
    turned = 0
    for e, before, adds, at, left in sort_plan():
        if e[0] == "across":
            for source, ready, each in ((keys[at], before - 4, 1), (keys[1 - left], before, 2 * len(e[1]))):
                for q in range(4):
                    pe.wait_ge(sort_dve, ready + (q + 1) * each)
                    if turned:
                        pe.wait_ge(sort_evac, turned - 4 + q + 1)
                    for b in range(4 * q, 4 * q + 4):
                        last = nc.tensor.transpose(turn[:, b, :], source[:, b * P:(b + 1) * P], ident[:, :])
                    last.then_inc(sort_turn, 1)
                turned += 4


def sort_on_scalar(nc, act, keys, turn, sort_turn, sort_evac):
    turned = 0
    for e, before, adds, at, left in sort_plan():
        if e[0] == "across":
            for target in (keys[1 - at], keys[left]):
                for q in range(4):
                    turned += 1
                    act.wait_ge(sort_turn, turned)
                    nc.scalar.copy(quarter(target, q), turn[:, 4 * q:4 * q + 4, :]).then_inc(sort_evac, 1)


def prepare_stage(nc, s, ins):
    with ExitStack() as ctx:
        sb = lambda name, shape, dt: ctx.enter_context(nc.sbuf_tensor(name, shape, dt))
        sem = s.sem
        keys = [sb("keys_even", [P, ROW], F32), sb("keys_odd", [P, ROW], F32)]
        src_i = sb("src_i", [P, EC], I32)
        dst_i = sb("dst_i", [P, EC], I32)
        dkey = sb("dkey", [P, EC], I32)
        dst_next = sb("dst_next", [P, EC], I32)
        padkey = sb("padkey", [P, P], I32)
        xs = sb("xs", [P, 4, 2, D], F32)
        w0 = sb("w0", [P, 2 * D], F32)
        b0 = sb("b0", [1, D], F32)
        xT = sb("xT", [P, 2, 2 * P], F32)
        ab = sb("ab", [P, 4, 2, 2 * D], F32)
        rest = sb("rest", [P, 2, 2, D], F32)
        turn = ctx.enter_context(nc.psum_tensor("turn", [P, 16, P], F32))
        xtp = ctx.enter_context(nc.psum_tensor("xtp", [P, 2, 4, P], F32))
        abp = ctx.enter_context(nc.psum_tensor("abp", [P, 2, 2, 2 * D], F32))
        load_weights, store_weights, turn_weights, fold_weights, clear_weights, beside = weights_work(
            nc, s, ins, ctx, turn)
        edges_in, w_in, x_pad = sem("edges_in"), sem("w_in"), sem("x_pad")
        x_in = [sem(f"x_in{i}") for i in range(4)]
        sort_dve, sort_turn, sort_evac = sem("sort_dve"), sem("sort_turn"), sem("sort_evac")
        dkey_made, keys_out = sem("dkey_made"), sem("keys_out")
        next_clear, next_in = sem("next_clear"), sem("next_in")
        xT_made, xT_evac, ab_made, ab_evac = sem("xT_made"), sem("xT_evac"), sem("ab_made"), sem("ab_evac")
        split_done = sem("split_done")
        b_out = [sem(f"b_out{i}") for i in range(4)]
        x_copied = sem("x_copied")
        NG = TILES // 2

        with nc.Block() as block:
            @block.sync
            def _(sp):
                sp.dma_start(src_i[0:EP, :], ins["src"].rearrange("(p c) -> p c", c=EC)).then_inc(edges_in, 16)
                sp.dma_start(dst_i[0:EP, :], ins["dst"].rearrange("(p c) -> p c", c=EC)).then_inc(edges_in, 16)
                sp.wait_ge(next_clear, 1)
                sp.dma_start(dst_next[0:EP - 1, :],
                             ins["dst"][1:1 + (EP - 1) * EC].rearrange("(p c) -> p c", c=EC)).then_inc(next_in, 16)
                sp.dma_start(dst_next[EP - 1:EP, 0:EC - 1],
                             ins["dst"][1 + (EP - 1) * EC:E].rearrange("(a c) -> a c", a=1)).then_inc(next_in, 16)
                sp.dma_start(w0[:, 0:D], ins["L0_gnn_W1"][0:D, :]).then_inc(w_in, 16)
                sp.dma_start(w0[:, D:2 * D], ins["L0_gnn_W1"][D:2 * D, :]).then_inc(w_in, 16)
                sp.dma_start(b0[:, :], ins["L0_gnn_b1"].rearrange("(a d) -> a d", a=1)).then_inc(w_in, 16)
                def load_x(i):
                    if i >= 4:
                        sp.wait_ge(xT_made, i - 3)
                    full = 2 if i < NG - 1 else 1
                    xt = ins["x"][2 * i * P:(2 * i + full) * P, :].rearrange("(t p) d -> p t d", p=P)
                    sp.dma_start(xs[:, i % 4, 0:full, :], xt).then_inc(x_in[i % 4], 16)
                    if full == 1:
                        sp.wait_ge(x_pad, 1)
                        sp.dma_start(xs[0:LASTROWS, i % 4, 1, :],
                                     ins["x"][(TILES - 1) * P:N, :]).then_inc(x_in[i % 4], 16)
                for i in range(4):
                    load_x(i)
                load_weights(sp)
                sp.dma_start(s.bx[0:N, D:2 * D], ins["x"][:, :]).then_inc(x_copied, 16)
                sp.wait_ge(dkey_made, 2)
                flat = s.keys1.rearrange("r e -> (r e)")
                whole = (E // P) * P
                cut = whole - (EP - 1) * EC
                sp.dma_start(flat[0:(EP - 1) * EC].rearrange("(p c) -> p c", c=EC),
                             dkey[0:EP - 1, :]).then_inc(keys_out, 16)
                sp.dma_start(flat[(EP - 1) * EC:whole].rearrange("(a c) -> a c", a=1),
                             dkey[EP - 1:EP, 0:cut]).then_inc(keys_out, 16)
                sp.dma_start(flat[whole:whole + 64].rearrange("(a c) -> a c", a=1),
                             padkey[0:1, 0:64]).then_inc(keys_out, 16)
                sp.dma_start(flat[whole + 64:whole + P].rearrange("(a c) -> a c", a=1),
                             dkey[EP - 1:EP, cut:EC]).then_inc(keys_out, 16)
                sp.dma_start(s.keys1[CHUNKS:STEPS, :], padkey[0:STEPS - CHUNKS, :]).then_inc(keys_out, 16)
                for i in range(NG):
                    if i + 4 < NG:
                        load_x(i + 4)
                    sp.wait_ge(ab_evac, i + 1)
                    full = 2 if i < NG - 1 else 1
                    out = s.bx[2 * i * P:(2 * i + full) * P, 0:D].rearrange("(t p) d -> p t d", p=P)
                    sp.dma_start(out, ab[:, i % 4, 0:full, D:2 * D]).then_inc(b_out[i % 4], 16)
                    if full == 1:
                        sp.dma_start(s.bx[(TILES - 1) * P:N, 0:D],
                                     ab[0:LASTROWS, i % 4, 1, D:2 * D]).then_inc(b_out[i % 4], 16)
                for i in range(4):
                    sp.wait_ge(b_out[i], 16 * (len(range(i, NG, 4)) + (i == (NG - 1) % 4)))
                store_weights(sp)
                done, left = sorted_at()
                sp.wait_ge(sort_dve, done)
                sp.dma_start(s.keys0.rearrange("(p c) e -> p (c e)", p=P),
                             keys[left].bitcast(I32)[:, :]).then_inc(keys_out, 16)
                sp.wait_ge(x_copied, 16)
                sp.wait_ge(keys_out, 16 * 6)

            @block.gpsimd
            def _(pool):
                for i in range(NG):
                    tab = s.split[:, 2 * i:2 * i + 2, :, :]
                    if i == NG - 4:
                        pool.wait_ge(xT_made, NG - 4)
                        nc.gpsimd.memset(xs[:, (NG - 1) % 4, 1, :], 0.0).then_inc(x_pad, 1)
                    pool.wait_ge(ab_evac, i + 1)
                    if i >= 2:
                        pool.wait_ge(split_done, 3 * (i - 1))
                    nc.gpsimd.tensor_tensor(rest[:, i % 2], ab[:, i % 4, :, 0:D], tab[:, :, 0, :],
                                            ALU.subtract).then_inc(split_done, 1)
                    pool.wait_ge(split_done, 3 * i + 1)
                    nc.gpsimd.tensor_copy(tab[:, :, 1, :], rest[:, i % 2]).then_inc(split_done, 1)
                    pool.wait_ge(split_done, 3 * i + 2)
                    nc.gpsimd.tensor_tensor(tab[:, :, 2, :], rest[:, i % 2], tab[:, :, 1, :],
                                            ALU.subtract).then_inc(split_done, 1)

            @block.scalar
            def _(act):
                for i in range(NG + 1):
                    if i < NG:
                        act.wait_ge(xT_made, i + 1)
                        if i >= 2:
                            act.wait_ge(ab_made, i - 1)
                        nc.scalar.copy(xT[:, i % 2, :], xtp[:, i % 2, 0:2]).then_inc(xT_evac, 1)
                    if i >= 1:
                        j = i - 1
                        act.wait_ge(ab_made, j + 1)
                        if j >= 4:
                            act.wait_ge(b_out[j % 4], 16 * (j // 4))
                            act.wait_ge(split_done, 3 * (j - 3))
                        nc.scalar.copy(s.split[:, 2 * j:2 * j + 2, 0, :], abp[:, j % 2, :, 0:D])
                        nc.scalar.copy(ab[:, j % 4], abp[:, j % 2]).then_inc(ab_evac, 1)
                sort_on_scalar(nc, act, keys, turn, sort_turn, sort_evac)

            @block.tensor
            def _(pe):
                turn_weights(pe)
                pe.wait_ge(w_in, 48)
                for i in range(NG + 1):
                    if i == 8:
                        fold_weights(pe)
                    if i < NG:
                        if i >= 2:
                            pe.wait_ge(xT_evac, i - 1)
                        pe.wait_ge(x_in[i % 4], 16 * (i // 4 + 1 + (i == NG - 1)))
                        for t in range(2):
                            last = nc.tensor.transpose(xtp[:, i % 2, t, :], xs[:, i % 4, t, :], s.ident_f[:, :])
                        last.then_inc(xT_made, 1)
                    if i >= 1:
                        j = i - 1
                        pe.wait_ge(xT_evac, j + 1)
                        if j >= 2:
                            pe.wait_ge(ab_evac, j - 1)
                        for t in range(2):
                            for side in range(2):
                                half = abp[:, j % 2, t, side * D:(side + 1) * D]
                                last = nc.tensor.matmul(half, xT[:, j % 2, t * P:(t + 1) * P],
                                                        w0[:, side * D:(side + 1) * D],
                                                        start=True, stop=(side == 1))
                                if side == 0:
                                    nc.tensor.matmul(half, s.ones_f[0:1, :], b0[:, :], start=False, stop=True)
                        last.then_inc(ab_made, 1)
                sort_on_tensor(nc, pe, keys, turn, s.ident_f, sort_dve, sort_turn, sort_evac)

            @block.vector
            def _(dve):
                clear_weights(dve)
                dve.memset(dst_next[:, :], LOW)
                dve.memset(s.falls[:, :], 0.0).then_inc(next_clear, 1)
                dve.memset(padkey[:, :], PAD)
                dve.memset(keys[1].bitcast(I32)[:, EC:ROW], PAD)
                dve.memset(keys[0].bitcast(I32)[:, :], PAD).then_inc(sort_dve, 1)
                dve.wait_ge(edges_in, 32)
                dve.tensor_scalar(src_i[0:EP, :], src_i[0:EP, :], 0, None, ALU.bitwise_or)
                dve.tensor_scalar(dkey[0:EP, :], dst_i[0:EP, :], 14, BASE, ALU.logical_shift_left,
                                  ALU.bitwise_or).then_inc(dkey_made, 1)
                dve.wait_ge(dkey_made, 1)
                dve.tensor_tensor(dkey[0:EP, :], dkey[0:EP, :], src_i[0:EP, :],
                                  ALU.bitwise_or).then_inc(dkey_made, 1)
                dve.wait_ge(dkey_made, 2)
                dve.tensor_scalar(src_i[0:EP, :], src_i[0:EP, :], 14, BASE, ALU.logical_shift_left,
                                  ALU.bitwise_or).then_inc(dkey_made, 1)
                dve.wait_ge(dkey_made, 3)
                dve.wait_ge(sort_dve, 1)
                dve.tensor_tensor(keys[0].bitcast(I32)[0:EP, 0:EC], src_i[0:EP, :], dst_i[0:EP, :],
                                  ALU.bitwise_or).then_inc(sort_dve, 1)
                dve.wait_ge(next_in, 32)
                dve.wait_ge(next_clear, 1)
                dve.wait_ge(dkey_made, 3)
                dve.scalar_tensor_tensor(dst_next[0:EP, :], dst_next[0:EP, :], 0, dst_i[0:EP, :],
                                         ALU.add, ALU.is_lt, accum_out=s.falls[0:EP, :])
                sort_on_vector(dve, keys, s.flip, sort_dve, sort_evac, beside)


def regroup_stage(nc, s, ins):
    with ExitStack() as ctx:
        sb = lambda name, shape, dt: ctx.enter_context(nc.sbuf_tensor(name, shape, dt))
        sem = s.sem
        keys = [sb("by_tile_even", [P, ROW], F32), sb("by_tile_odd", [P, ROW], F32)]
        src_i, dst_i, number = (sb(n, [P, EC], I32) for n in ("src_again", "dst_again", "edge_number"))
        tile = sb("edge_tile", [P, EC], I32)
        edge, key, features = sb("edge_idx", [P, 1], I32), sb("edge_key_rows", [P, 1], I32), sb("ef_rows", [P, DE], F32)
        turn = ctx.enter_context(nc.psum_tensor("turn_again", [P, 16, P], F32))
        count = ctx.enter_context(nc.psum_tensor("falls_counted", [P, 512], F32))
        counted, flag_made, edges_in = sem("falls_counted_up"), sem("flag_made"), sem("edges_again")
        numbered, keyed, key_out = sem("numbered"), sem("keyed"), sem("key_out")
        sort_dve, sort_turn, sort_evac = sem("by_tile_dve"), sem("by_tile_turn"), sem("by_tile_evac")
        order_out, edge_in, fetched, moved = sem("order_out"), sem("edge_in"), sem("fetched"), sem("moved")
        go_sp, go_pool = sem("regroup_sp_go"), sem("regroup_pool_go")
        done, left = sorted_at()

        def unsorted(engine, kind):
            engine.wait_ge(flag_made, 1)
            return load_values(nc, kind, s.unsorted[0:1, 0:1], 1)[0]

        with nc.Block() as block:
            @block.sync
            def _(sp):
                with sp.If(unsorted(sp, mybir.EngineType.SP)):
                    sp.dma_start(src_i[0:EP, :], ins["src"].rearrange("(p c) -> p c", c=EC)).then_inc(edges_in, 16)
                    sp.dma_start(dst_i[0:EP, :], ins["dst"].rearrange("(p c) -> p c", c=EC)).then_inc(edges_in, 16)
                    sp.wait_ge(keyed, 4)
                    sp.dma_start(s.edge_key.rearrange("(p c) a -> p (c a)", c=EC), dst_i[0:EP, :]).then_inc(key_out, 16)
                    sp.wait_ge(key_out, 16)
                    sp.wait_ge(sort_dve, done + 1)
                    sp.dma_start(s.order.rearrange("(p c) a -> p (c a)", p=P),
                                 keys[1 - left].bitcast(I32)[:, :]).then_inc(order_out, 16)
                    sp.wait_ge(order_out, 16)
                    flat = s.keys1.rearrange("r e -> (r e)").rearrange("(n a) -> n a", a=1)
                    with sp.Fori(0, CHUNKS - 1) as c:
                        sp.dma_start(edge[:, :], s.order[bass.ds(c * P, P), :]).then_inc(edge_in, 16)
                        sp.wait_ge(fetched, c * 32 + 32)
                        sp.sem_inc(go_sp, 1)
                        sp.dma_start(flat[bass.ds(c * P, P), :], key[:, :]).then_inc(moved, 16)
                        sp.dma_start(s.grouped_features[bass.ds(c * P, P), :], features[:, :]).then_inc(moved, 16)
                        sp.wait_ge(moved, c * 32 + 32)
                        sp.sem_inc(go_sp, 1)
                    sp.dma_start(edge[:, :], s.order[E - P:E, :]).then_inc(edge_in, 16)
                    sp.wait_ge(fetched, CHUNKS * 32)
                    sp.dma_start(flat[CHUNKS * P - 64:CHUNKS * P, :], key[64:P, :]).then_inc(moved, 16)
                    sp.dma_start(s.grouped_features[E - P:E, :], features[:, :]).then_inc(moved, 16)
                    sp.wait_ge(moved, CHUNKS * 32)

            @block.gpsimd
            def _(pool):
                with pool.If(unsorted(pool, mybir.EngineType.Pool)):
                    nc.gpsimd.iota(number[:, :], [[1, EC]], base=BASE, channel_multiplier=EC).then_inc(numbered, 1)
                    pool.wait_ge(key_out, 16)
                    with pool.Fori(0, CHUNKS) as c:
                        pool.wait_ge(edge_in, c * 16 + 16)
                        pool.sem_inc(go_pool, 1)
                        for rows, table in ((key, s.edge_key), (features, ins["edge_attr_64"])):
                            pool.indirect_dma_start(
                                out=rows[:, :], out_offset=None, in_=table[:, :],
                                in_offset=bass.IndirectOffsetOnAxis(ap=edge[:, 0:1], axis=0),
                            ).then_inc(fetched, 16)

            @block.tensor
            def _(pe):
                nc.tensor.matmul(count[0:1, 0:1], s.falls[:, :], s.sign[:, 0:1],
                                 start=True, stop=True).then_inc(counted, 1)
                with pe.If(unsorted(pe, mybir.EngineType.PE)):
                    sort_on_tensor(nc, pe, keys, turn, s.ident_f, sort_dve, sort_turn, sort_evac)

            @block.scalar
            def _(act):
                with act.If(unsorted(act, mybir.EngineType.Activation)):
                    sort_on_scalar(nc, act, keys, turn, sort_turn, sort_evac)

            @block.vector
            def _(dve):
                dve.wait_ge(counted, 1)
                dve.tensor_scalar(s.unsorted[:, :], count[0:1, 0:1], 1.0, None, ALU.min).then_inc(flag_made, 1)
                with dve.If(unsorted(dve, mybir.EngineType.DVE)):
                    dve.memset(keys[1].bitcast(I32)[:, EC:ROW], BASE | ((1 << 25) - 1))
                    dve.memset(keys[0].bitcast(I32)[:, :], BASE | ((1 << 25) - 1)).then_inc(sort_dve, 1)
                    dve.wait_ge(edges_in, 32)
                    dve.tensor_scalar(tile[0:EP, :], dst_i[0:EP, :], 7, 18, ALU.logical_shift_right,
                                      ALU.logical_shift_left).then_inc(keyed, 1)
                    dve.wait_ge(keyed, 1)
                    dve.wait_ge(numbered, 1)
                    dve.wait_ge(sort_dve, 1)
                    dve.tensor_tensor(keys[0].bitcast(I32)[0:EP, 0:EC], tile[0:EP, :], number[0:EP, :],
                                      ALU.bitwise_or).then_inc(sort_dve, 1)
                    dve.tensor_scalar(dst_i[0:EP, :], dst_i[0:EP, :], 14, BASE, ALU.logical_shift_left,
                                      ALU.bitwise_or).then_inc(keyed, 1)
                    dve.wait_ge(keyed, 2)
                    dve.tensor_tensor(dst_i[0:EP, :], dst_i[0:EP, :], src_i[0:EP, :],
                                      ALU.bitwise_or).then_inc(keyed, 2)
                    sort_on_vector(dve, keys, s.flip, sort_dve, sort_evac)
                    dve.wait_ge(sort_dve, done)
                    dve.tensor_scalar(keys[1 - left].bitcast(I32)[:, :],
                                      keys[left].bitcast(I32)[:, :], (1 << 18) - 1, None,
                                      ALU.bitwise_and).then_inc(sort_dve, 1)


def schedule_stage(nc, s):
    LAYERS = (0, 1)
    with ExitStack() as ctx:
        def sb(name, shape, dt):
            return [ctx.enter_context(nc.sbuf_tensor(f"{name}_{l}", shape, dt)) for l in LAYERS]

        def sem(name):
            return [s.sem(f"{name}_{l}") for l in LAYERS]
        lastkey, ends_i = sb("lastkey", [P, BLOCKS], I32), sb("ends_i", [P, BLOCKS], I32)
        ends, ended = sb("ends", [P, BLOCKS], F32), sb("ended", [P, BLOCKS, TILES], BF16)
        final = sb("final_step", [P, 1], F32)
        past = sb("past", [P, STEPS], BF16)
        chunk_of = sb("chunk_of", [P, BLOCKS], I32)
        rows = sb("rows", [P, BLOCKS, P], I32)
        stepkey, side = sb("stepkey", [P, STEPS], F32), sb("side", [P, STEPS], I32)
        crow = sb("crow", [1, STEPS], F32)
        tile_i, edge_i = sb("tile_i", [1, STEPS], I16), sb("edge_i", [1, STEPS], I16)
        gather_i, place = sb("gather_i", [P, STEPS], I32), sb("place", [P, STEPS], BF16)
        counted = ctx.enter_context(nc.psum_tensor("counted", [P, 4, 512], F32))
        few = [ctx.enter_context(nc.psum_tensor(f"few_{l}", [P, 512], F32)) for l in LAYERS]
        turned = ctx.enter_context(nc.psum_tensor("keys_turned", [P, 2, 4, P], F32))
        last_in, chain, ended_made, ended_counted = sem("last_in"), sem("chain"), sem("ended"), sem("ended_counted")
        past_made, listed_up, counted_up = sem("past_made"), sem("listed_up"), sem("counted_up")
        chunk_made, rows_in, tiles_made, made, stored = (
            sem("chunk_made"), sem("rows_in"), sem("tiles_made"), sem("made"), sem("stored"))
        turned_up, evac = s.sem("turned_up"), s.sem("evac")
        widths = [min(512, STEPS - 512 * b) for b in range(-(-STEPS // 512))]
        quads = [(b, min(b + 4, BLOCKS)) for b in range(0, BLOCKS, 4)]
        with nc.Block() as block:
            @block.sync
            def _(sp):
                for l, keys in enumerate((s.keys0, s.keys1)):
                    view = keys[0:STEPS, :].rearrange("(p j) e -> p j e", j=BLOCKS)[:, :, P - 1:P]
                    with nc.allow_non_contiguous_dma(reason="one key of each chunk"):
                        sp.dma_start(lastkey[l][:, :].rearrange("p (j a) -> p j a", a=1), view).then_inc(last_in[l], 16)
                for l in LAYERS:
                    sp.wait_ge(tiles_made[l], 1)
                    sp.dma_start(s.tile_of[l][:, :], tile_i[l][:, :]).then_inc(stored[l], 16)
                sp.wait_ge(tiles_made[1], 2)
                sp.dma_start(s.edge_of[:, :], edge_i[1][:, :]).then_inc(stored[1], 16)
                for l in LAYERS:
                    sp.wait_ge(made[l], 1 + len(widths))
                    sp.dma_start(s.gather_of[l][:, :], gather_i[l][:, :]).then_inc(stored[l], 16)
                    sp.dma_start(s.place_of[l][:, :], place[l][:, :]).then_inc(stored[l], 16)
                for l in LAYERS:
                    sp.wait_ge(stored[l], 16 * (3 + l))

            @block.gpsimd
            def _(pool):
                for l, keys in enumerate((s.keys0, s.keys1)):
                    pool.wait_ge(chunk_made[l], 1)
                    for b in range(BLOCKS):
                        pool.indirect_dma_start(
                            out=rows[l][:, b, :], out_offset=None, in_=keys[:, :],
                            in_offset=bass.IndirectOffsetOnAxis(ap=chunk_of[l][:, b:b + 1], axis=0),
                        ).then_inc(rows_in[l], 16)

            @block.tensor
            def _(pe):
                for l in LAYERS:
                    pe.wait_ge(ended_made[l], 1)
                    for j in range(BLOCKS):
                        last = nc.tensor.matmul(few[l][0:TILES, 0:1], ended[l][:, j, :], s.ones_b[:, 0:1],
                                                start=(j == 0), stop=(j == BLOCKS - 1))
                    last.then_inc(ended_counted[l], 1)
                for l in LAYERS:
                    pe.wait_ge(past_made[l], 1)
                    for b in range(BLOCKS):
                        last = nc.tensor.matmul(few[l][:, b:b + 1], past[l][0:TILES, b * P:(b + 1) * P],
                                                s.ones_b[0:TILES, 0:1], start=True, stop=True)
                    last.then_inc(listed_up[l], 1)
                for l in LAYERS:
                    if l:
                        pe.wait_ge(made[0], 1 + len(widths))
                    for b, w in enumerate(widths):
                        last = nc.tensor.matmul(counted[:, b, 0:w], s.ones_b[0:TILES, :],
                                                past[l][0:TILES, b * 512:b * 512 + w], start=True, stop=True)
                    last.then_inc(counted_up[l], 1)
                    pe.wait_ge(rows_in[l], 16 * BLOCKS)
                    for n, (b, e) in enumerate(quads):
                        n += l * len(quads)
                        if n >= 2:
                            pe.wait_ge(evac, n - 1)
                        for k in range(b, e):
                            last = nc.tensor.transpose(turned[:, n % 2, k - b, :], rows[l].bitcast(F32)[:, k, :],
                                                       s.ident_f[:, :])
                        last.then_inc(turned_up, 1)

            @block.vector
            def _(dve):
                for l in LAYERS:
                    dve.wait_ge(last_in[l], 16)
                    dve.tensor_scalar(ends_i[l][:, :], lastkey[l][:, :], 21, 127,
                                      ALU.logical_shift_right, ALU.bitwise_and).then_inc(chain[l], 1)
                    dve.wait_ge(chain[l], 1)
                    dve.tensor_scalar(ends[l][:, :], ends_i[l][:, :], float(TILES - 1), None,
                                      ALU.min).then_inc(chain[l], 1)
                    dve.wait_ge(chain[l], 2)
                    for j in range(BLOCKS):
                        last = dve.tensor_scalar(ended[l][:, j, :], s.lane_f[:, 0:TILES], ends[l][:, j:j + 1], None,
                                                 ALU.is_ge)
                    last.then_inc(ended_made[l], 1)
                for l in LAYERS:
                    dve.wait_ge(ended_counted[l], 1)
                    dve.tensor_tensor(final[l][0:TILES, :], few[l][0:TILES, 0:1], s.part_f[0:TILES, 0:1],
                                      ALU.add).then_inc(chain[l], 1)
                    dve.wait_ge(chain[l], 3)
                    dve.tensor_scalar(past[l][0:TILES, :], s.step_f[0:TILES, :], final[l][0:TILES, :], None,
                                      ALU.is_gt).then_inc(past_made[l], 1)
                for l in LAYERS:
                    dve.wait_ge(listed_up[l], 1)
                    dve.tensor_tensor(chunk_of[l][:, :], s.lane_step[:, :], few[l][:, 0:BLOCKS],
                                      ALU.subtract).then_inc(chunk_made[l], 1)
                for l in LAYERS:
                    dve.wait_ge(counted_up[l], 1)
                    for b, w in enumerate(widths):
                        cut = slice(b * 512, b * 512 + w)
                        last = dve.tensor_copy(tile_i[l][:, cut], counted[0:1, b, 0:w])
                        if l == 1:
                            dve.tensor_tensor(crow[l][:, cut], s.step_f[0:1, cut], counted[0:1, b, 0:w],
                                              ALU.subtract).then_inc(chain[l], 1)
                    last.then_inc(tiles_made[l], 1)
                    if l == 1:
                        dve.wait_ge(chain[l], 3 + len(widths))
                        dve.tensor_scalar(edge_i[l][:, :], crow[l][:, :], 2.0, float((E - P) // 64),
                                          ALU.mult, ALU.min).then_inc(tiles_made[l], 1)
                    for n, (b, e) in enumerate(quads):
                        n += l * len(quads)
                        dve.wait_ge(turned_up, n + 1)
                        dve.tensor_copy(stepkey[l][:, b * P:e * P],
                                        turned[:, n % 2].rearrange("p k e -> p (k e)")[:, 0:(e - b) * P]
                                        ).then_inc(evac, 1)
                    dve.wait_ge(evac, (l + 1) * len(quads))
                    dve.tensor_scalar(gather_i[l][:, :], stepkey[l].bitcast(I32)[:, :], LOW, None,
                                      ALU.bitwise_and).then_inc(made[l], 1)
                    dve.tensor_scalar(side[l][:, :], stepkey[l].bitcast(I32)[:, :], 14, LOW,
                                      ALU.logical_shift_right, ALU.bitwise_and).then_inc(chain[l], 1)
                    dve.wait_ge(chain[l], 4 + l * len(widths))
                    for b, w in enumerate(widths):
                        cut = slice(b * 512, b * 512 + w)
                        last = dve.scalar_tensor_tensor(place[l][:, cut], counted[:, b, 0:w], -float(P),
                                                        side[l][:, cut], ALU.mult, ALU.add)
                        last.then_inc(made[l], 1)


def edge_stage0(nc, s, ins):
    W = D + 1
    with ExitStack() as ctx:
        sb = lambda name, shape, dt: ctx.enter_context(nc.sbuf_tensor(name, shape, dt))
        ps = lambda name, shape, dt: ctx.enter_context(nc.psum_tensor(name, shape, dt))
        sem = s.sem
        idx = [sb(f"idx{q}", [P, G], I32) for q in range(R)]
        bx = [sb(f"bxrows{q}", [P, G, 2 * D + 1], F32) for q in range(R)]
        hot = [sb(f"hot{q}", [P, G, P], BF16) for q in range(R)]
        hotT = [sb(f"hotT{i}", [P, G, P], BF16) for i in range(2)]
        hotw = [sb(f"hotw{i}", [P, G, P], F32) for i in range(2)]
        h = sb("h", [P, 2, 4, D], F32)
        logit = sb("logit", [P, 2, G], F32)
        sig = sb("sig", [P, 2, G], F32)
        mask = sb("mask", [P, 2, G], F32)
        w2 = sb("w2", [P, D], F32)
        b2 = sb("b2", [P, 1], F32)
        tiny = sb("tiny", [P, 1], F32)
        hotT_ps = ps("hotT_ps", [P, G, P], BF16)
        pre = ps("pre", [P, 2, 4, D], F32)
        out = ps("scattered", [P, 2, 4, 256], F32)
        w_in, zeroed = sem("w2_in"), sem("zeroed")
        idx_in = [sem(f"idx_in{q}") for q in range(R)]
        rows_in = [sem(f"bx_in{q}") for q in range(R)]
        hot_made, hot_turned, hotT_made = sem("hot_made"), sem("hot_turned"), sem("hotT_made")
        pre_made, pre_used, dotted = sem("pre_made"), sem("pre_used"), sem("dotted")
        sig_made, mask_made, hotw_made = sem("sig_made"), sem("mask_made"), sem("hotw_made")
        scattered, added = sem("scattered_up"), sem("added")
        issue, act_go = sem("issue"), sem("act_go")
        tile_of, place_of = sb("tile_row", [1, STEPS], I16), sb("places", [P, STEPS], BF16)
        gather_of, acc = s.gather_of[0], s.acc
        steps_in = sem("steps_in")

        with nc.Block() as block:
            @block.sync
            def _(sp):
                def load_idx(g, q):
                    sp.dma_start(idx[q][:, :], gather_of[:, bass.ds(g * G, G)]).then_inc(idx_in[q], 16)
                for q in range(R):
                    load_idx(q, q)
                sp.dma_start(tile_of[:, :], s.tile_of[0][:, :]).then_inc(steps_in, 16)
                sp.dma_start(place_of[:, :], s.place_of[0][:, :]).then_inc(steps_in, 16)
                with nc.allow_non_contiguous_dma(reason="a row for every partition"):
                    sp.dma_start(w2[:, :], ins["L0_gnn_W2"].rearrange("d a -> a d").to_broadcast([P, D])
                                 ).then_inc(w_in, 16)
                    sp.dma_start(b2[:, :], ins["L0_gnn_b2"].rearrange("(a d) -> a d", a=1).to_broadcast([P, 1])
                                 ).then_inc(w_in, 16)

                with sp.Fori(1, BODIES) as o:
                    for q in range(R):
                        sp.wait_ge(rows_in[q], o * (16 * G))
                        load_idx(o * R + q, q)

            @block.gpsimd
            def _(pool):
                for q in range(R):
                    nc.gpsimd.memset(bx[q][:, :, 2 * D:2 * D + 1], 1.0).then_inc(zeroed, 1)

                def gather(q):
                    for k in range(G):
                        pool.indirect_dma_start(
                            out=bx[q][:, k, 0:2 * D], out_offset=None, in_=s.bx[:, :],
                            in_offset=bass.IndirectOffsetOnAxis(ap=idx[q][:, k:k + 1], axis=0),
                        ).then_inc(rows_in[q], 16)
                for q in range(R):
                    pool.wait_ge(idx_in[q], 16)
                    gather(q)
                with pool.Fori(1, BODIES) as o:
                    for q in range(R):
                        pool.wait_ge(idx_in[q], o * 16 + 16)
                        pool.wait_ge(scattered, (o - 1) * (2 * R) + 2 * q + 2)
                        pool.sem_inc(issue, 1)
                        gather(q)

            @block.tensor
            def _(pe):
                def turn(g, q, first):
                    pe.wait_ge(hot_made, g + 1)
                    if not first:
                        pe.wait_ge(hotT_made, g)
                    for k in range(G):
                        last = nc.tensor.transpose(hotT_ps[:, k, :], hot[q][:, k, :], s.ident_b[:, :])
                    last.then_inc(hot_turned, 1)

                def products(g, q, first):
                    tiles = load_values(nc, mybir.EngineType.PE, tile_of[0:1, bass.ds(g * G, G)], TILES - 1)
                    pe.wait_ge(hotT_made, g + 1)
                    for half in range(2):
                        if not first:
                            pe.wait_ge(pre_used, g * 2 + half - 1)
                        for k in range(4):
                            for part in range(3):
                                last = nc.tensor.matmul(pre[:, half, k, :], hotT[q % 2][:, 4 * half + k, :],
                                                        s.split[:, bass.ds(tiles[4 * half + k], 1), part, :],
                                                        start=(part == 0), stop=(part == 2))
                        last.then_inc(pre_made, 1)

                def scatter(g, q, first):
                    pe.wait_ge(hotw_made, g + 1)
                    for half in range(2):
                        if not first:
                            pe.wait_ge(added, g * 8 + 4 * half - 4)
                        for k in range(4):
                            last = nc.tensor.matmul(out[:, half, k, 0:W], hotw[q % 2][:, 4 * half + k, :],
                                                    bx[q][:, 4 * half + k, D:D + W], start=True, stop=True)
                        last.then_inc(scattered, 1)

                pe.wait_ge(zeroed, R)
                pe.wait_ge(steps_in, 32)
                for q in range(R):
                    if q >= 1:
                        products(q - 1, q - 1, q == 1)
                    turn(q, q, q == 0)
                    if q >= 2:
                        scatter(q - 2, q - 2, q == 2)
                with pe.Fori(1, BODIES) as o:
                    for q in range(R):
                        products(o * R + (q - 1), (q - 1) % R, False)
                        turn(o * R + q, q, False)
                        scatter(o * R + (q - 2), (q - 2) % R, False)
                products(GROUPS - 1, R - 1, False)
                scatter(GROUPS - 2, R - 2, False)
                scatter(GROUPS - 1, R - 1, False)

            @block.scalar
            def _(act):
                act.wait_ge(w_in, 32)
                act.wait_ge(zeroed, R + 1)

                def turn_evac(g, q, first):
                    act.wait_ge(hot_turned, g + 1)
                    if not first:
                        act.wait_ge(pre_made, g * 2 - 2)
                    act.sem_inc(act_go, 1)
                    nc.scalar.copy(hotT[q % 2][:, :, :], hotT_ps[:, :, :]).then_inc(hotT_made, 1)

                def weigh(g, q, first):
                    act.wait_ge(dotted, g + 1)
                    act.sem_inc(act_go, 1)
                    nc.scalar.activation(sig[:, q % 2, :], logit[:, q % 2, :], ACT.Sigmoid,
                                         bias=b2[:, 0:1]).then_inc(sig_made, 1)
                    act.wait_ge(sig_made, g + 1)
                    act.sem_inc(act_go, 1)
                    nc.scalar.activation(mask[:, q % 2, :], sig[:, q % 2, :], ACT.Identity,
                                         bias=tiny[:, 0:1]).then_inc(mask_made, 1)
                    act.wait_ge(mask_made, g + 1)
                    if not first:
                        act.wait_ge(scattered, g * 2 - 2)
                    act.sem_inc(act_go, 1)
                    for k in range(G):
                        last = nc.scalar.activation(hotw[q % 2][:, k, :], hot[q][:, k, :], ACT.Copy,
                                                    scale=mask[:, q % 2, k:k + 1])
                    last.then_inc(hotw_made, 1)

                for q in range(R):
                    turn_evac(q, q, q < 2)
                    if q >= 1:
                        weigh(q - 1, q - 1, q < 3)
                with act.Fori(1, BODIES) as o:
                    for q in range(R):
                        turn_evac(o * R + q, q, False)
                        weigh(o * R + (q - 1), (q - 1) % R, False)
                weigh(GROUPS - 1, R - 1, False)

            @block.vector
            def _(dve):
                dve.memset(tiny[:, :], 1e-30)
                dve.memset(acc[:, :, 0:W], 0.0).then_inc(zeroed, 1)
                dve.wait_ge(w_in, 32)
                dve.wait_ge(steps_in, 32)
                dve.wait_ge(zeroed, R + 1)

                every_lane = s.lane_b[:, :].rearrange("p (a e) -> p a e", a=1).to_broadcast([P, G, P])

                def start(g, q, older, tiles):
                    if g is not None and used(g, R):
                        dve.wait_ge(hotw_made, g - (R - 1))
                    if g is not None:
                        dve.tensor_tensor(hot[q][:, :, :], every_lane, spread_places(place_of, g),
                                          ALU.is_equal).then_inc(hot_made, 1)
                    for k in range(G):
                        if older is not None:
                            if k % 4 == 0:
                                dve.wait_ge(scattered, older * 2 + k // 4 + 1)
                            if used(older, 1) or k:
                                dve.wait_ge(added, older * 8 + k)
                            slot = acc[:, bass.ds(tiles[k], 1), 0:W]
                            dve.tensor_tensor(slot, slot, out[:, k // 4, k % 4:k % 4 + 1, 0:W],
                                              ALU.add).then_inc(added, 1)

                def finish(g, q, round_):
                    dve.wait_ge(rows_in[q], (round_ + 1) * (16 * G))
                    if used(g, 1):
                        dve.wait_ge(dotted, g)
                    for half in range(2):
                        dve.wait_ge(pre_made, g * 2 + half + 1)
                        dve.tensor_tensor(h[:, half], pre[:, half], bx[q][:, 4 * half:4 * half + 4, 0:D],
                                          ALU.add).then_inc(pre_used, 1)
                    if used(g, 2):
                        dve.wait_ge(sig_made, g - 1)
                    for half in range(2):
                        dve.wait_ge(pre_used, g * 2 + half + 1)
                        for k in range(4 * half, 4 * half + 4):
                            last = dve.scalar_tensor_tensor(h[:, half, k % 4, :], h[:, half, k % 4, :], 0.0, w2[:, :],
                                                            ALU.max, ALU.mult, accum_out=logit[:, q % 2, k:k + 1])
                    last.then_inc(dotted, 1)

                def tiles_for(g):
                    return load_values(nc, mybir.EngineType.DVE, tile_of[0:1, bass.ds(g * G, G)], TILES - 1)

                for q in range(R):
                    start(q, q, q - 3 if q >= 3 else None, tiles_for(0) if q >= 3 else None)
                    if q >= 1:
                        finish(q - 1, q - 1, 0)
                with dve.Fori(1, BODIES) as o:
                    for q in range(R):
                        start(o * R + q, q, o * R + (q - 3), tiles_for(o * R + (q - 3)))
                        finish(o * R + (q - 1), (q - 1) % R, o - 1 if q == 0 else o)
                start(None, None, GROUPS - 3, tiles_for(GROUPS - 3))
                finish(GROUPS - 1, R - 1, BODIES - 1)
                start(None, None, GROUPS - 2, tiles_for(GROUPS - 2))
                start(None, None, GROUPS - 1, tiles_for(GROUPS - 1))


PAIRS = TILES // 2
assert TILES % 2 == 0 and PAIRS % 2 == 1


def run_pairs(engine, steps, lead, first=4, unroll=4):
    whole = (PAIRS - 1 - first) // unroll
    for i in range(first):
        steps(i, i % unroll, i // unroll)
    with engine.Fori(first // unroll, first // unroll + whole) as o:
        for u in range(unroll):
            steps(o * unroll + u, u, o)
    for i in range(first + unroll * whole, PAIRS + lead):
        steps(i, i % unroll, i // unroll)


def runs(i, back):
    return not isinstance(i, int) or 0 <= i - back < PAIRS


def past_first(i, n):
    return not isinstance(i, int) or i >= n


def node_stage0(nc, s, ins):
    U = 4
    LEAD, FIRST = 8, 12
    with ExitStack() as ctx:
        sb = lambda name, shape, dt: ctx.enter_context(nc.sbuf_tensor(name, shape, dt))
        ps = lambda name, shape: ctx.enter_context(nc.psum_tensor(name, shape, F32))
        sem = s.sem
        ring = lambda name, shape: [sb(f"{name}{i}", shape, F32) for i in range(U)]
        wl, bias = sb("wl", [P, D], F32), sb("bias_parts", [3, 2 * D], BF16)
        has, half, den = sb("has", [P, TILES], F32), sb("half", [P, TILES], F32), sb("den", [P, TILES], F32)
        ka, kx = sb("ka", [P, TILES], F32), sb("kx", [P, TILES], F32)
        eps = sb("eps0", [P, 1], F32)
        x, scaled, mixed, mT = (ring(n, [P, 2, D]) for n in ("n_x", "scaled", "mixed", "mT"))
        y, x1, x1T, c, rest = (ring(n, [P, 2, D]) for n in ("y", "x1_", "x1T", "c_rows", "rest1_"))
        stats, mv = ring("stats0", [P, 2, 6]), ring("mv0", [P, 2, 2])
        std, rstd = ring("std0", [P, 2]), ring("rstd0", [P, 2])
        mT_ps, y_ps, x1T_ps = ps("mT_ps", [P, 2, 512]), ps("y_ps", [P, 2, 512]), ps("x1T_ps", [P, 2, 512])
        cd_ps = ps("cd_ps", [P, 2, 2, 2 * D])
        w_in, x_pad = sem("wl_in"), sem("n_x_pad")
        x_in = [sem(f"n_x_in{i}") for i in range(U)]
        x1_out = [sem(f"x1_out{i}") for i in range(U)]
        c_out = [sem(f"c_out{i}") for i in range(U)]
        factors, chain = sem("factors"), sem("n_chain")
        scaled_made, mixed_made, mT_made, mT_evac, y_made = (
            sem("scaled_made"), sem("mixed_made"), sem("mT_made"), sem("mT_evac"), sem("y_made"))
        y_sum, stats_made, var_made, std_made, rstd_made, x1_made = (
            sem("y_sum"), sem("stats_made"), sem("var_made"), sem("std_made"), sem("rstd_made"), sem("x1_made"))
        x1T_made, x1T_evac, cd_made, c_evac = sem("x1T_made"), sem("x1T_evac"), sem("cd_made"), sem("c_evac")
        hi_made, rest_made, mid_made, lo_made = sem("hi_made"), sem("rest_made"), sem("mid_made"), sem("lo_made")
        go, dve_go, sp_go = sem("n_go"), sem("n_dve_go"), sem("n_sp_go")
        acc = s.acc

        def split(i, part):
            return s.split[:, bass.ds(i * 2, 2), part, :]

        with nc.Block() as block:
            @block.sync
            def _(sp):
                sp.dma_start(wl[:, :], ins["L0_gnn_Wl"]).then_inc(w_in, 16)
                sp.dma_start(bias[:, :], s.row_parts[:, 8 * D:10 * D]).then_inc(w_in, 16)

                def rows_of(table, i):
                    return table[bass.ds(i * (2 * P), 2 * P), :].rearrange("(t p) d -> p t d", p=P)

                def move(i, store, table, tile, done):
                    if isinstance(i, int) and i == PAIRS - 1:
                        a = table[2 * i * P:(2 * i + 1) * P, :].rearrange("(t p) d -> p t d", p=P)
                        b = table[(TILES - 1) * P:N, :]
                        ends = ((a, tile[:, 0:1, :]), (b, tile[0:LASTROWS, 1, :]))
                    else:
                        ends = ((rows_of(table, i), tile[:, :, :]),)
                    for d, t in ends:
                        sp.dma_start(*((d, t) if store else (t, d))).then_inc(done, 16)

                def steps(i, u, o):
                    if runs(i, 0):
                        if past_first(i, 4):
                            sp.wait_ge(y_sum, i - 3)
                            sp.sem_inc(sp_go, 1)
                        if isinstance(i, int) and i == PAIRS - 1:
                            sp.wait_ge(x_pad, 1)
                        move(i, False, ins["x"], x[u], x_in[u])
                    if runs(i, 5):
                        sp.wait_ge(x1_made, i - 4)
                        sp.sem_inc(sp_go, 1)
                        move(i - 5, True, s.x1, x1[(u - 5) % U], x1_out[(u - 5) % U])
                    if runs(i, 7):
                        sp.wait_ge(c_evac, i - 6)
                        sp.sem_inc(sp_go, 1)
                        move(i - 7, True, s.c, c[(u - 7) % U], c_out[(u - 7) % U])
                run_pairs(sp, steps, LEAD, FIRST)
                for u in range(U):
                    n = len(range(u, PAIRS, U)) + (u == (PAIRS - 1) % U)
                    sp.wait_ge(x1_out[u], 16 * n)
                    sp.wait_ge(c_out[u], 16 * n)

            @block.gpsimd
            def _(pool):
                pool.wait_ge(y_sum, PAIRS - U)
                nc.gpsimd.memset(x[(PAIRS - 1) % U][:, 1, :], 0.0).then_inc(x_pad, 1)

            @block.scalar
            def _(act):
                act.wait_ge(factors, 1)

                def steps(i, u, o):
                    if runs(i, 0):
                        if past_first(i, 4):
                            act.wait_ge(mixed_made, i - 3)
                            act.sem_inc(go, 1)
                        for t in range(2):
                            last = nc.scalar.activation(scaled[u][:, t, :], acc[:, bass.ds(i * 2 + t, 1), 0:D],
                                                        ACT.Copy, scale=ka[:, bass.ds(i * 2 + t, 1)])
                        last.then_inc(scaled_made, 1)
                    if runs(i, 3):
                        v = (u - 3) % U
                        act.wait_ge(var_made, i - 2)
                        if past_first(i, 7):
                            act.wait_ge(rstd_made, i - 6)
                        act.sem_inc(go, 1)
                        nc.scalar.activation(std[v][:, :], mv[v][:, :, 1], ACT.Sqrt,
                                             bias=eps[:, 0:1]).then_inc(std_made, 1)
                    if runs(i, 1):
                        v = (u - 1) % U
                        act.wait_ge(mT_made, i)
                        if past_first(i, 5):
                            act.wait_ge(y_made, i - 4)
                        act.sem_inc(go, 1)
                        nc.scalar.copy(mT[v][:, :, :], mT_ps[:, (u - 1) % 2, 0:2 * P]).then_inc(mT_evac, 1)
                    if runs(i, 4):
                        act.wait_ge(x1T_made, i - 3)
                        if past_first(i, 8):
                            act.wait_ge(cd_made, i - 7)
                        act.sem_inc(go, 1)
                        nc.scalar.copy(x1T[u][:, :, :], x1T_ps[:, u % 2, 0:2 * P]).then_inc(x1T_evac, 1)
                    if runs(i, 5):
                        v = (u - 5) % U
                        act.wait_ge(cd_made, i - 4)
                        if past_first(i, 9):
                            act.wait_ge(c_out[v], (o - (2 if u >= 1 else 3)) * 16 + 16)
                        act.sem_inc(go, 1)
                        nc.scalar.copy(c[v][:, :, :], cd_ps[:, v % 2, :, 0:D]).then_inc(c_evac, 1)
                        nc.scalar.copy(split(i - 5, 0), cd_ps[:, v % 2, :, D:2 * D]).then_inc(hi_made, 1)
                    if runs(i, 7):
                        act.wait_ge(rest_made, i - 6)
                        act.sem_inc(go, 1)
                        nc.scalar.copy(split(i - 7, 1), rest[(u - 7) % U][:, :, :]).then_inc(mid_made, 1)

                run_pairs(act, steps, LEAD, FIRST)

            @block.tensor
            def _(pe):
                pe.wait_ge(w_in, 32)

                def steps(i, u, o):
                    if runs(i, 1):
                        v = (u - 1) % U
                        pe.wait_ge(mixed_made, i)
                        if past_first(i, 3):
                            pe.wait_ge(mT_evac, i - 2)
                        for t in range(2):
                            last = nc.tensor.transpose(mT_ps[:, v % 2, t * P:(t + 1) * P], mixed[v][:, t, :],
                                                       s.ident_f[:, :])
                        last.then_inc(mT_made, 1)
                    if runs(i, 2):
                        v = (u - 2) % U
                        pe.wait_ge(mT_evac, i - 1)
                        if past_first(i, 4):
                            pe.wait_ge(y_sum, i - 3)
                        for t in range(2):
                            there = y_ps[:, v % 2, t * D:(t + 1) * D]
                            nc.tensor.matmul(there, mT[v][:, t, :], wl[:, :], start=True, stop=False)
                            last = nc.tensor.matmul(there, s.ones_r[:, :], bias[:, 0:D], start=False, stop=True)
                        last.then_inc(y_made, 1)
                    if runs(i, 4):
                        pe.wait_ge(x1_made, i - 3)
                        if past_first(i, 6):
                            pe.wait_ge(x1T_evac, i - 5)
                        for t in range(2):
                            last = nc.tensor.transpose(x1T_ps[:, u % 2, t * P:(t + 1) * P], x1[u][:, t, :],
                                                       s.ident_f[:, :])
                        last.then_inc(x1T_made, 1)
                    if runs(i, 5):
                        v = (u - 5) % U
                        pe.wait_ge(x1T_evac, i - 4)
                        if past_first(i, 7):
                            pe.wait_ge(rest_made, i - 6)
                            pe.wait_ge(c_evac, i - 6)
                        for t in range(2):
                            for side in range(2):
                                there = cd_ps[:, v % 2, t, side * D:(side + 1) * D]
                                last = nc.tensor.matmul(there, x1T[v][:, t, :], s.w1cd[:, side * D:(side + 1) * D],
                                                        start=True, stop=(side == 1))
                                if side == 0:
                                    nc.tensor.matmul(there, s.ones_r[:, :], bias[:, D:2 * D], start=False, stop=True)
                        last.then_inc(cd_made, 1)
                run_pairs(pe, steps, LEAD, FIRST)

            @block.vector
            def _(dve):
                sums = acc[:, :, D]
                dve.memset(eps[:, :], 1e-5)
                dve.tensor_scalar(half[:, :], sums, 0.0, 0.5, ALU.is_gt, ALU.mult).then_inc(chain, 1)
                dve.tensor_scalar(den[:, :], sums, 1e-9, None, ALU.add).then_inc(chain, 1)
                dve.wait_ge(chain, 2)
                dve.reciprocal(has[:, :], den[:, :]).then_inc(chain, 1)
                dve.tensor_scalar(kx[:, :], half[:, :], -1.0, 1.0, ALU.mult, ALU.add)
                dve.wait_ge(chain, 3)
                dve.tensor_tensor(ka[:, :], half[:, :], has[:, :], ALU.mult).then_inc(factors, 1)
                dve.wait_ge(factors, 1)

                def steps(i, u, o):
                    if runs(i, 2):
                        v = (u - 2) % U
                        dve.wait_ge(y_made, i - 1)
                        if past_first(i, 6):
                            dve.wait_ge(x1_made, i - 5)
                        dve.scalar_tensor_tensor(y[v][:, :, :].rearrange("p t d -> p (t d)"),
                                                 y_ps[:, v % 2, 0:2 * D], 0.0,
                                                 x[v][:, :, :].rearrange("p t d -> p (t d)"),
                                                 ALU.max, ALU.add).then_inc(y_sum, 1)
                    if runs(i, 3):
                        v = (u - 3) % U
                        dve.wait_ge(std_made, i - 2)
                        dve.reciprocal(rstd[v][:, :], std[v][:, :]).then_inc(rstd_made, 1)
                    if runs(i, 2):
                        v = (u - 2) % U
                        dve.wait_ge(y_sum, i - 1)
                        for t in range(2):
                            last = dve.bn_stats(stats[v][:, t, :], y[v][:, t, :])
                        last.then_inc(stats_made, 1)
                    if runs(i, 3):
                        v = (u - 3) % U
                        dve.wait_ge(rstd_made, i - 2)
                        if past_first(i, 7):
                            dve.wait_ge(x1T_made, i - 6)
                            dve.wait_ge(x1_out[v], (o - (1 if u == 3 else 2)) * 16 + 16)
                        for t in range(2):
                            last = dve.tensor_scalar(x1[v][:, t, :], y[v][:, t, :], mv[v][:, t, 0:1],
                                                     rstd[v][:, t:t + 1], ALU.subtract, ALU.mult)
                        last.then_inc(x1_made, 1)
                    if runs(i, 2):
                        v = (u - 2) % U
                        dve.wait_ge(stats_made, i - 1)
                        dve.sem_inc(dve_go, 1)
                        for t in range(2):
                            last = dve.bn_aggr(mv[v][:, t, :], stats[v][:, t, :])
                        last.then_inc(var_made, 1)
                    if runs(i, 0):
                        dve.wait_ge(scaled_made, i + 1)
                        last_one = isinstance(i, int) and i == PAIRS - 1
                        dve.wait_ge(x_in[u], o * 16 + 16 + 16 * last_one)
                        if past_first(i, 4):
                            dve.wait_ge(mT_made, i - 3)
                        for t in range(2):
                            last = dve.scalar_tensor_tensor(mixed[u][:, t, :], x[u][:, t, :],
                                                            kx[:, bass.ds(i * 2 + t, 1)], scaled[u][:, t, :],
                                                            ALU.mult, ALU.add)
                        last.then_inc(mixed_made, 1)
                    if runs(i, 6):
                        v = (u - 6) % U
                        dve.wait_ge(hi_made, i - 5)
                        if past_first(i, 10):
                            dve.wait_ge(lo_made, i - 9)
                        dve.tensor_tensor(rest[v][:, :, :], cd_ps[:, v % 2, :, D:2 * D], split(i - 6, 0),
                                          ALU.subtract).then_inc(rest_made, 1)
                    if runs(i, 8):
                        dve.wait_ge(mid_made, i - 7)
                        dve.tensor_tensor(split(i - 8, 2), rest[u][:, :, :], split(i - 8, 1),
                                          ALU.subtract).then_inc(lo_made, 1)
                run_pairs(dve, steps, LEAD, FIRST)


def loop_groups(engine, steps, lead):
    for q in range(R):
        steps(q, q, 0)
    with engine.Fori(1, BODIES) as o:
        for q in range(R):
            steps(o * R + q, q, o)
    for q in range(lead):
        steps(GROUPS + q, q, BODIES)


def has(g, back):
    return not isinstance(g, int) or 0 <= g - back < GROUPS


def used(g, n):
    return not isinstance(g, int) or g >= n


def edge_stage1(nc, s, ins):
    W = D + 1
    with ExitStack() as ctx:
        sb = lambda name, shape, dt: ctx.enter_context(nc.sbuf_tensor(name, shape, dt))
        ps = lambda name, shape, dt: ctx.enter_context(nc.psum_tensor(name, shape, dt))
        sem = s.sem
        step_rows, place_of = sb("step_rows1", [2, STEPS], I16), sb("places1", [P, STEPS], BF16)
        tile_of, edge_of = step_rows[0:1, :], step_rows[1:2, :]
        idx = [sb(f"idx1_{q}", [P, G], I32) for q in range(R)]
        crows = [sb(f"crows{q}", [P, G, D], F32) for q in range(R)]
        ef = [sb(f"ef{q}", [P, G, DE], F32) for q in range(R)]
        hot = [sb(f"hot1_{q}", [P, G, P], BF16) for q in range(R)]
        hotT = [sb(f"hotT1_{i}", [P, G, P], BF16) for i in range(2)]
        efT = [sb(f"efT{i}", [P, G // 2, P], F32) for i in range(2)]
        w1e2, gw2 = sb("w1e2", [P, 2, D], F32), sb("gate_w2", [P, 2], F32)
        hotw = [sb(f"hotw1_{i}", [P, G, P], F32) for i in range(2)]
        h = [sb(f"h1_{i}", [P, G, D], F32) for i in range(2)]
        z = [sb(f"z{i}", [P, G, W], F32) for i in range(2)]
        sq = sb("sq", [P, 4, D], BF16)
        ss, lnv, rstd = (sb(n, [P, 2, G], F32) for n in ("ss", "lnv", "rstd1"))
        eg, eg1, gate = (sb(n, [P, 2, G], F32) for n in ("eg", "eg1", "gate"))
        ln_g, neg_b, gb, eps = (
            sb(n, [P, w], F32) for n, w in (("ln_g", D), ("neg_b", D), ("neg_gate_b", 1), ("eps1", 1)))
        hotT_ps = ps("hotT1_ps", [P, G, P], BF16)
        efT_ps = ps("efT_ps", [P, 4, P], F32)
        pre = ps("pre1", [P, 2, 4, D], F32)
        out = ps("scattered1", [P, 3, 512], F32)
        gate_ps = ps("gate_ps", [P, 512], F32)
        w_in, zeroed, steps_in, negated = sem("w1_in"), sem("zeroed1"), sem("steps1_in"), sem("negated")
        idx_in = [sem(f"idx1_in{q}") for q in range(R)]
        rows_in = [sem(f"c_in{q}") for q in range(R)]
        ef_in = [sem(f"ef_in{q}") for q in range(R)]
        hot_made, hot_turned, hotT_made = sem("hot1_made"), sem("hot1_turned"), sem("hotT1_made")
        ef_turned, efT_made = sem("ef_turned"), sem("efT_made")
        pre_made, pre_used = sem("pre1_made"), sem("pre1_used")
        gate_made, gate_read = sem("gate_made"), sem("gate_read")
        ss_made, ln_made, rstd_made = sem("ss_made"), sem("ln_made"), sem("rstd1_made")
        eg1_made, gates_made, hotw_made = sem("eg1_made"), sem("gates_made"), sem("hotw1_made")
        scaled, z_made = sem("z_scaled"), sem("z_made")
        scattered, added = sem("scattered1_up"), sem("added1")
        issue, act_go, sp_go = sem("issue1"), sem("act_go1"), sem("sp_go1")
        acc = s.acc
        slot = [(k // 3, (k % 3) * W) for k in range(G)]

        with nc.Block() as block:
            @block.sync
            def _(sp):
                def load_idx(g, q):
                    sp.dma_start(idx[q][:, :], s.gather_of[1][:, bass.ds(g * G, G)]).then_inc(idx_in[q], 16)
                for q in range(R):
                    load_idx(q, q)
                sp.dma_start(tile_of, s.tile_of[1][:, :]).then_inc(steps_in, 16)
                sp.dma_start(edge_of, s.edge_of[:, :]).then_inc(steps_in, 16)
                sp.dma_start(place_of[:, :], s.place_of[1][:, :]).then_inc(steps_in, 16)
                row = lambda name, n: ins[name].rearrange("(a d) -> a d", a=1).to_broadcast([P, n])
                sp.dma_start(ln_g[:, :], row("L1_gnn_ln_g", D)).then_inc(w_in, 16)
                sp.dma_start(neg_b[:, :], row("L1_gnn_ln_b", D)).then_inc(w_in, 16)
                sp.dma_start(gb[:, :], row("L1_gnn_gate_b", 1)).then_inc(w_in, 16)
                sp.wait_ge(zeroed, 1)
                for half in range(2):
                    there = slice(half * DE, (half + 1) * DE)
                    sp.dma_start(w1e2[there, half, :], s.w1e[:, :]).then_inc(w_in, 16)
                    sp.dma_start(gw2[there, half:half + 1], ins["L1_gnn_gate_w"]).then_inc(w_in, 16)
                sp.wait_ge(steps_in, 48)

                def load(g, q, features):
                    edges = load_values(nc, mybir.EngineType.SP, edge_of[0:1, bass.ds(g * G, G)], (E - P) // 64)
                    for k in range(G):
                        sp.dma_start(ef[q][:, k, :],
                                     features[bass.ds(edges[k] * 64, P), :]).then_inc(ef_in[q], 16)

                def load_all(features):
                    for q in range(R):
                        load(q, q, features)
                    with sp.Fori(1, BODIES) as o:
                        for q in range(R):
                            sp.wait_ge(rows_in[q], o * (16 * G))
                            sp.sem_inc(sp_go, 1)
                            sp.wait_ge(ef_turned, (o - 1) * R + q + 1)
                            sp.sem_inc(sp_go, 1)
                            load_idx(o * R + q, q)
                            load(o * R + q, q, features)
                regrouped = load_values(nc, mybir.EngineType.SP, s.unsorted[0:1, 0:1], 1)[0]
                with sp.If(regrouped):
                    load_all(s.grouped_features)
                with sp.Else():
                    load_all(ins["edge_attr_64"])

            @block.gpsimd
            def _(pool):
                pool.wait_ge(zeroed, 1)
                for i in range(2):
                    nc.gpsimd.memset(z[i][:, :, D:W], 1.0).then_inc(zeroed, 1)

                def gather(q):
                    for k in range(G):
                        pool.indirect_dma_start(
                            out=crows[q][:, k, :], out_offset=None, in_=s.c[:, :],
                            in_offset=bass.IndirectOffsetOnAxis(ap=idx[q][:, k:k + 1], axis=0),
                        ).then_inc(rows_in[q], 16)
                for q in range(R):
                    pool.wait_ge(idx_in[q], 16)
                    gather(q)
                with pool.Fori(1, BODIES) as o:
                    for q in range(R):
                        pool.wait_ge(idx_in[q], o * 16 + 16)
                        pool.wait_ge(pre_used, (o - 1) * (2 * R) + 2 * q + 2)
                        pool.sem_inc(issue, 1)
                        gather(q)

            @block.tensor
            def _(pe):
                pe.wait_ge(steps_in, 48)
                pe.wait_ge(w_in, 16 * 7)
                pe.wait_ge(zeroed, 3)
                pe.wait_ge(added, 1)

                def steps(g, q, o):
                    if has(g, 1):
                        par = (q - 1) % 2
                        tiles = load_values(nc, mybir.EngineType.PE, tile_of[0:1, bass.ds((g - 1) * G, G)], TILES - 1)
                        pe.wait_ge(hotT_made, g)
                        pe.wait_ge(efT_made, g)
                        for half in range(2):
                            if used(g, 2):
                                pe.wait_ge(pre_used, g * 2 + half - 3)
                            for k in range(4):
                                for part in range(3):
                                    nc.tensor.matmul(pre[:, half, k, :], hotT[par][:, 4 * half + k, :],
                                                     s.split[:, bass.ds(tiles[4 * half + k], 1), part, :],
                                                     start=(part == 0), stop=False)
                                last = nc.tensor.matmul(pre[:, half, k, :], efT[par][:, 2 * half + k // 2, :],
                                                        w1e2[:, k % 2, :], start=False, stop=True)
                            last.then_inc(pre_made, 1)
                        if used(g, 2):
                            pe.wait_ge(gate_read, g - 1)
                        for k in range(G // 2):
                            last = nc.tensor.matmul(gate_ps[:, 2 * k:2 * k + 2], efT[par][:, k, :], gw2[:, :],
                                                    start=True, stop=True)
                        last.then_inc(gate_made, 1)
                    if has(g, 0):
                        pe.wait_ge(ef_in[q], o * (16 * G) + 16 * G)
                        if used(g, 1):
                            pe.wait_ge(efT_made, g)
                        for k in range(G // 2):
                            last = nc.tensor.transpose(efT_ps[:, k, :],
                                                       ef[q][:, 2 * k:2 * k + 2, :].rearrange("p a d -> p (a d)"),
                                                       s.ident_f[:, :])
                        last.then_inc(ef_turned, 1)
                        pe.wait_ge(hot_made, g + 1)
                        if used(g, 1):
                            pe.wait_ge(hotT_made, g)
                        for k in range(G):
                            last = nc.tensor.transpose(hotT_ps[:, k, :], hot[q][:, k, :], s.ident_b[:, :])
                        last.then_inc(hot_turned, 1)
                    if has(g, 3):
                        par = (q - 3) % 2
                        pe.wait_ge(hotw_made, g - 2)
                        for k in range(G):
                            if k % 4 == 0:
                                pe.wait_ge(z_made, g * 2 - 5 + k // 4)
                            bank, at = slot[k]
                            if used(g, 4) and at == 0:
                                pe.wait_ge(added, (g - 4) * G + min(k + 3, G) + 1)
                            last = nc.tensor.matmul(out[:, bank, at:at + W], hotw[par][:, k, :], z[par][:, k, :],
                                                    start=True, stop=True)
                            if k in (2, 5, 7):
                                last.then_inc(scattered, 1)
                loop_groups(pe, steps, 4)

            @block.scalar
            def _(act):
                act.preload_act_table_set("natural_log_exp_and_others")
                act.wait_ge(negated, 2)

                def steps(g, q, o):
                    par, other = q % 2, 1 - q % 2
                    if has(g, 2):
                        for half in range(2):
                            if used(g, 3) or half:
                                act.wait_ge(ss_made, g * 2 - 4 + half)
                            act.wait_ge(pre_used, g * 2 + half - 3)
                            act.sem_inc(act_go, 1)
                            for k in range(4 * half, 4 * half + 4):
                                last = nc.scalar.activation(sq[:, k % 4, :], h[par][:, k, :], ACT.Square,
                                                            accum_out=ss[:, par, k:k + 1])
                            last.then_inc(ss_made, 1)
                        act.wait_ge(ss_made, g * 2 - 2)
                        act.sem_inc(act_go, 1)
                        nc.scalar.activation(lnv[:, par, :], ss[:, par, :], ACT.Ln, bias=eps[:, 0:1],
                                             scale=1.0 / D).then_inc(ln_made, 1)
                    if has(g, 3):
                        act.wait_ge(gates_made, g - 2)
                        act.sem_inc(act_go, 1)
                        for k in range(G):
                            last = nc.scalar.activation(hotw[other][:, k, :], hot[(q - 3) % R][:, k, :], ACT.Copy,
                                                        scale=gate[:, other, k:k + 1])
                        last.then_inc(hotw_made, 1)
                    if has(g, 2):
                        act.wait_ge(ln_made, g - 1)
                        if used(g, 4):
                            act.wait_ge(scaled, g * 2 - 6)
                        act.sem_inc(act_go, 1)
                        nc.scalar.activation(rstd[:, par, :], lnv[:, par, :], ACT.Exp,
                                             scale=-0.5).then_inc(rstd_made, 1)
                    if has(g, 0):
                        act.wait_ge(ef_turned, g + 1)
                        if used(g, 2):
                            act.wait_ge(gate_made, g - 1)
                        act.sem_inc(act_go, 1)
                        nc.scalar.copy(efT[par][:, :, :], efT_ps[:, :, :]).then_inc(efT_made, 1)
                        act.wait_ge(hot_turned, g + 1)
                        act.sem_inc(act_go, 1)
                        nc.scalar.copy(hotT[par][:, :, :], hotT_ps[:, :, :]).then_inc(hotT_made, 1)
                    if has(g, 1):
                        act.wait_ge(gate_made, g)
                        if used(g, 3):
                            act.wait_ge(eg1_made, g - 2)
                        act.sem_inc(act_go, 1)
                        nc.scalar.activation(eg[:, other, :], gate_ps[:, 0:G], ACT.Exp, bias=gb[:, 0:1],
                                             scale=-1.0).then_inc(gate_read, 1)
                loop_groups(act, steps, 3)

            @block.vector
            def _(dve):
                dve.memset(w1e2[:, :, :], 0.0)
                dve.memset(gw2[:, :], 0.0).then_inc(zeroed, 1)
                dve.memset(eps[:, :], 1e-5)
                dve.memset(acc[:, :, 0:W], 0.0).then_inc(added, 1)
                dve.wait_ge(w_in, 16 * 7)
                dve.wait_ge(steps_in, 48)
                dve.tensor_scalar(neg_b[:, :], neg_b[:, :], -1.0, None, ALU.mult).then_inc(negated, 1)
                dve.tensor_scalar(gb[:, :], gb[:, :], -1.0, None, ALU.mult).then_inc(negated, 1)
                dve.wait_ge(negated, 2)
                dve.wait_ge(zeroed, 3)
                every_lane = s.lane_b[:, :].rearrange("p (a e) -> p a e", a=1).to_broadcast([P, G, P])
                spread_b = neg_b[:, :].rearrange("p (a d) -> p a d", a=1).to_broadcast([P, 4, D])

                def steps(g, q, o):
                    par, other = q % 2, 1 - q % 2
                    if has(g, 0):
                        if used(g, R):
                            dve.wait_ge(hotw_made, g - (R - 1))
                        dve.tensor_tensor(hot[q][:, :, :], every_lane, spread_places(place_of, g),
                                          ALU.is_equal).then_inc(hot_made, 1)
                    if has(g, 3):
                        dve.wait_ge(rstd_made, g - 2)
                    if has(g, 4):
                        tiles = load_values(nc, mybir.EngineType.DVE, tile_of[0:1, bass.ds((g - 4) * G, G)], TILES - 1)
                    for k in range(G):
                        if has(g, 3):
                            last = dve.scalar_tensor_tensor(z[other][:, k, 0:D], h[other][:, k, :],
                                                            rstd[:, other, k:k + 1], ln_g[:, :], ALU.mult, ALU.mult)
                            if k % 4 == 3:
                                last.then_inc(scaled, 1)
                        if has(g, 4):
                            bank, at = slot[k]
                            if at == 0:
                                dve.wait_ge(scattered, g * 3 + bank - 11)
                            dve.wait_ge(added, (g - 4) * G + k + 1)
                            place = acc[:, bass.ds(tiles[k], 1), 0:W]
                            dve.tensor_tensor(place, place, out[:, bank:bank + 1, at:at + W],
                                              ALU.add).then_inc(added, 1)
                        if has(g, 3) and k % 4 == 3:
                            half = k // 4
                            dve.wait_ge(scaled, g * 2 + half - 5)
                            part = z[other][:, 4 * half:4 * half + 4, 0:D]
                            dve.tensor_tensor(part, part, spread_b, ALU.max).then_inc(z_made, 1)
                    if has(g, 1):
                        p1 = (q - 1) % R
                        dve.wait_ge(rows_in[p1], o * (16 * G) + (0 if q == 0 else 16 * G))
                        if used(g, 3):
                            dve.wait_ge(scaled, g * 2 - 4)
                            dve.wait_ge(ss_made, g * 2 - 4)
                        for half in range(2):
                            dve.wait_ge(pre_made, g * 2 + half - 1)
                            dve.tensor_tensor(h[other][:, 4 * half:4 * half + 4, :], pre[:, half],
                                              crows[p1][:, 4 * half:4 * half + 4, :], ALU.add).then_inc(pre_used, 1)
                    if has(g, 2):
                        dve.wait_ge(gate_read, g - 1)
                        if used(g, 4):
                            dve.wait_ge(hotw_made, g - 3)
                        dve.tensor_scalar(eg1[:, par, :], eg[:, par, :], 1.0, None, ALU.add).then_inc(eg1_made, 1)
                        dve.wait_ge(eg1_made, g - 1)
                        dve.reciprocal(gate[:, par, :], eg1[:, par, :]).then_inc(gates_made, 1)
                loop_groups(dve, steps, 4)


def node_stage1(nc, s, ins, result):
    with ExitStack() as ctx:
        sb = lambda name, shape, dt: ctx.enter_context(nc.sbuf_tensor(name, shape, dt))
        ps = lambda name, shape: ctx.enter_context(nc.psum_tensor(name, shape, F32))
        sem = s.sem
        U, FIRST, LEAD = 6, 6, 4
        wfold, whh = sb("wfold_sb", [P, 3 * D], F32), sb("whh_sb", [P, 3 * D], F32)
        AUG = 12
        aug_w, aug = sb("aug_w", [AUG, 4 * D], BF16), sb("aug", [P, TILES, AUG], BF16)
        pair_aug = [sb(f"pair_aug{i}", [P, 2, AUG], BF16) for i in range(2)]
        s_rest = sb("s_rest", [P, TILES], F32)
        w_in = sem("gru_w_in")
        x = [sb(f"g_x{i}", [P, 2, D], F32) for i in range(U)]
        both = [sb(f"sums{i}", [P, 2, D], F32) for i in range(2)]
        T = [sb(f"gT{i}", [P, 4, P], F32) for i in range(2)]
        augT = [sb(f"augT{i}", [AUG, 2, P], BF16) for i in range(2)]
        rz = [sb(f"rz{i}", [P, 2, 2 * D], F32) for i in range(2)]
        t1, t2, new, diff, kept = ([sb(f"{n}{i}", [P, 2, D], F32) for i in range(2)]
                                   for n in ("t1_", "t2_", "new", "diff", "kept"))
        stats, mv = sb("stats1", [P, 2, 2, 6], F32), sb("mv1", [P, TILES, 2], F32)
        std, rstd = sb("g_std", [P, TILES], F32), sb("g_rstd", [P, TILES], F32)
        eps = sb("g_eps", [P, 1], F32)
        T_ps = ps("T_ps", [P, 2, 4, P])
        aug_ps = ctx.enter_context(nc.psum_tensor("aug_ps", [P, 2, 1024], BF16))
        rz_ps, n_ps = ps("rz_ps", [P, 2, 2, 2 * D]), ps("n_ps", [P, 2, 2, 2 * D])
        x_pad = sem("g_x_pad")
        x_in = [sem(f"g_x_in{i}") for i in range(U)]
        both_made, T_made, T_evac, rz_made, n_made = (
            sem("both_made"), sem("T_made"), sem("T_evac"), sem("rz_made"), sem("n_made"))
        gates, t1_made, t2_made, new_made, diff_made, zd_made = (
            sem("g_gates"), sem("t1_made"), sem("t2_made"), sem("new_made"), sem("diff_made"), sem("zd_made"))
        kept_made, y_made, stats_made, var_made, std_made, rstd_made, o_made = (
            sem("kept_made"), sem("gy_made"), sem("g_stats"), sem("g_var"), sem("g_std_made"), sem("g_rstd_made"),
            sem("o_made"))
        o_made_act = sem("o_made_act")
        stored, go, eps_made = sem("stored_out"), sem("g_go"), sem("g_eps_made")
        dve_go, aggr_made, sp_go, aug_made = sem("g_dve_go"), sem("g_aggr_made"), sem("g_sp_go"), sem("aug_made")
        mv2 = sb("mv_pair", [P, 2, 2, 2], F32)
        acc = s.acc
        CHUNK = 14
        STORES = TILES // CHUNK
        ON_VECTOR = 7
        shift = sb("shift", [P, TILES], F32)
        assert STORES * CHUNK == TILES

        with nc.Block() as block:
            @block.sync
            def _(sp):
                for t, w in ((wfold, s.wfold), (whh, s.whh)):
                    sp.dma_start(t[:, :], w[:, :]).then_inc(w_in, 16)
                for a in range(3):
                    sp.dma_start(aug_w[3 * a:3 * a + 3, :], s.row_parts[:, 0:4 * D]).then_inc(w_in, 16)
                sp.dma_start(aug_w[9:12, :], s.row_parts[:, 4 * D:8 * D]).then_inc(w_in, 16)

                def steps(i, u, o):
                    if past_first(i, U):
                        sp.wait_ge(y_made, i - (U - 1))
                        sp.sem_inc(sp_go, 1)
                    if isinstance(i, int) and i == PAIRS - 1:
                        sp.wait_ge(x_pad, 1)
                        a = s.x1[2 * i * P:(2 * i + 1) * P, :].rearrange("(t p) d -> p t d", p=P)
                        sp.dma_start(x[u][:, 0:1, :], a).then_inc(x_in[u], 16)
                        sp.dma_start(x[u][0:LASTROWS, 1, :], s.x1[(TILES - 1) * P:N, :]).then_inc(x_in[u], 16)
                    else:
                        a = s.x1[bass.ds(i * (2 * P), 2 * P), :].rearrange("(t p) d -> p t d", p=P)
                        sp.dma_start(x[u][:, :, :], a).then_inc(x_in[u], 16)
                run_pairs(sp, steps, 0, FIRST, U)
                for c in range(STORES):
                    sp.wait_ge(o_made, c + 1)
                    sp.wait_ge(o_made_act, c + 1)
                    full = CHUNK if c < STORES - 1 else CHUNK - 1
                    view = result[c * CHUNK * P:(c * CHUNK + full) * P, :].rearrange("(t p) d -> p t d", p=P)
                    sp.dma_start(view, acc[:, c * CHUNK:c * CHUNK + full, 0:D]).then_inc(stored, 16)
                sp.dma_start(result[(TILES - 1) * P:N, :], acc[0:LASTROWS, TILES - 1, 0:D]).then_inc(stored, 16)
                sp.wait_ge(stored, 16 * (STORES + 1))

            @block.gpsimd
            def _(pool):
                pool.wait_ge(aug_made, 8)

                def steps(i, u, o):
                    if past_first(i, 2):
                        pool.wait_ge(T_made, i - 1)
                    nc.gpsimd.tensor_copy(both[u % 2][:, :, :], acc[:, bass.ds(i * 2, 2), 0:D])
                    nc.gpsimd.tensor_copy(pair_aug[u % 2][:, :, :], aug[:, bass.ds(i * 2, 2), :]).then_inc(both_made, 1)
                    if isinstance(i, int) and i == PAIRS - 1:
                        pool.wait_ge(y_made, PAIRS - U)
                        nc.gpsimd.memset(x[u][:, 1, :], 0.0).then_inc(x_pad, 1)
                run_pairs(pool, steps, 0, FIRST, U)

            @block.tensor
            def _(pe):
                pe.wait_ge(w_in, 16 * 6)

                def steps(i, u, o):
                    par, other = u % 2, 1 - u % 2
                    if runs(i, 1):
                        v = (u - 1) % U
                        last_one = isinstance(i, int) and i == PAIRS
                        pe.wait_ge(x_in[v], (o + (1 if u >= 1 else 0)) * 16 + 16 * last_one)
                        pe.wait_ge(both_made, i)
                        if past_first(i, 3):
                            pe.wait_ge(T_evac, (i - 2) * 2)
                        for t in range(2):
                            nc.tensor.transpose(T_ps[:, other, t, :], both[other][:, t, :], s.ident_f[:, :])
                            nc.tensor.transpose(T_ps[:, other, 2 + t, :], x[v][:, t, :], s.ident_f[:, :])
                            last = nc.tensor.transpose(aug_ps[0:AUG, other, t * P:(t + 1) * P],
                                                       pair_aug[other][:, t, :], s.ident_b[:, :])
                        last.then_inc(T_made, 1)
                    if runs(i, 2):
                        pe.wait_ge(T_evac, i * 2 - 2)
                        if past_first(i, 4):
                            pe.wait_ge(gates, i - 3)
                        for t in range(2):
                            nc.tensor.matmul(rz_ps[:, par, t, :], T[par][:, t, :], wfold[:, 0:2 * D],
                                             start=True, stop=False)
                            nc.tensor.matmul(rz_ps[:, par, t, :], T[par][:, 2 + t, :], whh[:, 0:2 * D],
                                             start=False, stop=False)
                            last = nc.tensor.matmul(rz_ps[:, par, t, :], augT[par][:, t, :], aug_w[:, 0:2 * D],
                                                    start=False, stop=True)
                        last.then_inc(rz_made, 1)
                        if past_first(i, 4):
                            pe.wait_ge(t2_made, i - 3)
                        for t in range(2):
                            for side, part, weight in ((0, T[par][:, t, :], wfold), (1, T[par][:, 2 + t, :], whh)):
                                there = n_ps[:, par, t, side * D:(side + 1) * D]
                                nc.tensor.matmul(there, part, weight[:, 2 * D:3 * D], start=True, stop=False)
                                last = nc.tensor.matmul(there, augT[par][:, t, :],
                                                        aug_w[:, (2 + side) * D:(3 + side) * D],
                                                        start=False, stop=True)
                        last.then_inc(n_made, 1)
                run_pairs(pe, steps, LEAD, FIRST, U)

            @block.scalar
            def _(act):
                def steps(i, u, o):
                    par, other = u % 2, 1 - u % 2
                    if runs(i, 3):
                        act.wait_ge(rz_made, i - 2)
                        if past_first(i, 5):
                            act.wait_ge(zd_made, i - 4)
                        act.sem_inc(go, 1)
                        nc.scalar.activation(rz[other][:, :, :], rz_ps[:, other], ACT.Sigmoid).then_inc(gates, 1)
                    if runs(i, 1):
                        act.wait_ge(T_made, i)
                        if past_first(i, 3):
                            act.wait_ge(n_made, i - 2)
                        act.sem_inc(go, 1)
                        nc.scalar.copy(T[other][:, :, :], T_ps[:, other]).then_inc(T_evac, 1)
                        nc.scalar.copy(augT[other][:, :, :], aug_ps[0:AUG, other, 0:2 * P]).then_inc(T_evac, 1)
                    if runs(i, 3):
                        act.wait_ge(t2_made, i - 2)
                        if past_first(i, 5):
                            act.wait_ge(kept_made, i - 4)
                        act.sem_inc(go, 1)
                        nc.scalar.activation(new[other][:, :, :], t2[other][:, :, :], ACT.Tanh).then_inc(new_made, 1)
                run_pairs(act, steps, LEAD, FIRST, U)
                act.wait_ge(var_made, PAIRS)
                act.wait_ge(eps_made, 1)
                nc.scalar.activation(std[:, :], mv[:, :, 1], ACT.Sqrt, bias=eps[:, 0:1]).then_inc(std_made, 1)
                act.wait_ge(rstd_made, 3)
                with act.Fori(0, STORES) as c:
                    for t in range(ON_VECTOR, CHUNK):
                        place = acc[:, bass.ds(c * CHUNK + t, 1), 0:D]
                        last = nc.scalar.activation(place, place, ACT.Identity,
                                                    bias=shift[:, bass.ds(c * CHUNK + t, 1)],
                                                    scale=rstd[:, bass.ds(c * CHUNK + t, 1)])
                    last.then_inc(o_made_act, 1)

            @block.vector
            def _(dve):
                dve.memset(eps[:, :], 1e-5).then_inc(eps_made, 1)
                sums = acc[:, :, D]
                dve.tensor_copy(aug[:, :, 0], sums).then_inc(aug_made, 1)
                dve.wait_ge(aug_made, 1)
                dve.tensor_tensor(s_rest[:, :], sums, aug[:, :, 0], ALU.subtract).then_inc(aug_made, 1)
                dve.wait_ge(aug_made, 2)
                dve.tensor_copy(aug[:, :, 3], s_rest[:, :]).then_inc(aug_made, 1)
                dve.wait_ge(aug_made, 3)
                dve.tensor_tensor(aug[:, :, 6], s_rest[:, :], aug[:, :, 3], ALU.subtract).then_inc(aug_made, 1)
                dve.wait_ge(aug_made, 4)
                for a in range(3):
                    again = aug[:, :, 3 * a:3 * a + 1].to_broadcast([P, TILES, 2])
                    dve.tensor_copy(aug[:, :, 3 * a + 1:3 * a + 3], again).then_inc(aug_made, 1)
                dve.memset(aug[:, :, 9:12], 1.0).then_inc(aug_made, 1)

                def steps(i, u, o):
                    par, other = u % 2, 1 - u % 2
                    if runs(i, 4):
                        xi = x[(u - 4) % U]
                        dve.wait_ge(new_made, i - 3)
                        dve.tensor_tensor(diff[par][:, :, :], xi[:, :, :], new[par][:, :, :],
                                          ALU.subtract).then_inc(diff_made, 1)
                        dve.tensor_tensor(kept[par][:, :, :], xi[:, :, :], new[par][:, :, :],
                                          ALU.add).then_inc(kept_made, 1)
                    if runs(i, 3):
                        dve.wait_ge(gates, i - 2)
                        dve.wait_ge(n_made, i - 2)
                        dve.tensor_tensor(t1[other][:, :, :], rz[other][:, :, 0:D], n_ps[:, other, :, D:2 * D],
                                          ALU.mult).then_inc(t1_made, 1)
                    if runs(i, 4):
                        dve.wait_ge(diff_made, i - 3)
                        dve.tensor_tensor(diff[par][:, :, :], rz[par][:, :, D:2 * D], diff[par][:, :, :],
                                          ALU.mult).then_inc(zd_made, 1)
                    if runs(i, 3):
                        dve.wait_ge(t1_made, i - 2)
                        if past_first(i, 5):
                            dve.wait_ge(new_made, i - 4)
                        dve.tensor_tensor(t2[other][:, :, :], t1[other][:, :, :], n_ps[:, other, :, 0:D],
                                          ALU.add).then_inc(t2_made, 1)
                    if runs(i, 4):
                        dve.wait_ge(zd_made, i - 3)
                        dve.tensor_tensor(acc[:, bass.ds((i - 4) * 2, 2), 0:D], kept[par][:, :, :],
                                          diff[par][:, :, :], ALU.add).then_inc(y_made, 1)
                        dve.wait_ge(y_made, i - 3)
                        dve.sem_inc(dve_go, 1)
                        for t in range(2):
                            last = dve.bn_stats(stats[:, par, t, :], acc[:, bass.ds((i - 4) * 2 + t, 1), 0:D])
                        last.then_inc(stats_made, 1)
                        dve.wait_ge(stats_made, i - 3)
                        dve.sem_inc(dve_go, 1)
                        for t in range(2):
                            last = dve.bn_aggr(mv2[:, par, t, :], stats[:, par, t, :])
                        last.then_inc(aggr_made, 1)
                        dve.wait_ge(aggr_made, i - 3)
                        dve.tensor_copy(mv[:, bass.ds((i - 4) * 2, 2), :], mv2[:, par]).then_inc(var_made, 1)
                run_pairs(dve, steps, LEAD, FIRST, U)
                dve.wait_ge(std_made, 1)
                dve.reciprocal(rstd[:, :], std[:, :]).then_inc(rstd_made, 1)
                dve.wait_ge(rstd_made, 1)
                dve.wait_ge(var_made, PAIRS)
                dve.tensor_tensor(shift[:, :], mv[:, :, 0], rstd[:, :], ALU.mult).then_inc(rstd_made, 1)
                dve.wait_ge(rstd_made, 2)
                dve.tensor_scalar(shift[:, :], shift[:, :], -1.0, None, ALU.mult).then_inc(rstd_made, 1)
                with dve.Fori(0, STORES) as c:
                    for t in range(ON_VECTOR):
                        place = acc[:, bass.ds(c * CHUNK + t, 1), 0:D]
                        last = dve.tensor_scalar(place, place, mv[:, bass.ds(c * CHUNK + t, 1), 0:1],
                                                 rstd[:, bass.ds(c * CHUNK + t, 1)], ALU.subtract, ALU.mult)
                    last.then_inc(o_made, 1)


_INS = ['x', 'src', 'dst', 'edge_attr_64', 'L0_gnn_W1', 'L0_gnn_b1', 'L0_gnn_W2', 'L0_gnn_b2', 'L0_gnn_Wl',
        'L0_gnn_bl', 'L1_gnn_W1', 'L1_gnn_b1', 'L1_gnn_ln_g', 'L1_gnn_ln_b', 'L1_gnn_W2', 'L1_gnn_b2',
        'L1_gnn_gate_w', 'L1_gnn_gate_b', 'L1_gnn_W_ih', 'L1_gnn_b_ih', 'L1_gnn_W_hh', 'L1_gnn_b_hh']


def program(nc, ins, out):
    with ExitStack() as ctx:
        s = Shared()
        sb = lambda name, shape, dt: ctx.enter_context(nc.sbuf_tensor(name, shape, dt))
        sem = lambda name: ctx.enter_context(nc.semaphore(name))
        s.lane_b = sb("lane_b", [P, P], BF16)
        s.ident_b, s.ident_f = sb("ident_b", [P, P], BF16), sb("ident_f", [P, P], F32)
        s.ones_f = sb("ones_f", [1, P], F32)
        s.tile_of = [nc.dram_tensor(f"tile_of{l}", (1, STEPS), I16).ap() for l in range(2)]
        s.edge_of = nc.dram_tensor("edge_of", (1, STEPS), I16).ap()
        s.gather_of = [nc.dram_tensor(f"gather_of{l}", (P, STEPS), I32).ap() for l in range(2)]
        s.place_of = [nc.dram_tensor(f"place_of{l}", (P, STEPS), BF16).ap() for l in range(2)]
        s.const_i, s.const_f = sem("const_i"), sem("const_f")
        s.keys0 = nc.dram_tensor("keys0", (KEYROWS, P), I32).ap()
        s.keys1 = nc.dram_tensor("keys1", (STEPS, P), I32).ap()
        s.falls, s.unsorted = sb("falls", [P, 1], F32), sb("unsorted", [1, 1], I32)
        s.edge_key = nc.dram_tensor("edge_key", (E, 1), I32).ap()
        s.order = nc.dram_tensor("order", (KEYROWS * P, 1), I32).ap()
        s.grouped_features = nc.dram_tensor("grouped_features", (E, DE), F32).ap()
        s.bx = nc.dram_tensor("bx", (N, 2 * D), F32).ap()
        s.x1 = nc.dram_tensor("x1", (N, D), F32).ap()
        s.c = nc.dram_tensor("c", (N, D), F32).ap()
        s.split = sb("split", [P, TILES, 3, D], BF16)
        s.w1cd, s.w1e = sb("w1cd", [P, 2 * D], F32), sb("w1e", [DE, D], F32)
        s.wfold, s.whh = (nc.dram_tensor(n, (P, 3 * D), F32).ap() for n in ("wfold", "whhT"))
        s.row_parts = nc.dram_tensor("row_parts_table", (3, 10 * D), BF16).ap()
        s.ones_r = sb("ones_r", [3, P], BF16)
        with ExitStack() as early:
            s.sem = early.enter_context(part_semaphores(nc))
            brief = lambda name, shape, dt: early.enter_context(nc.sbuf_tensor(name, shape, dt))
            s.lane_i, s.part_i = brief("lane_i", [P, P], I32), brief("part_i", [P, P], I32)
            s.lane_f, s.part_f = brief("lane_f", [P, P], F32), brief("part_f", [P, P], F32)
            s.ones_b = brief("ones_b", [P, P], BF16)
            s.lane_step_i, s.lane_step = brief("lane_step_i", [P, BLOCKS], I32), brief("lane_step", [P, BLOCKS], F32)
            s.bit, s.sign, s.flip = brief("bit", [P, 8], I32), brief("sign", [P, 9], F32), brief("flip", [P, 8], F32)
            s.step_i = early.enter_context(nc.sbuf_tensor("step_i", [P, STEPS], I32))
            s.step_f = early.enter_context(nc.sbuf_tensor("step_f", [P, STEPS], F32))
            constants_stage(nc, s, ins)
            prepare_stage(nc, s, ins)
            regroup_stage(nc, s, ins)
            schedule_stage(nc, s)
        with ExitStack() as late:
            s.acc = late.enter_context(nc.sbuf_tensor("acc", [P, TILES, D + 1], F32))
            with part_semaphores(nc) as s.sem:
                edge_stage0(nc, s, ins)
                node_stage0(nc, s, ins)
            s.sem = lambda name: late.enter_context(nc.semaphore(name))
            edge_stage1(nc, s, ins)
            node_stage1(nc, s, ins, out)


def kernel(**inputs):
    import numpy as _np
    import concourse.bacc as _bacc
    from concourse import mybir as _mybir
    from concourse.bass_utils import run_bass_kernel_spmd as _run

    nc = _bacc.Bacc("TRN2", target_bir_lowering=False, num_devices=1)
    arrays, args = {}, {}
    for name in _INS:
        a = _np.ascontiguousarray(inputs[name])
        arrays[f"in_{name}"] = a
        args[name] = nc.dram_tensor(f"in_{name}", a.shape, _mybir.dt.from_np(a.dtype), kind="ExternalInput").ap()
    out = nc.dram_tensor("out_0", (N, D), _mybir.dt.float32, kind="ExternalOutput").ap()
    program(nc, args, out)
    r = _run(nc, [arrays], core_ids=[0])
    return r.results[0]["out_0"]
```
